# Optimizing a Trainium2 kernel written in Bass

```python
import numpy as np
import jax
import jax.numpy as jnp

def _softmax(x, axis=-1):
    return jax.nn.softmax(x, axis=axis)

def _gelu(x):
    return jax.nn.gelu(x, approximate=True)

def _silu(x):
    return jax.nn.silu(x)

def _sigmoid(x):
    return jax.nn.sigmoid(x)

def _layernorm(x, axis=-1, eps=1e-05):
    m = jnp.mean(x, axis=axis, keepdims=True)
    v = jnp.var(x, axis=axis, keepdims=True)
    return (x - m) / jnp.sqrt(v + eps)

def _scatter_add(tgt, idx, src, axis=0):
    return tgt.at[idx].add(src)

def _segment_sum(src, seg, n):
    return jax.ops.segment_sum(src, seg, n)
kernel_name = 'mk_lm_tower_d2_tok_ids256_r4_8c5da0'

def setup_inputs(seed: int=0):
    np.random.seed(seed)
    _w = jnp.asarray

    def _rec_inputs():
        import jax
        import jax.numpy as jnp
        _rk = jax.random.key(seed)
        x = jax.random.randint(jax.random.fold_in(_rk, 1), (32, 512), 0, 12564, jnp.int32)
        return x
    x = _rec_inputs()

    def _L0_tok_setup():
        import jax, jax.numpy as jnp
        import numpy as np
        VOCAB, N_TURNS, OUT_DIM, POLY_DEG = (50257, 4, 64, 4)
        key = jax.random.key(seed)
        k1, k2, k3 = jax.random.split(key, 3)
        token_ids = jax.random.randint(k1, (16, 1024), 0, VOCAB)
        turns = jax.random.normal(k2, (VOCAB, N_TURNS), dtype=jnp.float32) * 3.0
        poly_coeffs = jax.random.normal(k3, (N_TURNS, POLY_DEG + 1, OUT_DIM), dtype=jnp.float32) * 0.01
        return {'token_ids': token_ids, 'turns': turns, 'poly_coeffs': poly_coeffs}
    _L0_tok_all = _L0_tok_setup()
    _L0_tok_in = {k: v for k, v in _L0_tok_all.items() if k in ('turns', 'poly_coeffs')}
    del _L0_tok_all

    def _L0_attn_setup():
        import jax, jax.numpy as jnp
        import numpy as np
        STD = 0.02
        key = jax.random.key(seed)
        k1, k2, k3 = jax.random.split(key, 3)
        b, n_t, n, n_h = (2, 512, 64, 8)
        r_prime = jax.random.normal(k1, (b, n_t, n), dtype=jnp.float32)
        Q = STD * jax.random.normal(k2, (n_h, n, n), dtype=jnp.float32)
        E = STD * jax.random.normal(k3, (n_h, n, n), dtype=jnp.float32)
        return {'r_prime': r_prime, 'Q': Q, 'E': E}
    _L0_attn_all = _L0_attn_setup()
    _L0_attn_in = {k: v for k, v in _L0_attn_all.items() if k in ('Q', 'E')}
    del _L0_attn_all

    def _L0_ffn_setup():
        import jax, jax.numpy as jnp
        import numpy as np
        E = 8
        K = 2
        D = 64
        H = 128
        DOUT = 64
        EPS = 1e-05
        key = jax.random.key(seed)
        ks = jax.random.split(key, 9)
        s = 0.02
        return {'x': jax.random.normal(ks[0], (4, 2048, D), jnp.float32), 'gamma': 1.0 + 0.05 * jax.random.normal(ks[1], (D,), jnp.float32), 'beta': 0.05 * jax.random.normal(ks[2], (D,), jnp.float32), 'Wr': 0.01 * jax.random.normal(ks[3], (D, E), jnp.float32), 'br': jnp.zeros((E,), jnp.float32), 'W1': s * jax.random.normal(ks[4], (E, D, H), jnp.float32), 'b1': s * jax.random.normal(ks[5], (E, H), jnp.float32), 'W2': s * jax.random.normal(ks[6], (E, H, DOUT), jnp.float32), 'b2': s * jax.random.normal(ks[7], (E, DOUT), jnp.float32)}
    _L0_ffn_all = _L0_ffn_setup()
    _L0_ffn_in = {k: v for k, v in _L0_ffn_all.items() if k in ('gamma', 'beta', 'Wr', 'br', 'W1', 'b1', 'W2', 'b2')}
    del _L0_ffn_all

    def _L1_attn_setup():
        import jax, jax.numpy as jnp
        import numpy as np
        import math
        B, T, D_MODEL = (1, 512, 64)
        N_Q, N_KV = (16, 1)
        D_HEAD = D_MODEL // N_KV
        QPG = N_Q // N_KV
        ROPE_BASE = 10000.0
        WINDOW = 128
        EPS = 1.1920929e-07
        NEG = -1e+30

        def _rope(x, base=ROPE_BASE):
            t, d = (x.shape[-2], x.shape[-1])
            freqs = base ** (-2.0 * jnp.arange(d // 2, dtype=jnp.float32) / d)
            theta = jnp.arange(t, dtype=jnp.float32)[:, None] * freqs[None, :]
            cos, sin = (jnp.cos(theta), jnp.sin(theta))
            x1, x2 = (x[..., 0::2], x[..., 1::2])
            r1 = x1 * cos - x2 * sin
            r2 = x1 * sin + x2 * cos
            return jnp.stack([r1, r2], axis=-1).reshape(x.shape)

        def _rmsnorm(x, w):
            return x * jax.lax.rsqrt(jnp.mean(x * x, axis=-1, keepdims=True) + EPS) * w
        key = jax.random.key(seed)
        k0, k1, k2, k3 = jax.random.split(key, 4)
        x = jax.random.normal(k0, (B, T, D_MODEL), dtype=jnp.float32)
        wq = jax.random.normal(k1, (QPG * N_KV * D_HEAD, D_MODEL), dtype=jnp.float32) * 0.02
        wkv = jax.random.normal(k2, (2 * D_HEAD * N_KV, D_MODEL), dtype=jnp.float32) * 0.02
        wo = jax.random.normal(k3, (D_MODEL, D_HEAD * N_Q * N_KV), dtype=jnp.float32) * 0.02
        q_norm_w = jnp.ones((D_HEAD,), dtype=jnp.float32)
        k_norm_w = jnp.ones((D_HEAD,), dtype=jnp.float32)
        return {'x': x, 'wq': wq, 'wkv': wkv, 'wo': wo, 'q_norm_w': q_norm_w, 'k_norm_w': k_norm_w}
    _L1_attn_all = _L1_attn_setup()
    _L1_attn_in = {k: v for k, v in _L1_attn_all.items() if k in ('wq', 'wkv', 'wo', 'q_norm_w', 'k_norm_w')}
    del _L1_attn_all

    def _L1_ffn_setup():
        import jax, jax.numpy as jnp
        import numpy as np
        B, S, D = (8, 1024, 64)
        H = 4 * D
        CAPACITY = 0.5
        key = jax.random.key(seed)
        ks = jax.random.split(key, 6)
        x = jax.random.normal(ks[0], (B, S, D), dtype=jnp.float32)
        attention_mask = jnp.zeros((B, 1, 1, S), dtype=jnp.float32)
        wr = jax.random.normal(ks[1], (D, 1), dtype=jnp.float32) * 0.02
        br = jnp.zeros((1,), dtype=jnp.float32)
        w1 = jax.random.normal(ks[2], (D, H), dtype=jnp.float32) * 0.02
        b1 = jnp.zeros((H,), dtype=jnp.float32)
        w2 = jax.random.normal(ks[3], (H, D), dtype=jnp.float32) * 0.02
        b2 = jnp.zeros((D,), dtype=jnp.float32)
        return {'x': x, 'attention_mask': attention_mask, 'wr': wr, 'br': br, 'w1': w1, 'b1': b1, 'w2': w2, 'b2': b2}
    _L1_ffn_all = _L1_ffn_setup()
    _L1_ffn_in = {k: v for k, v in _L1_ffn_all.items() if k in ('attention_mask', 'wr', 'br', 'w1', 'b1', 'w2', 'b2')}
    del _L1_ffn_all
    return {'x': x, 'L0_tok_turns': _L0_tok_in['turns'], 'L0_tok_poly_coeffs': _L0_tok_in['poly_coeffs'], 'L0_attn_Q': _L0_attn_in['Q'], 'L0_attn_E': _L0_attn_in['E'], 'L0_ffn_gamma': _L0_ffn_in['gamma'], 'L0_ffn_beta': _L0_ffn_in['beta'], 'L0_ffn_Wr': _L0_ffn_in['Wr'], 'L0_ffn_br': _L0_ffn_in['br'], 'L0_ffn_W1': _L0_ffn_in['W1'], 'L0_ffn_b1': _L0_ffn_in['b1'], 'L0_ffn_W2': _L0_ffn_in['W2'], 'L0_ffn_b2': _L0_ffn_in['b2'], 'L1_attn_wq': _L1_attn_in['wq'], 'L1_attn_wkv': _L1_attn_in['wkv'], 'L1_attn_wo': _L1_attn_in['wo'], 'L1_attn_q_norm_w': _L1_attn_in['q_norm_w'], 'L1_attn_k_norm_w': _L1_attn_in['k_norm_w'], 'L1_ffn_attention_mask': _L1_ffn_in['attention_mask'], 'L1_ffn_wr': _L1_ffn_in['wr'], 'L1_ffn_br': _L1_ffn_in['br'], 'L1_ffn_w1': _L1_ffn_in['w1'], 'L1_ffn_b1': _L1_ffn_in['b1'], 'L1_ffn_w2': _L1_ffn_in['w2'], 'L1_ffn_b2': _L1_ffn_in['b2']}

def reference(x, L0_tok_turns, L0_tok_poly_coeffs, L0_attn_Q, L0_attn_E, L0_ffn_gamma, L0_ffn_beta, L0_ffn_Wr, L0_ffn_br, L0_ffn_W1, L0_ffn_b1, L0_ffn_W2, L0_ffn_b2, L1_attn_wq, L1_attn_wkv, L1_attn_wo, L1_attn_q_norm_w, L1_attn_k_norm_w, L1_ffn_attention_mask, L1_ffn_wr, L1_ffn_br, L1_ffn_w1, L1_ffn_b1, L1_ffn_w2, L1_ffn_b2):
    import jax
    import jax.numpy as jnp

    def _L0_tok_ref(token_ids, turns, poly_coeffs):
        import jax, jax.numpy as jnp
        import numpy as np
        VOCAB, N_TURNS, OUT_DIM, POLY_DEG = (50257, 4, 64, 4)
        base_turns = turns[token_ids]
        x = jax.lax.stop_gradient(jnp.trunc(base_turns)).astype(jnp.float32)
        degs = jnp.arange(POLY_DEG + 1, dtype=jnp.float32)
        xp = x[..., None] ** degs
        emb = jnp.einsum('bstd,tdo->bso', xp, poly_coeffs)
        return emb

    def _L0_attn_ref(r_prime, Q, E):
        import jax, jax.numpy as jnp
        import numpy as np
        STD = 0.02
        Omega = jnp.einsum('bti,hij,buj->bhtu', r_prime, Q, r_prime)
        n_t = r_prime.shape[1]
        mask = jnp.tril(jnp.ones((n_t, n_t), dtype=r_prime.dtype))
        Omega = Omega * mask
        r = jnp.einsum('bhtu,hij,buj->bti', Omega, E, r_prime)
        return r

    def _L0_ffn_ref(x, gamma, beta, Wr, br, W1, b1, W2, b2):
        import jax, jax.numpy as jnp
        import numpy as np
        E = 8
        K = 2
        D = 64
        H = 128
        DOUT = 64
        EPS = 1e-05
        mu = jnp.mean(x, axis=-1, keepdims=True)
        var = jnp.mean(jnp.square(x - mu), axis=-1, keepdims=True)
        xn = (x - mu) * jax.lax.rsqrt(var + EPS) * gamma + beta
        logits = jnp.einsum('bsd,de->bse', xn, Wr) + br
        top_vals, top_idx = jax.lax.top_k(logits, K)
        w = jax.nn.softmax(top_vals, axis=-1)
        w_full = jnp.einsum('bsk,bske->bse', w, jax.nn.one_hot(top_idx, E, dtype=w.dtype))
        y = jnp.zeros(x.shape[:-1] + (DOUT,), x.dtype)
        for e in range(E):
            h = jax.nn.gelu(jnp.einsum('bsd,dh->bsh', xn, W1[e]) + b1[e], approximate=False)
            y_e = jnp.einsum('bsh,hd->bsd', h, W2[e]) + b2[e]
            y = y + y_e * w_full[..., e, None]
        return y

    def _L1_attn_ref(x, wq, wkv, wo, q_norm_w, k_norm_w):
        import jax, jax.numpy as jnp
        import numpy as np
        import math
        B, T, D_MODEL = (1, 512, 64)
        N_Q, N_KV = (16, 1)
        D_HEAD = D_MODEL // N_KV
        QPG = N_Q // N_KV
        ROPE_BASE = 10000.0
        WINDOW = 128
        EPS = 1.1920929e-07
        NEG = -1e+30

        def _rope(x, base=ROPE_BASE):
            t, d = (x.shape[-2], x.shape[-1])
            freqs = base ** (-2.0 * jnp.arange(d // 2, dtype=jnp.float32) / d)
            theta = jnp.arange(t, dtype=jnp.float32)[:, None] * freqs[None, :]
            cos, sin = (jnp.cos(theta), jnp.sin(theta))
            x1, x2 = (x[..., 0::2], x[..., 1::2])
            r1 = x1 * cos - x2 * sin
            r2 = x1 * sin + x2 * cos
            return jnp.stack([r1, r2], axis=-1).reshape(x.shape)

        def _rmsnorm(x, w):
            return x * jax.lax.rsqrt(jnp.mean(x * x, axis=-1, keepdims=True) + EPS) * w
        Bx, Tx, C = x.shape
        q = x @ wq.T
        kv = x @ wkv.T
        k, v = (kv[..., :N_KV * D_HEAD], kv[..., N_KV * D_HEAD:])
        q = q.reshape(Bx, Tx, QPG, N_KV, D_HEAD).transpose(0, 2, 3, 1, 4)
        k = k.reshape(Bx, Tx, 1, N_KV, D_HEAD).transpose(0, 2, 3, 1, 4)
        v = v.reshape(Bx, Tx, 1, N_KV, D_HEAD).transpose(0, 2, 3, 1, 4)
        q = _rmsnorm(_rope(q), q_norm_w)
        k = _rmsnorm(_rope(k), k_norm_w)
        rows = jnp.arange(Tx)[:, None]
        cols = jnp.arange(Tx)[None, :]
        mask = (cols <= rows) & (rows - cols <= WINDOW)
        scale = 1.0 / math.sqrt(D_HEAD)
        scores = jnp.einsum('bqgtd,bqgsd->bqgts', q, k) * scale
        scores = jnp.where(mask[None, None, None], scores, NEG)
        attn = jax.nn.softmax(scores, axis=-1)
        out = jnp.einsum('bqgts,bqgsd->bqgtd', attn, v)
        out = out.transpose(0, 3, 1, 2, 4).reshape(Bx, Tx, QPG * N_KV * D_HEAD)
        return out @ wo.T

    def _L1_ffn_ref(x, attention_mask, wr, br, w1, b1, w2, b2):
        import jax, jax.numpy as jnp
        import numpy as np
        B, S, D = (8, 1024, 64)
        H = 4 * D
        CAPACITY = 0.5
        b, s, d = x.shape
        weights = (jnp.einsum('bsd,do->bso', x, wr) + br)[..., 0]
        k = max(1, int(CAPACITY * s))
        kk = k - 1 if k > 1 else 1
        _, idx = jax.lax.top_k(weights, k)
        sel_idx = idx[:, :kk]
        sel = jnp.take_along_axis(x, sel_idx[:, :, None], axis=1)
        h = jax.nn.gelu(jnp.einsum('bkd,dh->bkh', sel, w1) + b1)
        y = jnp.einsum('bkh,hd->bkd', h, w2) + b2
        w_sel = jnp.take_along_axis(weights, sel_idx, axis=1)
        y = y * w_sel[..., None]
        batch_idx = jnp.arange(b)[:, None]
        processed = jnp.zeros_like(x).at[batch_idx, sel_idx].set(y)
        return processed + x
    h = _L0_tok_ref(x, L0_tok_turns, L0_tok_poly_coeffs)
    h = h + _L0_attn_ref(_layernorm(h, axis=-1), L0_attn_Q, L0_attn_E)
    h = h + _L0_ffn_ref(_layernorm(h, axis=-1), L0_ffn_gamma, L0_ffn_beta, L0_ffn_Wr, L0_ffn_br, L0_ffn_W1, L0_ffn_b1, L0_ffn_W2, L0_ffn_b2)
    h = h + _L1_attn_ref(_layernorm(h, axis=-1), L1_attn_wq, L1_attn_wkv, L1_attn_wo, L1_attn_q_norm_w, L1_attn_k_norm_w)
    h = h + _L1_ffn_ref(_layernorm(h, axis=-1), L1_ffn_attention_mask, L1_ffn_wr, L1_ffn_br, L1_ffn_w1, L1_ffn_b1, L1_ffn_w2, L1_ffn_b2)
    return h

_drawn_inputs = setup_inputs


def setup_inputs(seed=0):
    import zlib

    import numpy as np

    out = dict(_drawn_inputs(seed))
    spreads = {'L0_ffn_br': (0.0, 0.8),
     'L1_attn_q_norm_w': (1.0, 0.6),
     'L1_attn_k_norm_w': (1.0, 0.6),
     'L1_ffn_b1': (0.0, 2.0),
     'L1_ffn_b2': (0.0, 2.0)}
    factors = {'L0_ffn_gamma': 23.514,
     'L0_ffn_beta': 25.689,
     'L0_ffn_Wr': 8.0,
     'L0_ffn_W1': 8.0,
     'L0_ffn_b1': 64.0,
     'L0_ffn_W2': 8.0,
     'L0_ffn_b2': 64.0,
     'L1_attn_wq': 8.0,
     'L1_attn_wkv': 8.0,
     'L1_attn_wo': 8.0,
     'L1_ffn_wr': 8.0,
     'L1_ffn_w1': 54.296,
     'L1_ffn_w2': 41.468}
    for name, (base, spread) in spreads.items():
        noise = np.random.default_rng([zlib.crc32(name.encode()), seed]).standard_normal(out[name].shape)
        drawn = base * np.exp(spread * noise) if base else spread * noise
        out[name] = jnp.asarray(drawn.astype(out[name].dtype))
    for name, factor in factors.items():
        out[name] = (out[name] * factor).astype(out[name].dtype)
    return out
```

```python
from contextlib import ExitStack

import numpy as np

import concourse.bass as bass
from concourse import mybir

F32 = mybir.dt.float32
BF16 = mybir.dt.bfloat16
I32 = mybir.dt.int32
U32 = mybir.dt.uint32
ALU = mybir.AluOpType
ACT = mybir.ActivationFunctionType
AX = mybir.AxisListType.X

P = 128
B, S, D = 32, 512, 64
NT = S // P
TURNS, DEG = 4, 5
NF = TURNS * DEG
H0 = 8
HP0 = H0 // 2
NE, HID = 8, 128
NQ = 16
NP = NQ // 2
FF = 256
FC = FF // P
KEEP = 255
EPS = 1e-5
RMS_EPS = 1.1920929e-07
NEG = -1e30
TAKEN = -3.0e38
QK = NQ + 1
VC = D + 1
BANK = 512


def wait(eng, sem, value):
    if isinstance(value, int) and value <= 0:
        return
    eng.wait_ge(sem, value)


def apart(eng, passed):
    eng.sem_inc(passed, 1)


def each(ap, n):
    return ap.unsqueeze(2).broadcast_to([ap.shape[0], ap.shape[1], n])


def flat(ap):
    return ap.rearrange("p a b -> p (a b)")


def row(hid, b):
    return hid[:, bass.ds(b, 1), :, :].rearrange("p o a b -> p (o a) b")


LN_STEPS = 4


def layernorm_dve(eng, b, src, cent, sq, st, dst, step, var_ready, rstd_ready, ready):
    base = LN_STEPS * b
    eng.tensor_reduce(st[:, 0, :], src, AX, ALU.add).then_inc(step, 1)
    eng.wait_ge(step, base + 1)
    eng.tensor_scalar(st[:, 1, :], st[:, 0, :], 1.0 / D, None, ALU.mult).then_inc(step, 1)
    eng.wait_ge(step, base + 2)
    eng.tensor_tensor(cent, src, each(st[:, 1, :], D), ALU.subtract).then_inc(step, 1)
    eng.wait_ge(step, base + 3)
    eng.tensor_tensor(sq, cent, cent, ALU.mult).then_inc(step, 1)
    eng.wait_ge(step, base + 4)
    eng.tensor_reduce(st[:, 2, :], sq, AX, ALU.add).then_inc(var_ready, 1)
    eng.wait_ge(rstd_ready, b + 1)
    for d in dst:
        last = eng.tensor_tensor(d, cent, each(st[:, 3, :], D), ALU.mult)
    last.then_inc(ready, 1)


def rstd_pool(eng, n, out, ssum, tmp, mhalf, width, eps, sum_ready, tmp_ready, ready, passed):
    eng.wait_ge(sum_ready, n + 1)
    apart(eng, passed)
    eng.tensor_scalar(tmp, ssum, 1.0 / width, eps, ALU.mult, ALU.add).then_inc(tmp_ready, 1)
    eng.wait_ge(tmp_ready, n + 1)
    eng.tensor_tensor(out, tmp, mhalf, ALU.pow).then_inc(ready, 1)


def batches(eng, body, first=0, last=B):
    body(first)
    with eng.Fori(first + 1, last, 1) as b:
        body(b)


def embed_attend_experts(nc, w, ids, turns, hid, psum):
    with ExitStack() as ctx:
        def sb(name, shape, dt=F32):
            return ctx.enter_context(nc.sbuf_tensor(name, shape, dt))

        def sem(name):
            return ctx.enter_context(nc.semaphore(name))

        def bank(n, lo, hi, parts=P):
            return psum[0:parts, n * BANK + lo:n * BANK + hi]

        idx = sb("idx", [P, NT], I32)
        gath = sb("gath", [P, NT * TURNS])
        tk = sb("tk", [P, 6, NT * TURNS])
        tki = sb("tki", [P, NT * TURNS], I32)
        xp = sb("xp", [P, NT, TURNS, DEG])
        xpT = sb("xpT", [NF, S])
        h0 = sb("h0", [P, NT, D])
        lnc = sb("lnc", [P, NT, D])
        lnq = sb("lnq", [P, NT, D])
        lns = sb("lns", [P, 5, NT])
        r2 = sb("r2", [P, NT, 2, D])
        rT = sb("rT", [P, S])
        AT = sb("AT", [P, HP0, S])
        V0 = sb("V0", [P, 2, H0 * D])
        Om = sb("Om", [P, 2, H0, P])
        Gs = sb("Gs", [D, D])
        GEs = sb("GEs", [P, HP0, D])
        h1 = sb("h1", [P, NT, D])
        zc = sb("zc", [P, NT, D])
        zq = sb("zq", [P, NT, D])
        zs = sb("zs", [P, 6, NT])
        z = sb("z", [P, NT, D])
        xnT = sb("xnT", [D, S])
        lg = sb("lg", [P, NT, NE])
        top = sb("top", [P, NT, 8])
        topi = sb("topi", [P, NT, 8], U32)
        topf = sb("topf", [P, NT, 8])
        gd = sb("gd", [P, 4, NT])
        gw = sb("gw", [P, 4, NT, NE])
        wfull = sb("wfull", [P, NT, NE])
        wT = sb("wT", [NT * NE, P])
        g = sb("g", [P, 2, S])
        ytmp = sb("ytmp", [P, 2, NT, D])
        acc = sb("acc", [P, NT, D])

        s_ids = sem("s_ids")
        s_gath = sem("s_gath")
        s_tk = sem("s_tk")
        s_xp = sem("s_xp")
        s_xpT = sem("s_xpT")
        s_xpTs = sem("s_xpTs")
        s_h0 = sem("s_h0")
        s_h0s = sem("s_h0s")
        s_ln = sem("s_ln")
        s_var = sem("s_var")
        s_vt = sem("s_vt")
        s_rstd = sem("s_rstd")
        s_r = sem("s_r")
        s_rT = sem("s_rT")
        s_rTs = sem("s_rTs")
        s_A = sem("s_A")
        s_As = sem("s_As")
        s_V = sem("s_V")
        s_Vs = sem("s_Vs")
        s_Om = sem("s_Om")
        s_Oms = sem("s_Oms")
        s_G = sem("s_G")
        s_Gs = sem("s_Gs")
        s_GE = sem("s_GE")
        s_GEs = sem("s_GEs")
        s_att = sem("s_att")
        s_h1 = sem("s_h1")
        s_zln = sem("s_zln")
        s_zvar = sem("s_zvar")
        s_zvt = sem("s_zvt")
        s_zrstd = sem("s_zrstd")
        s_z = sem("s_z")
        s_zT = sem("s_zT")
        s_xn = sem("s_xn")
        s_lg = sem("s_lg")
        s_gate = sem("s_gate")
        s_gd = sem("s_gd")
        s_th = sem("s_th")
        s_w = sem("s_w")
        s_wT = sem("s_wT")
        s_wTs = sem("s_wTs")
        s_b2 = sem("s_b2")
        s_acc0 = sem("s_acc0")
        s_hT = sem("s_hT")
        s_g = sem("s_g")
        s_y = sem("s_y")
        s_yt = sem("s_yt")
        s_acc = sem("s_acc")

        GATE_STEPS = 5 + 2 * NT
        TK_STEPS = 9

        passed_pool, passed_pe, passed_dve = (sem(f"s1_passed_{e}") for e in ("pool", "pe", "dve"))

        block = ctx.enter_context(nc.Block())

        @block.sync
        def _(sp):
            def load(b):
                wait(sp, s_gath, 64 * b)
                sp.dma_start(idx[:, :], ids[:, bass.ds(b * NT, NT)]).then_inc(s_ids, 16)
            batches(sp, load)

        @block.gpsimd
        def _(pool):
            def gather(b):
                pool.wait_ge(s_ids, 16 * b + 16)
                wait(pool, s_xp, b)
                apart(pool, passed_pool)
                for j in range(NT):
                    pool.indirect_dma_start(gath[:, j * TURNS:(j + 1) * TURNS], None, turns,
                                            bass.IndirectOffsetOnAxis(ap=idx[:, j:j + 1], axis=0)
                                            ).then_inc(s_gath, 16)

            def attend_norm(b):
                rstd_pool(pool, b, lns[:, 3, :], lns[:, 2, :], lns[:, 4, :], w["mhalf"][:, 0:NT], D, EPS,
                          s_var, s_vt, s_rstd, passed_pool)

            def expert_norm(b):
                pool.wait_ge(s_zvar, b + 1)
                apart(pool, passed_pool)
                v, t, r = zs[:, 2, :], zs[:, 4, :], zs[:, 5, :]
                pool.tensor_scalar(t, v, 1.0 / D, EPS, ALU.mult, ALU.add).then_inc(s_zvt, 1)
                pool.wait_ge(s_zvt, 6 * b + 1)
                pool.tensor_tensor(r, t, w["mhalf"][:, 0:NT], ALU.pow).then_inc(s_zvt, 1)
                pool.wait_ge(s_zvt, 6 * b + 2)
                pool.tensor_tensor(t, r, r, ALU.mult).then_inc(s_zvt, 1)
                pool.wait_ge(s_zvt, 6 * b + 3)
                pool.tensor_tensor(t, t, v, ALU.mult).then_inc(s_zvt, 1)
                pool.wait_ge(s_zvt, 6 * b + 4)
                apart(pool, passed_pool)
                pool.tensor_scalar(t, t, 1.0 / D, EPS, ALU.mult, ALU.add).then_inc(s_zvt, 1)
                pool.wait_ge(s_zvt, 6 * b + 5)
                pool.tensor_tensor(t, t, w["mhalf"][:, 0:NT], ALU.pow).then_inc(s_zvt, 1)
                pool.wait_ge(s_zvt, 6 * b + 6)
                pool.tensor_tensor(zs[:, 3, :], t, r, ALU.mult).then_inc(s_zrstd, 1)

            gather(0)
            attend_norm(0)
            def both(b):
                gather(b)
                expert_norm(b - 1)
                attend_norm(b)

            both(1)
            with pool.Fori(2, B, 1) as b:
                both(b)
            expert_norm(B - 1)

        @block.tensor
        def _(pe):
            def mm(out, lhsT, rhs, start=True, stop=True):
                return pe.matmul(out, lhsT, rhs, start=start, stop=stop)

            def embed(b):
                wait(pe, s_h1, NT * b)
                pe.wait_ge(s_xp, b + 1)
                for j in range(NT):
                    last = pe.transpose(bank(0, j * P, j * P + P, NF), xp[:, j, :, :].rearrange("p a b -> p (a b)"),
                                        w["ident"][:, :])
                last.then_inc(s_xpT, 1)
                wait(pe, s_Vs, NT * b)
                pe.wait_ge(s_xpTs, b + 1)
                for j in range(NT):
                    last = mm(bank(1, j * D, j * D + D), xpT[:, j * P:(j + 1) * P], w["coef"][:, :])
                last.then_inc(s_h0, 1)

            def project(b):
                pe.wait_ge(s_r, b + 1)
                for j in range(NT):
                    last = pe.transpose(bank(0, j * P, j * P + P), r2[:, j, :, :].rearrange("p a b -> p (a b)"),
                                        w["ident"][:, :])
                last.then_inc(s_rT, 1)
                pe.wait_ge(s_rTs, b + 1)
                for p in range(HP0):
                    if p == 1:
                        wait(pe, s_Oms, NT * b)
                    if p >= 2:
                        pe.wait_ge(s_As, HP0 * b + p - 1)
                    mm(bank(1 + p % 2, 0, S), w["qw0"][:, p * P:(p + 1) * P], rT[0:D, :]).then_inc(s_A, 1)

            def attend(b, j):
                t = slice(j * P, (j + 1) * P)
                if j == 0:
                    pe.wait_ge(s_As, HP0 * b + HP0)
                else:
                    pe.wait_ge(s_Vs, NT * b + j)
                    pe.wait_ge(s_Oms, NT * b + j)
                mm(bank(1, 0, H0 * D), rT[0:D, t], w["ew0"][0:D, :]).then_inc(s_V, 1)
                if j == 0:
                    wait(pe, s_Oms, NT * b)
                for h in range(H0):
                    c = slice((h % 2) * D, (h % 2) * D + D)
                    o = (2 + h % 2) * BANK + h // 2 * P
                    last = mm(psum[:, o:o + P], rT[c, t], AT[c, h // 2, t])
                last.then_inc(s_Om, 1)
                if j >= 1:
                    r = r2[:, j - 1, 0, :]
                    pe.wait_ge(s_h1, NT * b + j)
                    apart(pe, passed_pe)
                    mm(bank(0, 0, D, D), r, r).then_inc(s_G, 1)
                    pe.wait_ge(s_Gs, 3 * b + j)
                    apart(pe, passed_pe)
                    for half in range(2):
                        o = half * D
                        last = mm(psum[o:o + D, D:D + HP0 * D], Gs[:, :],
                                  w["ew0"][:, :].rearrange("p (c two d) -> p c two d", two=2, d=D)[:, :, half, :])
                    last.then_inc(s_GE, 1)
                pe.wait_ge(s_Vs, NT * b + j + 1)
                pe.wait_ge(s_Oms, NT * b + j + 1)
                if j >= 1:
                    pe.wait_ge(s_GEs, 3 * b + j)
                dst = bank(0, 5 * D, 6 * D)
                for h in range(H0):
                    last = mm(dst, Om[:, j % 2, (h % 2) * HP0 + h // 2, :], V0[:, j % 2, h * D:(h + 1) * D], h == 0,
                              j == 0 and h == H0 - 1)
                if j >= 1:
                    for p in range(HP0):
                        last = mm(dst, AT[:, p, t], GEs[:, p, :], False, p == HP0 - 1)
                last.then_inc(s_att, 1)

            def expert_input(b):
                pe.wait_ge(s_z, b + 1)
                wait(pe, s_acc0, b)
                apart(pe, passed_pe)
                for j in range(NT):
                    last = pe.transpose(bank(4, j * P, j * P + P, D), z[:, j, :], w["ident"][:, :])
                last.then_inc(s_zT, 1)

            def gate_logits(b):
                pe.wait_ge(s_xn, b + 1)
                for j in range(NT):
                    last = mm(bank(4, j * NE, j * NE + NE), xnT[:, j * P:(j + 1) * P], w["wr0"][:, :])
                last.then_inc(s_lg, 1)

            def gate_bias(b):
                pe.wait_ge(s_w, b + 1)
                pe.transpose(bank(4, P, 2 * P, NT * NE), wfull[:, :, :].rearrange("p a b -> p (a b)"),
                             w["ident"][:, :]).then_inc(s_wT, 1)
                pe.wait_ge(s_wTs, b + 1)
                for j in range(NT):
                    last = mm(bank(4, 2 * P + j * D, 2 * P + j * D + D), wT[:, :], w["b2p"][:, j, :])
                last.then_inc(s_b2, 1)

            def expert_hidden(b, e):
                wait(pe, s_g, NE * b + e - 1)
                mm(bank(5 + e % 2, 0, S), w["w1e"][:, e, :], xnT[:, :]).then_inc(s_hT, 1)

            def expert_out(b, e):
                pe.wait_ge(s_g, NE * b + e + 1)
                wait(pe, s_yt, NE * b + e)
                for j in range(NT):
                    last = mm(bank(7, j * D, j * D + D), g[:, e % 2, j * P:(j + 1) * P], w["w2e"][:, e, :])
                last.then_inc(s_y, 1)

            def experts(b, j):
                for e in (2 * j, 2 * j + 1):
                    expert_out(b, e)
                    if e + 2 < NE:
                        expert_hidden(b, e + 2)

            embed(0)
            project(0)
            for j in range(NT):
                attend(0, j)
            def both(b):
                expert_input(b - 1)
                embed(b)
                gate_logits(b - 1)
                project(b)
                expert_hidden(b - 1, 0)
                expert_hidden(b - 1, 1)
                gate_bias(b - 1)
                for j in range(NT):
                    attend(b, j)
                    experts(b - 1, j)

            both(1)
            with pe.Fori(2, B, 1) as b:
                both(b)
            expert_input(B - 1)
            gate_logits(B - 1)
            gate_bias(B - 1)
            expert_hidden(B - 1, 0)
            expert_hidden(B - 1, 1)
            for j in range(NT):
                experts(B - 1, j)

        @block.scalar
        def _(act):
            def embed(b):
                act.wait_ge(s_xpT, b + 1)
                act.copy(xpT[:, :], bank(0, 0, S, NF)).then_inc(s_xpTs, 1)

            def project(b):
                act.wait_ge(s_rT, b + 1)
                act.copy(rT[:, :], bank(0, 0, S)).then_inc(s_rTs, 1)
                for p in range(HP0):
                    act.wait_ge(s_A, HP0 * b + p + 1)
                    act.copy(AT[:, p, :], bank(1 + p % 2, 0, S)).then_inc(s_As, 1)

            def attend(b, j):
                act.wait_ge(s_V, NT * b + j + 1)
                if j >= 2:
                    act.wait_ge(s_att, NT * b + j - 1)
                act.copy(V0[:, j % 2, :], bank(1, 0, H0 * D)).then_inc(s_Vs, 1)
                if j >= 1:
                    act.wait_ge(s_GE, 3 * b + j)
                    act.wait_ge(s_att, NT * b + j)
                    act.copy(GEs[:, :, :].rearrange("p a b -> p (a b)"), bank(0, D, D + HP0 * D)).then_inc(s_GEs, 1)

            def expert_input(b):
                act.wait_ge(s_zT, b + 1)
                wait(act, s_hT, NE * b)
                act.activation(xnT[:, :], bank(4, 0, S, D), ACT.Identity, bias=w["bet"][:, 0:1],
                               scale=w["gam"][:, 0:1]).then_inc(s_xn, 1)

            def gate(b):
                act.wait_ge(s_gd, b + 1)
                act.activation(gd[:, 1, :], gd[:, 0, :], ACT.Tanh, scale=0.5).then_inc(s_th, 1)

            def gate_bias(b):
                act.wait_ge(s_wT, b + 1)
                act.copy(wT[:, :], bank(4, P, 2 * P, NT * NE)).then_inc(s_wTs, 1)

            def gelu(b, e):
                act.wait_ge(s_hT, NE * b + e + 1)
                wait(act, s_y, NE * b + e - 1)
                act.activation(g[:, e % 2, :], bank(5 + e % 2, 0, S), ACT.Gelu,
                               bias=w["b1e"][:, e:e + 1]).then_inc(s_g, 1)

            embed(0)
            project(0)
            for j in range(NT):
                attend(0, j)
            def both(b):
                expert_input(b - 1)
                embed(b)
                gate(b - 1)
                project(b)
                gate_bias(b - 1)
                gelu(b - 1, 0)
                gelu(b - 1, 1)
                for j in range(NT):
                    attend(b, j)
                    if j + 1 < NT:
                        gelu(b - 1, 2 * j + 2)
                        gelu(b - 1, 2 * j + 3)

            both(1)
            with act.Fori(2, B, 1) as b:
                both(b)
            expert_input(B - 1)
            gate(B - 1)
            gate_bias(B - 1)
            for e in range(NE):
                gelu(B - 1, e)

        @block.vector
        def _(dve):
            def powers(b):
                base = TK_STEPS * b
                xv = xp[:, :, :, :].rearrange("p a t d -> p (a t) d")
                dve.wait_ge(s_gath, 64 * b + 64)
                wait(dve, s_xpT, b)
                dve.scalar_tensor_tensor(tk[:, 0, :], gath[:, :], -1.0, gath[:, :], ALU.mult, ALU.max).then_inc(s_tk, 1)
                dve.wait_ge(s_tk, base + 1)
                dve.tensor_copy(tki[:, :], tk[:, 0, :]).then_inc(s_tk, 1)
                dve.wait_ge(s_tk, base + 2)
                dve.tensor_copy(tk[:, 1, :], tki[:, :]).then_inc(s_tk, 1)
                dve.wait_ge(s_tk, base + 3)
                dve.tensor_tensor(tk[:, 2, :], tk[:, 1, :], tk[:, 0, :], ALU.is_gt).then_inc(s_tk, 1)
                dve.wait_ge(s_tk, base + 4)
                dve.tensor_tensor(tk[:, 3, :], tk[:, 1, :], tk[:, 2, :], ALU.subtract).then_inc(s_tk, 1)
                dve.tensor_scalar(tk[:, 4, :], gath[:, :], 0.0, 2.0, ALU.is_ge, ALU.mult).then_inc(s_tk, 1)
                dve.wait_ge(s_tk, base + 6)
                dve.scalar_tensor_tensor(xv[:, :, 1], tk[:, 4, :], -1.0, tk[:, 3, :], ALU.add, ALU.mult).then_inc(s_tk, 1)
                dve.wait_ge(s_tk, base + 7)
                dve.tensor_tensor(xv[:, :, 2], xv[:, :, 1], xv[:, :, 1], ALU.mult).then_inc(s_tk, 1)
                dve.wait_ge(s_tk, base + 8)
                dve.tensor_tensor(xv[:, :, 3], xv[:, :, 1], xv[:, :, 2], ALU.mult).then_inc(s_tk, 1)
                dve.tensor_tensor(xv[:, :, 4], xv[:, :, 2], xv[:, :, 2], ALU.mult).then_inc(s_xp, 1)

            def attend_input(b):
                dve.wait_ge(s_h0, b + 1)
                dve.tensor_copy(flat(h0[:, :, :]), bank(1, 0, NT * D)).then_inc(s_h0s, 1)
                dve.wait_ge(s_h0s, b + 1)
                wait(dve, s_att, NT * b)
                layernorm_dve(dve, b, h0[:, :, :], lnc[:, :, :], lnq[:, :, :], lns, [r2[:, :, 0, :], r2[:, :, 1, :]],
                              s_ln, s_var, s_rstd, s_r)

            def attend(b, j):
                dve.wait_ge(s_Om, NT * b + j + 1)
                if j >= 2:
                    dve.wait_ge(s_att, NT * b + j - 1)
                dve.tensor_tensor(Om[:, j % 2, :, :], psum[:, 2 * BANK:4 * BANK].rearrange("p (h t) -> p h t", t=P),
                                  w["causal"][:, :].unsqueeze(1).broadcast_to([P, H0, P]), ALU.mult).then_inc(s_Oms, 1)
                if j >= 1:
                    dve.wait_ge(s_G, 3 * b + j)
                    if j == 1:
                        dve.tensor_copy(Gs[:, :], bank(0, 0, D, D)).then_inc(s_Gs, 1)
                    else:
                        dve.wait_ge(s_GE, 3 * b + j - 1)
                        dve.tensor_tensor(Gs[:, :], Gs[:, :], bank(0, 0, D, D), ALU.add).then_inc(s_Gs, 1)

            def residual(b, j):
                dve.wait_ge(s_att, NT * b + j + 1)
                dve.tensor_tensor(h1[:, j, :], h0[:, j, :], bank(0, 5 * D, 6 * D), ALU.add).then_inc(s_h1, 1)

            def expert_input(b):
                dve.wait_ge(s_h1, NT * b + NT)
                wait(dve, s_zT, b)
                layernorm_dve(dve, b, h1[:, :, :], zc[:, :, :], zq[:, :, :], zs, [z[:, :, :]],
                              s_zln, s_zvar, s_zrstd, s_z)

            def gate(b):
                base = GATE_STEPS * b
                dve.wait_ge(s_lg, b + 1)
                dve.tensor_tensor(lg[:, :, :], bank(4, 0, NT * NE).rearrange("p (a e) -> p a e", e=NE),
                                  w["br0"][:, :].unsqueeze(1).broadcast_to([P, NT, NE]), ALU.add).then_inc(s_gate, 1)
                dve.wait_ge(s_gate, base + 1)
                apart(dve, passed_dve)
                for j in range(NT):
                    dve.max(top[:, j, :], lg[:, j, :]).then_inc(s_gate, 1)
                for j in range(NT):
                    dve.wait_ge(s_gate, base + 2 + j)
                    apart(dve, passed_dve)
                    dve.max_index(topi[:, j, :], top[:, j, :], lg[:, j, :]).then_inc(s_gate, 1)
                dve.tensor_tensor(gd[:, 0, :], top[:, :, 0], top[:, :, 1], ALU.subtract).then_inc(s_gd, 1)
                dve.wait_ge(s_gate, base + 1 + 2 * NT)
                dve.tensor_copy(topf[:, :, :], topi[:, :, :]).then_inc(s_gate, 1)
                dve.wait_ge(s_gate, base + 2 + 2 * NT)
                for k in range(2):
                    dve.tensor_tensor(gw[:, k, :, :], w["iota8"][:, :].unsqueeze(1).broadcast_to([P, NT, NE]),
                                      each(topf[:, :, k], NE), ALU.is_equal)
                dve.wait_ge(s_th, b + 1)
                dve.tensor_scalar(gd[:, 2, :], gd[:, 1, :], 0.5, 0.5, ALU.mult, ALU.add)
                dve.tensor_scalar(gd[:, 3, :], gd[:, 1, :], -0.5, 0.5, ALU.mult, ALU.add).then_inc(s_gate, 1)
                dve.wait_ge(s_gate, base + 3 + 2 * NT)
                for k in range(2):
                    dve.tensor_tensor(gw[:, 2 + k, :, :], gw[:, k, :, :], each(gd[:, 2 + k, :], NE),
                                      ALU.mult).then_inc(s_gate, 1)
                dve.wait_ge(s_gate, base + 5 + 2 * NT)
                wait(dve, s_wT, b)
                dve.tensor_tensor(wfull[:, :, :], gw[:, 2, :, :], gw[:, 3, :, :], ALU.add).then_inc(s_w, 1)

            def start_sum(b):
                dve.wait_ge(s_b2, b + 1)
                dve.tensor_tensor(flat(acc[:, :, :]), flat(h1[:, :, :]), bank(4, 2 * P, 2 * P + NT * D),
                                  ALU.add).then_inc(s_acc0, 1)

            def add_expert(b, e):
                dve.wait_ge(s_y, NE * b + e + 1)
                dve.tensor_tensor(ytmp[:, e % 2, :, :], bank(7, 0, NT * D).rearrange("p (a d) -> p a d", d=D),
                                  each(wfull[:, :, e], D), ALU.mult).then_inc(s_yt, 1)
                dve.wait_ge(s_yt, NE * b + e + 1)
                if e == 0:
                    dve.wait_ge(s_acc0, b + 1)
                else:
                    dve.wait_ge(s_acc, NE * b + e)
                dst = acc[:, :, :] if e < NE - 1 else row(hid, b)
                dve.tensor_tensor(dst, acc[:, :, :], ytmp[:, e % 2, :, :], ALU.add).then_inc(s_acc, 1)

            dve.memset(xp[:, :, :, 0:1], 1.0)
            powers(0)
            attend_input(0)
            for j in range(NT):
                attend(0, j)
                residual(0, j)
            def both(b):
                expert_input(b - 1)
                powers(b)
                gate(b - 1)
                attend_input(b)
                start_sum(b - 1)
                for j in range(NT):
                    attend(b, j)
                    add_expert(b - 1, 2 * j)
                    residual(b, j)
                    add_expert(b - 1, 2 * j + 1)

            both(1)
            with dve.Fori(2, B, 1) as b:
                both(b)
            expert_input(B - 1)
            gate(B - 1)
            start_sum(B - 1)
            for e in range(NE):
                add_expert(B - 1, e)


def windowed_attention(nc, w, hid, psum):
    with ExitStack() as ctx:
        def sb(name, shape, dt=F32):
            return ctx.enter_context(nc.sbuf_tensor(name, shape, dt))

        def sem(name):
            return ctx.enter_context(nc.semaphore(name))

        lnc = sb("lnc2", [P, NT, D])
        lnq = sb("lnq2", [P, NT, D])
        lns = sb("lns2", [P, 5, NT])
        x2 = sb("x2", [P, NT, D])
        xT = sb("xT", [D, S])
        sq = sb("sq", [P, QK, D])
        ss = sb("ss", [P, 3, QK])
        ra = sb("ra", [P, QK, D])
        rb = sb("rb", [P, QK, D])
        rc = sb("rc", [P, QK, D])
        qn = sb("qn", [P, QK + 1, D])
        qT = sb("qT", [P, 2, NP, P])
        qTb = sb("qTb", [P, 2, NP, P], BF16)
        kT = sb("kT", [P, S])
        kTb = sb("kTb", [P, S], BF16)
        vv = sb("vv", [P, NT, VC])
        mb = sb("mb", [P, 2, NQ], BF16)
        prob = sb("prob", [P, 2, 2, 2, P])
        rcp = sb("rcp", [P, 2, 2])
        o = sb("o", [P, NQ, D])
        oT = sb("oT", [P, NP, P])

        s_ln = sem("s2_ln")
        s_var = sem("s2_var")
        s_vt = sem("s2_vt")
        s_rstd = sem("s2_rstd")
        s_x = sem("s2_x")
        s_xT = sem("s2_xT")
        s_xTs = sem("s2_xTs")
        s_qkv = sem("s2_qkv")
        s_sq = sem("s2_sq")
        s_ssum = sem("s2_ssum")
        s_sst = sem("s2_sst")
        s_rms = sem("s2_rms")
        s_rab = sem("s2_rab")
        s_rot = sem("s2_rot")
        s_qn = sem("s2_qn")
        s_qkT = sem("s2_qkT")
        s_qTs = sem("s2_qTs")
        s_qTb = sem("s2_qTb")
        s_S1 = sem("s2_S1")
        s_m = sem("s2_m")
        s_ST = sem("s2_ST")
        s_e = sem("s2_e")
        s_p = sem("s2_p")
        s_pv = sem("s2_pv")
        s_rcp = sem("s2_rcp")
        s_o = sem("s2_o")
        s_oT = sem("s2_oT")
        s_oTs = sem("s2_oTs")
        s_y = sem("s2_y")
        s_h = sem("s2_h")

        proj = psum[:, 0:3 * BANK]
        qk_ps = proj[:, 0:QK * D].rearrange("p (h d) -> p h d", d=D)
        v_ps = proj[:, QK * D:(QK + 1) * D]
        kT_ps = proj[:, 1152:1152 + P]
        y_ps = proj[:, 1280:1280 + D]

        def blocks(j):
            return 2 if j > 0 else 1

        def pair(bank):
            return psum[:, bank * BANK:(bank + 2) * BANK].rearrange("p (h c) -> p h c", h=2)

        def probs(j, i):
            return prob[:, i % 2, :, :, :]

        def tiles(eng, step, final):
            def batch(b, last):
                for j in range(NT):
                    if j + 1 < NT:
                        step(b, j, b, j + 1)
                    elif not last:
                        step(b, j, b + 1, 0)
                    else:
                        final(b, j)
            batch(0, False)
            with eng.Fori(1, B - 1, 1) as b:
                batch(b, False)
            batch(B - 1, True)

        passed_pool, passed_pe, passed_dve = (sem(f"s2_passed_{e}") for e in ("pool", "pe", "dve"))

        block = ctx.enter_context(nc.Block())

        @block.gpsimd
        def _(pool):
            def norm(b):
                rstd_pool(pool, b, lns[:, 3, :], lns[:, 2, :], lns[:, 4, :], w["mhalf"][:, 0:NT], D, EPS,
                          s_var, s_vt, s_rstd, passed_pool)

            def rotate(b, j):
                n = NT * b + j
                rstd_pool(pool, n, ss[:, 2, :], ss[:, 0, :], ss[:, 1, :], w["mhalf"][:, :], D, RMS_EPS,
                          s_ssum, s_sst, s_rms, passed_pool)
                pool.wait_ge(s_rab, n + 1)
                pool.tensor_tensor(rc[:, :, :], ra[:, :, :], rb[:, :, :], ALU.add).then_inc(s_rot, 1)

            def round_qk(b, j):
                n = NT * b + j
                pool.wait_ge(s_qTs, n + 1)
                wait(pool, s_m, NP * (n - 1))
                apart(pool, passed_pool)
                pool.tensor_copy(kTb[:, j * P:(j + 1) * P], kT[:, j * P:(j + 1) * P])
                pool.tensor_copy(qTb[:, j % 2, :, :], qT[:, j % 2, :, :]).then_inc(s_qTb, 1)

            def window(b, j, i):
                n = NP * (NT * b + j) + i
                pool.wait_ge(s_e, n + 1)
                apart(pool, passed_pool)
                p = probs(j, i)
                last = pool.affine_select(out=p[:, :, 0, :], in_=p[:, :, 0, :], compare_op=ALU.is_ge, fill=0.0, base=0,
                                          pattern=[[0, 2], [1, P]], channel_multiplier=-1)
                if blocks(j) == 2:
                    last = pool.affine_select(out=p[:, :, 1, :], in_=p[:, :, 1, :], compare_op=ALU.is_ge, fill=0.0,
                                              base=0, pattern=[[0, 2], [-1, P]], channel_multiplier=1)
                last.then_inc(s_p, 1)

            def step(b, j, nb, nj):
                if nj == 0:
                    norm(nb)
                for i in range(3):
                    window(b, j, i)
                rotate(nb, nj)
                for i in range(3, NP):
                    window(b, j, i)
                round_qk(nb, nj)

            norm(0)
            rotate(0, 0)
            round_qk(0, 0)
            tiles(pool, step, lambda b, j: [window(b, j, i) for i in range(NP)])

        @block.tensor
        def _(pe):
            def mm(out, lhsT, rhs, start=True, stop=True):
                return pe.matmul(out, lhsT, rhs, start=start, stop=stop, skip_group_check=True)

            def transpose_x(b):
                pe.wait_ge(s_x, b + 1)
                wait(pe, s_oTs, 2 * NT * b - 2)
                apart(pe, passed_pe)
                for j in range(NT):
                    last = pe.transpose(proj[0:D, j * P:(j + 1) * P], x2[:, j, :], w["ident"][:, :])
                last.then_inc(s_xT, 1)

            def project(b, j):
                n = NT * b + j
                pe.wait_ge(s_xTs, b + 1)
                wait(pe, s_oTs, 2 * n - 2)
                wait(pe, s_h, n - 1)
                wait(pe, s_qTs, n)
                t = xT[:, j * P:(j + 1) * P]
                mm(proj[:, 0:BANK], t, w["wq1"][:, 0:BANK])
                mm(proj[:, BANK:2 * BANK], t, w["wq1"][:, BANK:2 * BANK])
                mm(proj[:, 2 * BANK:2 * BANK + 2 * D], t, w["wkv"][:, :]).then_inc(s_qkv, 1)

            def transpose_qk(b, j):
                n = NT * b + j
                pe.wait_ge(s_qn, n + 1)
                for i in range(NP):
                    pe.transpose(proj[:, i * P:(i + 1) * P], flat(qn[:, 2 * i:2 * i + 2, :]), w["ident"][:, :])
                pe.transpose(kT_ps, flat(qn[:, NQ:NQ + 2, :]), w["ident"][:, :]).then_inc(s_qkT, 1)

            def scores(b, j, i):
                n = NP * (NT * b + j) + i
                if i == 0:
                    pe.wait_ge(s_qTb, NT * b + j + 1)
                wait(pe, s_m, n)
                keys = P * blocks(j)
                first = P * (2 - blocks(j))
                for hh in range(2):
                    dst = pair(3)[:, hh, 0:keys]
                    c = slice(hh * D, hh * D + D)
                    mm(dst, w["identb"][:, :], w["wmask"][:, first:2 * P], True, False)
                    last = mm(dst, qTb[c, j % 2, i, :], kTb[c, (j + 1) * P - keys:(j + 1) * P], False, True)
                last.then_inc(s_S1, 1)

            def shifted(b, j, i):
                n = NP * (NT * b + j) + i
                pe.wait_ge(s_m, n + 1)
                wait(pe, s_e, n)
                for hh in range(2):
                    c = slice(hh * D, hh * D + D)
                    shift = mb[:, j % 2, 2 * i + hh:2 * i + hh + 1].broadcast_to([P, P])
                    for k in range(blocks(j)):
                        dst = pair(5)[:, hh, k * P:(k + 1) * P]
                        mm(dst, kT[c, (j - k) * P:(j - k + 1) * P], qT[c, j % 2, i, :], True, False)
                        last = mm(dst, shift, w["nidentb"][:, :], False, True)
                last.then_inc(s_ST, 1)

            def weigh(b, j, i):
                n = NP * (NT * b + j) + i
                pe.wait_ge(s_p, n + 1)
                wait(pe, s_o, n)
                for hh in range(2):
                    lo = 7 * BANK + hh * VC
                    for k in range(blocks(j)):
                        last = mm(psum[:, lo:lo + VC], probs(j, i)[:, hh, k, :], vv[:, j - k, :], k == 0,
                                  k == blocks(j) - 1)
                last.then_inc(s_pv, 1)

            def heads(b, j, mid):
                scores(b, j, 0)
                for i in range(NP):
                    if i + 1 < NP:
                        scores(b, j, i + 1)
                    shifted(b, j, i)
                    if i >= 1:
                        weigh(b, j, i - 1)
                    if i == 5 and mid is not None:
                        mid()
                weigh(b, j, NP - 1)

            def output(b, j):
                n = NT * b + j
                pe.wait_ge(s_o, NP * (n + 1))
                for c in range(2):
                    for i in range(NP // 2):
                        h = 2 * (c * NP // 2 + i)
                        last = pe.transpose(proj[:, c * BANK + i * P:c * BANK + (i + 1) * P],
                                            flat(o[:, h:h + 2, :]), w["ident"][:, :])
                    last.then_inc(s_oT, 1)
                for c in range(2):
                    pe.wait_ge(s_oTs, 2 * n + c + 1)
                    for i in range(c * NP // 2, (c + 1) * NP // 2):
                        last = mm(y_ps, oT[:, i, :], w["wo1"][:, i, :], i == 0, i == NP - 1)
                last.then_inc(s_y, 1)

            def step(b, j, nb, nj):
                n = NT * b + j
                if nj == 0:
                    transpose_x(nb)
                project(nb, nj)

                def mid():
                    transpose_qk(nb, nj)
                heads(b, j, mid)
                pe.wait_ge(s_qTs, n + 2)
                output(b, j)

            def final(b, j):
                heads(b, j, None)
                output(b, j)

            transpose_x(0)
            project(0, 0)
            transpose_qk(0, 0)
            tiles(pe, step, final)

        @block.scalar
        def _(act):
            def copy_xT(b):
                act.wait_ge(s_xT, b + 1)
                act.copy(xT[:, :], proj[0:D, 0:S]).then_inc(s_xTs, 1)

            def squares(b, j):
                n = NT * b + j
                act.wait_ge(s_qkv, n + 1)
                wait(act, s_ssum, n)
                wait(act, s_pv, NP * (n - 2))
                act.activation(sq[:, :, :], qk_ps, ACT.Square)
                act.copy(vv[:, j, 0:D], v_ps).then_inc(s_sq, 1)

            def copy_qk(b, j):
                n = NT * b + j
                act.wait_ge(s_qkT, n + 1)
                act.activation(flat(qT[:, j % 2, :, :]), proj[:, 0:NP * P], ACT.Copy, scale=w["qscale"][:, 0:1])
                act.activation(kT[:, j * P:(j + 1) * P], kT_ps, ACT.Copy, scale=w["knw"][:, 0:1]).then_inc(s_qTs, 1)

            def exps(b, j, i):
                n = NP * (NT * b + j) + i
                act.wait_ge(s_ST, n + 1)
                wait(act, s_pv, n - 1)
                n_k = blocks(j)
                act.activation(probs(j, i)[:, :, 0:n_k, :],
                               pair(5)[:, :, 0:n_k * P].rearrange("p h (k t) -> p h k t", t=P),
                               ACT.Exp).then_inc(s_e, 1)

            def output(b, j):
                n = NT * b + j
                for c in range(2):
                    act.wait_ge(s_oT, 2 * n + c + 1)
                    if c == 0:
                        wait(act, s_y, n)
                    act.copy(flat(oT[:, c * NP // 2:(c + 1) * NP // 2, :]),
                             proj[:, c * BANK:(c + 1) * BANK]).then_inc(s_oTs, 1)

            def step(b, j, nb, nj):
                if nj == 0:
                    copy_xT(nb)
                squares(nb, nj)
                for i in range(NP):
                    exps(b, j, i)
                    if i == 6:
                        copy_qk(nb, nj)
                output(b, j)

            def final(b, j):
                for i in range(NP):
                    exps(b, j, i)
                output(b, j)

            copy_xT(0)
            squares(0, 0)
            copy_qk(0, 0)
            tiles(act, step, final)

        @block.vector
        def _(dve):
            def norm(b):
                wait(dve, s_xT, b)
                layernorm_dve(dve, b, row(hid, b), lnc[:, :, :], lnq[:, :, :], lns, [x2[:, :, :]],
                              s_ln, s_var, s_rstd, s_x)

            def rotate(b, j):
                n = NT * b + j
                dve.wait_ge(s_sq, n + 1)
                wait(dve, s_rot, n)
                even = qk_ps[:, :, 0::2]
                odd = qk_ps[:, :, 1::2]
                dve.tensor_tensor(ra[:, :, :], qk_ps, w["cos_t"][:, j, :].unsqueeze(1).broadcast_to([P, QK, D]),
                                  ALU.mult)
                dve.tensor_tensor(rb[:, :, 0::2], odd, w["nsin_t"][:, j, :].unsqueeze(1).broadcast_to([P, QK, D // 2]),
                                  ALU.mult)
                dve.tensor_tensor(rb[:, :, 1::2], even, w["sin_t"][:, j, :].unsqueeze(1).broadcast_to([P, QK, D // 2]),
                                  ALU.mult).then_inc(s_rab, 1)
                dve.tensor_reduce(ss[:, 0, :], sq[:, :, :], AX, ALU.add).then_inc(s_ssum, 1)

            def normalise(b, j):
                n = NT * b + j
                dve.wait_ge(s_rot, n + 1)
                dve.wait_ge(s_rms, n + 1)
                wait(dve, s_qkT, n)
                dve.tensor_tensor(qn[:, 0:QK, :], rc[:, :, :], each(ss[:, 2, :], D), ALU.mult)
                dve.tensor_tensor(qn[:, QK:QK + 1, :], rc[:, NQ:QK, :], each(ss[:, 2, NQ:QK], D),
                                  ALU.mult).then_inc(s_qn, 1)

            def maximum(b, j, i):
                n = NP * (NT * b + j) + i
                dve.wait_ge(s_S1, n + 1)
                if i == 0:
                    wait(dve, s_ST, n - NP)
                dve.tensor_reduce(mb[:, j % 2, 2 * i:2 * i + 2],
                                  pair(3)[:, :, 0:P * blocks(j)], AX, ALU.max).then_inc(s_m, 1)

            def divide(b, j, i):
                n = NP * (NT * b + j) + i
                dve.wait_ge(s_pv, n + 1)
                if i == 0:
                    wait(dve, s_oT, 2 * (NT * b + j))
                pv = psum[:, 7 * BANK:7 * BANK + 2 * VC].rearrange(
                    "p (h c) -> p h c", c=VC)
                dve.reciprocal(rcp[:, i % 2, :], pv[:, :, D]).then_inc(s_rcp, 1)
                dve.wait_ge(s_rcp, n + 1)
                dve.tensor_tensor(o[:, 2 * i:2 * i + 2, :], pv[:, :, 0:D], each(rcp[:, i % 2, :], D),
                                  ALU.mult).then_inc(s_o, 1)

            def residual(b, j):
                dve.wait_ge(s_y, NT * b + j + 1)
                dst = row(hid, b)[:, j, :]
                dve.tensor_tensor(dst, dst, y_ps, ALU.add).then_inc(s_h, 1)

            def heads(b, j, early, mid):
                maximum(b, j, 0)
                maximum(b, j, 1)
                if early is not None:
                    early()
                for i in range(2, NP):
                    maximum(b, j, i)
                    divide(b, j, i - 2)
                    if i == 4 and mid is not None:
                        mid()
                divide(b, j, NP - 2)
                divide(b, j, NP - 1)

            def step(b, j, nb, nj):
                if nj == 0:
                    norm(nb)

                def early():
                    rotate(nb, nj)

                def mid():
                    normalise(nb, nj)
                heads(b, j, early, mid)
                residual(b, j)

            def final(b, j):
                heads(b, j, None, None)
                residual(b, j)

            dve.memset(vv[:, :, D:VC], 1.0)
            norm(0)
            rotate(0, 0)
            normalise(0, 0)
            tiles(dve, step, final)


def feed_forward(nc, w, hid, zw, wall, w_dram, psum):
    with ExitStack() as ctx:
        def sb(name, shape, dt=F32):
            return ctx.enter_context(nc.sbuf_tensor(name, shape, dt))

        def sem(name):
            return ctx.enter_context(nc.semaphore(name))

        def bank(n, lo, hi, parts=P):
            return psum[0:parts, n * BANK + lo:n * BANK + hi]

        lnc = sb("lnc3", [P, NT, D])
        lnq = sb("lnq3", [P, NT, D])
        lns = sb("lns3", [P, 5, NT])
        x3 = sb("x3", [P, NT, D])
        xT = sb("xT3", [D, S])
        gf = sb("gf", [P, FC, S])
        wcol = sb("wcol", [P, NT])
        yb = sb("yb", [P, NT, D])
        wrow = sb("wrow", [1, S])

        s_ln = sem("s3_ln")
        s_var = sem("s3_var")
        s_vt = sem("s3_vt")
        s_rstd = sem("s3_rstd")
        s_x = sem("s3_x")
        s_base = sem("s3_base")
        s_xT = sem("s3_xT")
        s_xTs = sem("s3_xTs")
        s_w = sem("s3_w")
        s_wrow = sem("s3_wrow")
        s_wall = sem("s3_wall")
        s_wback = sem("s3_wback")
        s_wcol = sem("s3_wcol")
        s_h = sem("s3_h")
        s_g = sem("s3_g")
        s_y = sem("s3_y")
        s_yb = sem("s3_yb")
        s_zw = sem("s3_zw")

        passed_pool, passed_pe, passed_dve = (sem(f"s3_passed_{e}") for e in ("pool", "pe", "dve"))

        block = ctx.enter_context(nc.Block())

        @block.sync
        def _(sp):
            def store(b):
                sp.wait_ge(s_wrow, b + 1)
                sp.dma_start(w_dram[bass.ds(b, 1), :], wrow[:, :]).then_inc(s_wall, 16)
            batches(sp, store)
            sp.wait_ge(s_wall, 16 * B)
            sp.dma_start(wall[:, :], w_dram[:, :]).then_inc(s_wback, 16)
            sp.wait_ge(s_wback, 16)

        @block.gpsimd
        def _(pool):
            batches(pool, lambda b: rstd_pool(pool, b, lns[:, 3, :], lns[:, 2, :], lns[:, 4, :],
                                              w["mhalf"][:, 0:NT], D, EPS, s_var, s_vt, s_rstd, passed_pool))

        @block.tensor
        def _(pe):
            def transpose_x(b):
                pe.wait_ge(s_x, b + 1)
                wait(pe, s_xTs, b)
                apart(pe, passed_pe)
                for j in range(NT):
                    last = pe.transpose(bank(0, j * P, j * P + P, D), x3[:, j, :], w["ident"][:, :])
                last.then_inc(s_xT, 1)

            def feed(b):
                pe.wait_ge(s_xTs, b + 1)
                wait(pe, s_wcol, b)
                wait(pe, s_wrow, b)
                for j in range(NT):
                    pe.matmul(bank(6, j, j + 1), xT[:, j * P:(j + 1) * P], w["wrf"][:, :], start=True, stop=True)
                pe.matmul(bank(7, 0, S, 1), w["wrf"][:, :], xT[:, :], start=True, stop=True).then_inc(s_w, 1)
                for c in range(FC):
                    wait(pe, s_g, FC * b)
                    pe.matmul(bank(1 + c, 0, S), w["w1f"][:, c * P:(c + 1) * P], xT[:, :], start=True,
                              stop=True).then_inc(s_h, 1)

            def out(b):
                pe.wait_ge(s_g, FC * b + FC)
                wait(pe, s_yb, b)
                for j in range(NT):
                    for c in range(FC):
                        last = pe.matmul(bank(5, j * D, j * D + D), gf[:, c, j * P:(j + 1) * P], w["w2f"][:, c, :],
                                         start=c == 0, stop=c == FC - 1)
                last.then_inc(s_y, 1)

            transpose_x(0)
            def both(b):
                feed(b - 1)
                transpose_x(b)
                out(b - 1)

            both(1)
            with pe.Fori(2, B, 1) as b:
                both(b)
            feed(B - 1)
            out(B - 1)

        @block.scalar
        def _(act):
            def copy_xT(b):
                act.wait_ge(s_xT, b + 1)
                wait(act, s_h, FC * b)
                act.copy(xT[:, :], bank(0, 0, S, D)).then_inc(s_xTs, 1)

            def feed(b):
                act.wait_ge(s_w, b + 1)
                wait(act, s_wall, 16 * b)
                act.activation(wrow[:, :], bank(7, 0, S, 1), ACT.Identity,
                               bias=w["brf"][0:1, 0:1]).then_inc(s_wrow, 1)
                for c in range(FC):
                    act.wait_ge(s_h, FC * b + c + 1)
                    wait(act, s_y, b)
                    act.activation(gf[:, c, :], bank(1 + c, 0, S), ACT.Gelu_apprx_tanh,
                                   bias=w["b1f"][:, c:c + 1]).then_inc(s_g, 1)

            copy_xT(0)
            def both(b):
                feed(b - 1)
                copy_xT(b)

            both(1)
            with act.Fori(2, B, 1) as b:
                both(b)
            feed(B - 1)

        @block.vector
        def _(dve):
            def norm(b):
                wait(dve, s_xT, b)
                layernorm_dve(dve, b, row(hid, b), lnc[:, :, :], lnq[:, :, :], lns, [x3[:, :, :]],
                              s_ln, s_var, s_rstd, s_x)
                dve.wait_ge(s_x, b + 1)
                dve.tensor_tensor(row(hid, b), row(hid, b), x3[:, :, :], ALU.add).then_inc(s_base, 1)

            def out(b):
                dve.wait_ge(s_w, b + 1)
                wait(dve, s_zw, b)
                dve.tensor_scalar(wcol[:, :], bank(6, 0, NT), w["brf"][:, 0:1], None, ALU.add).then_inc(s_wcol, 1)
                dve.wait_ge(s_y, b + 1)
                dve.tensor_tensor(yb[:, :, :], bank(5, 0, NT * D).rearrange("p (a d) -> p a d", d=D),
                                  w["b2f"][:, :].unsqueeze(1).broadcast_to([P, NT, D]), ALU.add).then_inc(s_yb, 1)
                dve.wait_ge(s_yb, b + 1)
                dve.tensor_tensor(row(zw, b), yb[:, :, :], each(wcol[:, :], D), ALU.mult).then_inc(s_zw, 1)

            norm(0)
            def both(b):
                norm(b)
                out(b - 1)

            both(1)
            with dve.Fori(2, B, 1) as b:
                both(b)
            out(B - 1)


def select_and_store(nc, w, hid, zw, wall, psum, out):
    OG = 4
    ROUNDS = (KEEP + 1) // 8
    with ExitStack() as ctx:
        def sb(name, shape, dt=F32):
            return ctx.enter_context(nc.sbuf_tensor(name, shape, dt))

        def sem(name):
            return ctx.enter_context(nc.semaphore(name))

        work = sb("work", [B, S])
        t8 = sb("t8", [B, 8])
        i8 = sb("i8", [B, 8], U32)
        i8f = sb("i8f", [B, 8])
        drop = sb("drop", [B, S])
        sel = sb("sel", [B, S])
        selT = sb("selT", [P, NT, B])
        add = sb("add", [P, 2, OG, NT, D])

        s_top = sem("s4_top")
        s_rep = sem("s4_rep")
        s_idx = sem("s4_idx")
        s_sel = sem("s4_sel")
        s_selT = sem("s4_selT")
        s_selTs = sem("s4_selTs")
        s_add = sem("s4_add")
        s_out = sem("s4_out")
        s_done = sem("s4_done")

        out_v = out.rearrange("b (j p) d -> p b j d", p=P)
        passed_pool, passed_pe, passed_dve = (sem(f"s4_passed_{e}") for e in ("pool", "pe", "dve"))

        block = ctx.enter_context(nc.Block())

        @block.vector
        def _(dve):
            dve.max(t8[:, :], wall[:, :]).then_inc(s_top, 1)
            dve.wait_ge(s_top, 1)
            dve.match_replace(work[:, :], t8[:, :], wall[:, :], TAKEN).then_inc(s_rep, 1)

            with dve.Fori(1, ROUNDS - 1, 1) as r:
                dve.wait_ge(s_rep, r)
                apart(dve, passed_dve)
                dve.max(t8[:, :], work[:, :]).then_inc(s_top, 1)
                dve.wait_ge(s_top, r + 1)
                apart(dve, passed_dve)
                dve.match_replace(work[:, :], t8[:, :], work[:, :], TAKEN).then_inc(s_rep, 1)
            dve.wait_ge(s_rep, ROUNDS - 1)
            dve.max(t8[:, :], work[:, :]).then_inc(s_top, 1)
            dve.wait_ge(s_top, ROUNDS)
            dve.max_index(i8[:, :], t8[:, :], work[:, :]).then_inc(s_idx, 1)
            dve.match_replace(work[:, :], t8[:, :], work[:, :], TAKEN).then_inc(s_rep, 1)
            dve.wait_ge(s_idx, 1)
            dve.tensor_copy(i8f[:, :], i8[:, :]).then_inc(s_idx, 1)
            dve.wait_ge(s_idx, 2)
            dve.tensor_scalar(drop[:, :], w["iota_row"][:, :], i8f[:, 7:8], None, ALU.is_equal).then_inc(s_idx, 1)
            dve.wait_ge(s_idx, 3)
            dve.wait_ge(s_rep, ROUNDS)
            dve.scalar_tensor_tensor(sel[:, :], work[:, :], TAKEN, drop[:, :], ALU.is_equal,
                                     ALU.subtract).then_inc(s_sel, 1)
            dve.wait_ge(s_selT, 1)
            dve.tensor_copy(selT[:, :, :].rearrange("p a b -> p (a b)"), psum[:, 0:NT * B]).then_inc(s_selTs, 1)
            dve.wait_ge(s_selTs, 1)
            for q in range(B // OG):
                rows = slice(q * OG, (q + 1) * OG)
                if q >= 2:
                    dve.wait_ge(s_out, q - 1)
                m = selT[:, :, rows].rearrange("p a b -> p b a").unsqueeze(3).broadcast_to([P, OG, NT, D])
                dve.tensor_tensor(add[:, q % 2, :, :, :], zw[:, rows, :, :], m, ALU.mult).then_inc(s_add, 1)
                dve.wait_ge(s_add, q + 1)
                dve.tensor_tensor(hid[:, rows, :, :], hid[:, rows, :, :], add[:, q % 2, :, :, :],
                                  ALU.add).then_inc(s_out, 1)

        @block.tensor
        def _(pe):
            pe.wait_ge(s_sel, 1)
            for j in range(NT):
                last = pe.transpose(psum[:, j * B:(j + 1) * B], sel[:, j * P:(j + 1) * P], w["ident"][0:B, 0:B])
            last.then_inc(s_selT, 1)

        @block.sync
        def _(sp):
            for q in range(B // OG):
                sp.wait_ge(s_out, q + 1)
                sp.dma_start(out_v[:, q * OG:(q + 1) * OG, :, :].rearrange("p b j d -> p (b j) d"),
                             hid[:, q * OG:(q + 1) * OG, :, :].rearrange("p b j d -> p (b j) d")).then_inc(s_done, 16)
            sp.wait_ge(s_done, 16 * (B // OG))


SHAPES = {
    "ident": (P, [P]), "causal": (P, [P]), "wmask_f": (P, [2 * P]), "cos_t": (P, [NT, D]), "sin_t": (P, [NT, D // 2]),
    "nsin_t": (P, [NT, D // 2]), "iota8": (P, [NE]), "iota_row": (B, [S]), "mhalf": (P, [QK]),
    "coef": (NF, [D]), "qw0": (D, [H0 * D]), "ew0": (D, [H0 * D]), "gam": (D, [1]), "bet": (D, [1]),
    "wr0": (D, [NE]), "br0": (P, [NE]), "w1e": (D, [NE, HID]), "b1e": (P, [NE]), "w2e": (P, [NE, D]),
    "b2p": (NT * NE, [NT, D]), "wq1": (D, [NQ * D]), "wkv": (D, [2 * D]), "wo1": (P, [NP, D]), "qnw": (P, [1]),
    "knw": (P, [1]), "wrf": (D, [1]), "brf": (P, [1]), "w1f": (D, [FF]), "b1f": (P, [FC]), "w2f": (P, [FC, D]),
    "b2f": (P, [D]),
}


def tower(nc, a, ids, turns, out):
    with ExitStack() as ctx:
        def sb(name, shape, dt=F32):
            return ctx.enter_context(nc.sbuf_tensor(name, shape, dt))

        def sem(name):
            return ctx.enter_context(nc.semaphore(name))

        w = {}
        for name, (parts, free) in SHAPES.items():
            w[name] = sb("c_" + name, [parts] + free)
        w["identb"] = sb("identb", [P, P], BF16)
        w["nidentb"] = sb("nidentb", [P, P], BF16)
        w["wmask"] = sb("wmask", [P, 2 * P], BF16)
        w["qscale"] = sb("qscale", [P, 1])
        hid = sb("hid", [P, B, NT, D])
        zw = sb("zw", [P, B, NT, D])
        wall = sb("wall", [B, S])
        w_dram = nc.dram_tensor("router_weights", (B, S), F32).ap()
        psum = ctx.enter_context(nc.psum_tensor("psum", [P, 8 * BANK], F32))

        s_load = sem("s_load")
        with nc.Block() as block:
            @block.sync
            def _(sp):
                for name in SHAPES:
                    parts, free = SHAPES[name]
                    dst = w[name]
                    dst = dst[:, :] if len(free) == 1 else dst[:, :, :]
                    sp.dma_start(dst, a[name]).then_inc(s_load, 16)

            @block.vector
            def _(dve):
                dve.wait_ge(s_load, 16 * len(SHAPES))
                dve.tensor_copy(w["identb"][:, :], w["ident"][:, :])
                dve.tensor_scalar(w["nidentb"][:, :], w["ident"][:, :], -1.0, None, ALU.mult)
                dve.tensor_copy(w["wmask"][:, :], w["wmask_f"][:, :])
                dve.tensor_scalar(w["qscale"][:, :], w["qnw"][:, :], float(D) ** -0.5, None, ALU.mult)

        embed_attend_experts(nc, w, ids, turns, hid, psum)
        windowed_attention(nc, w, hid, psum)
        feed_forward(nc, w, hid, zw, wall, w_dram, psum)
        select_and_store(nc, w, hid, zw, wall, psum, out)


def layouts(x):
    f = {k: np.asarray(v) for k, v in x.items()}
    t = np.arange(S, dtype=np.float32)[:, None]
    freq = np.float32(10000.0) ** (-2.0 * np.arange(D // 2, dtype=np.float32) / D)
    theta = (t * freq[None, :].astype(np.float32)).astype(np.float32)
    cos = np.cos(theta).astype(np.float32).reshape(NT, P, D // 2).transpose(1, 0, 2)
    sin = np.sin(theta).astype(np.float32).reshape(NT, P, D // 2).transpose(1, 0, 2)
    q, k = np.arange(P)[:, None], np.arange(2 * P)[None, :] - P
    b2p = np.zeros((NT, NE, NT, D), np.float32)
    for j in range(NT):
        b2p[j, :, j, :] = f["L0_ffn_b2"]
    arrays = {
        "ident": np.eye(P, dtype=np.float32),
        "causal": np.triu(np.ones((P, P), np.float32)),
        "wmask_f": np.where((k <= q) & (q - k <= P), 0.0, NEG).astype(np.float32),
        "cos_t": np.repeat(cos, 2, axis=2), "sin_t": sin, "nsin_t": -sin,
        "iota8": np.tile(np.arange(NE, dtype=np.float32), (P, 1)),
        "iota_row": np.tile(np.arange(S, dtype=np.float32), (B, 1)),
        "mhalf": np.full((P, QK), -0.5, np.float32),
        "coef": f["L0_tok_poly_coeffs"].reshape(NF, D),
        "qw0": f["L0_attn_Q"].transpose(1, 0, 2).reshape(D, H0 * D),
        "ew0": f["L0_attn_E"].transpose(2, 0, 1).reshape(D, H0 * D),
        "gam": f["L0_ffn_gamma"].reshape(D, 1), "bet": f["L0_ffn_beta"].reshape(D, 1),
        "wr0": f["L0_ffn_Wr"], "br0": np.tile(f["L0_ffn_br"], (P, 1)),
        "w1e": f["L0_ffn_W1"].transpose(1, 0, 2), "b1e": f["L0_ffn_b1"].T,
        "w2e": f["L0_ffn_W2"].transpose(1, 0, 2), "b2p": b2p.reshape(NT * NE, NT, D),
        "wq1": f["L1_attn_wq"].T, "wkv": f["L1_attn_wkv"].T,
        "wo1": f["L1_attn_wo"].T.reshape(NP, P, D).transpose(1, 0, 2),
        "qnw": np.tile(f["L1_attn_q_norm_w"], 2).reshape(P, 1),
        "knw": np.tile(f["L1_attn_k_norm_w"], 2).reshape(P, 1),
        "wrf": f["L1_ffn_wr"], "brf": np.tile(f["L1_ffn_br"], (P, 1)),
        "w1f": f["L1_ffn_w1"], "b1f": f["L1_ffn_b1"].reshape(FC, P).T,
        "w2f": f["L1_ffn_w2"].reshape(FC, P, D).transpose(1, 0, 2), "b2f": np.tile(f["L1_ffn_b2"], (P, 1)),
    }
    arrays = {k: np.ascontiguousarray(v) for k, v in arrays.items()}
    ids = np.ascontiguousarray(f["x"].reshape(B * NT, P).T)
    return arrays, ids, np.ascontiguousarray(f["L0_tok_turns"])


def kernel(**inputs):
    import concourse.bacc as bacc
    from concourse.bass_utils import run_bass_kernel_spmd

    arrays, ids, turns = layouts(inputs)
    nc = bacc.Bacc("TRN2", target_bir_lowering=False, num_devices=1)
    feeds, a = {}, {}
    for name, v in arrays.items():
        feeds["in_" + name] = v
        a[name] = nc.dram_tensor("in_" + name, v.shape, F32, kind="ExternalInput").ap()
    feeds["in_ids"], feeds["in_turns"] = ids, turns
    ids_d = nc.dram_tensor("in_ids", ids.shape, mybir.dt.from_np(ids.dtype), kind="ExternalInput").ap()
    turns_d = nc.dram_tensor("in_turns", turns.shape, F32, kind="ExternalInput").ap()
    out = nc.dram_tensor("out", (B, S, D), F32, kind="ExternalOutput").ap()
    tower(nc, a, ids_d, turns_d, out)
    r = run_bass_kernel_spmd(nc, [feeds], core_ids=[0])
    return r.results[0]["out"]
```

```python
from contextlib import ExitStack

import numpy as np

import concourse.bass as bass
from concourse import mybir

F32 = mybir.dt.float32
BF16 = mybir.dt.bfloat16
F16 = mybir.dt.float16
I32 = mybir.dt.int32
U32 = mybir.dt.uint32
ALU = mybir.AluOpType
ACT = mybir.ActivationFunctionType
AX = mybir.AxisListType.X

P = 128
B, S, D = 32, 512, 64
NT = S // P
TURNS, DEG = 4, 5
NF = TURNS * DEG
H0 = 8
HP0 = H0 // 2
NE, HID = 8, 128
NQ = 16
NP = NQ // 2
FF = 256
FC = FF // P
KEEP = 255
EPS = 1e-5
RMS_EPS = 1.1920929e-07
NEG = -1e30
TAKEN = -3.0e38
QK = NQ + 1
VC = D + 1
BANK = 512


def wait(eng, sem, value):
    if isinstance(value, int) and value <= 0:
        return
    eng.wait_ge(sem, value)


def apart(eng, passed):
    eng.sem_inc(passed, 1)


def each(ap, n):
    return ap.unsqueeze(2).broadcast_to([ap.shape[0], ap.shape[1], n])


def flat(ap):
    return ap.rearrange("p a b -> p (a b)")


def row(hid, b):
    return hid[:, bass.ds(b, 1), :, :].rearrange("p o a b -> p (o a) b")


LN_STEPS = 4


def layernorm_dve(eng, b, src, cent, sq, st, dst, step, var_ready, rstd_ready, ready):
    base = LN_STEPS * b
    eng.tensor_reduce(st[:, 0, :], src, AX, ALU.add).then_inc(step, 1)
    eng.wait_ge(step, base + 1)
    eng.tensor_scalar(st[:, 1, :], st[:, 0, :], 1.0 / D, None, ALU.mult).then_inc(step, 1)
    eng.wait_ge(step, base + 2)
    eng.tensor_tensor(cent, src, each(st[:, 1, :], D), ALU.subtract).then_inc(step, 1)
    eng.wait_ge(step, base + 3)
    eng.tensor_tensor(sq, cent, cent, ALU.mult).then_inc(step, 1)
    eng.wait_ge(step, base + 4)
    eng.tensor_reduce(st[:, 2, :], sq, AX, ALU.add).then_inc(var_ready, 1)
    eng.wait_ge(rstd_ready, b + 1)
    for d in dst:
        last = eng.tensor_tensor(d, cent, each(st[:, 3, :], D), ALU.mult)
    last.then_inc(ready, 1)


def rstd_pool(eng, n, out, ssum, tmp, mhalf, width, eps, sum_ready, tmp_ready, ready, passed):
    eng.wait_ge(sum_ready, n + 1)
    apart(eng, passed)
    eng.tensor_scalar(tmp, ssum, 1.0 / width, eps, ALU.mult, ALU.add).then_inc(tmp_ready, 1)
    eng.wait_ge(tmp_ready, n + 1)
    eng.tensor_tensor(out, tmp, mhalf, ALU.pow).then_inc(ready, 1)


def batches(eng, body, first=0, last=B):
    body(first)
    with eng.Fori(first + 1, last, 1) as b:
        body(b)


def embed_attend_experts(nc, w, ids, turns, hid, psum):
    with ExitStack() as ctx:
        def sb(name, shape, dt=F32):
            return ctx.enter_context(nc.sbuf_tensor(name, shape, dt))

        def sem(name):
            return ctx.enter_context(nc.semaphore(name))

        def bank(n, lo, hi, parts=P):
            return psum[0:parts, n * BANK + lo:n * BANK + hi]

        idx = sb("idx", [P, NT], I32)
        gath = sb("gath", [P, NT * TURNS])
        tk = sb("tk", [P, 6, NT * TURNS])
        tki = sb("tki", [P, NT * TURNS], I32)
        xp = sb("xp", [P, NT, TURNS, DEG])
        xpT = sb("xpT", [NF, S])
        h0 = sb("h0", [P, NT, D])
        lnc = sb("lnc", [P, NT, D])
        lnq = sb("lnq", [P, NT, D])
        lns = sb("lns", [P, 5, NT])
        r2 = sb("r2", [P, NT, 2, D])
        rT = sb("rT", [P, S])
        AT = sb("AT", [P, HP0, S])
        V0 = sb("V0", [P, 2, H0 * D])
        Om = sb("Om", [P, 2, H0, P])
        Gs = sb("Gs", [D, D])
        GEs = sb("GEs", [P, HP0, D])
        h1 = sb("h1", [P, NT, D])
        zc = sb("zc", [P, NT, D])
        zq = sb("zq", [P, NT, D])
        zs = sb("zs", [P, 6, NT])
        z = sb("z", [P, NT, D])
        xnT = sb("xnT", [D, S])
        lg = sb("lg", [P, NT, NE])
        top = sb("top", [P, NT, 8])
        topi = sb("topi", [P, NT, 8], U32)
        topf = sb("topf", [P, NT, 8])
        gd = sb("gd", [P, 4, NT])
        gw = sb("gw", [P, 4, NT, NE])
        wfull = sb("wfull", [P, NT, NE])
        wT = sb("wT", [NT * NE, P])
        g = sb("g", [P, 2, S])
        ytmp = sb("ytmp", [P, 2, NT, D])
        acc = sb("acc", [P, NT, D])

        s_ids = sem("s_ids")
        s_gath = sem("s_gath")
        s_tk = sem("s_tk")
        s_xp = sem("s_xp")
        s_xpT = sem("s_xpT")
        s_xpTs = sem("s_xpTs")
        s_h0 = sem("s_h0")
        s_h0s = sem("s_h0s")
        s_ln = sem("s_ln")
        s_var = sem("s_var")
        s_vt = sem("s_vt")
        s_rstd = sem("s_rstd")
        s_r = sem("s_r")
        s_rT = sem("s_rT")
        s_rTs = sem("s_rTs")
        s_A = sem("s_A")
        s_As = sem("s_As")
        s_V = sem("s_V")
        s_Vs = sem("s_Vs")
        s_Om = sem("s_Om")
        s_Oms = sem("s_Oms")
        s_G = sem("s_G")
        s_Gs = sem("s_Gs")
        s_GE = sem("s_GE")
        s_GEs = sem("s_GEs")
        s_att = sem("s_att")
        s_h1 = sem("s_h1")
        s_zln = sem("s_zln")
        s_zvar = sem("s_zvar")
        s_zvt = sem("s_zvt")
        s_zrstd = sem("s_zrstd")
        s_z = sem("s_z")
        s_zT = sem("s_zT")
        s_xn = sem("s_xn")
        s_lg = sem("s_lg")
        s_gate = sem("s_gate")
        s_gd = sem("s_gd")
        s_th = sem("s_th")
        s_w = sem("s_w")
        s_wT = sem("s_wT")
        s_wTs = sem("s_wTs")
        s_b2 = sem("s_b2")
        s_acc0 = sem("s_acc0")
        s_hT = sem("s_hT")
        s_g = sem("s_g")
        s_y = sem("s_y")
        s_yt = sem("s_yt")
        s_acc = sem("s_acc")

        GATE_STEPS = 5 + 2 * NT
        TK_STEPS = 9

        passed_pool, passed_pe, passed_dve = (sem(f"s1_passed_{e}") for e in ("pool", "pe", "dve"))

        block = ctx.enter_context(nc.Block())

        @block.sync
        def _(sp):
            def load(b):
                wait(sp, s_gath, 64 * b)
                sp.dma_start(idx[:, :], ids[:, bass.ds(b * NT, NT)]).then_inc(s_ids, 16)
            batches(sp, load)

        @block.gpsimd
        def _(pool):
            def gather(b):
                pool.wait_ge(s_ids, 16 * b + 16)
                wait(pool, s_xp, b)
                apart(pool, passed_pool)
                for j in range(NT):
                    pool.indirect_dma_start(gath[:, j * TURNS:(j + 1) * TURNS], None, turns,
                                            bass.IndirectOffsetOnAxis(ap=idx[:, j:j + 1], axis=0)
                                            ).then_inc(s_gath, 16)

            def attend_norm(b):
                rstd_pool(pool, b, lns[:, 3, :], lns[:, 2, :], lns[:, 4, :], w["mhalf"][:, 0:NT], D, EPS,
                          s_var, s_vt, s_rstd, passed_pool)

            def expert_norm(b):
                pool.wait_ge(s_zvar, b + 1)
                apart(pool, passed_pool)
                v, t, r = zs[:, 2, :], zs[:, 4, :], zs[:, 5, :]
                pool.tensor_scalar(t, v, 1.0 / D, EPS, ALU.mult, ALU.add).then_inc(s_zvt, 1)
                pool.wait_ge(s_zvt, 6 * b + 1)
                pool.tensor_tensor(r, t, w["mhalf"][:, 0:NT], ALU.pow).then_inc(s_zvt, 1)
                pool.wait_ge(s_zvt, 6 * b + 2)
                pool.tensor_tensor(t, r, r, ALU.mult).then_inc(s_zvt, 1)
                pool.wait_ge(s_zvt, 6 * b + 3)
                pool.tensor_tensor(t, t, v, ALU.mult).then_inc(s_zvt, 1)
                pool.wait_ge(s_zvt, 6 * b + 4)
                apart(pool, passed_pool)
                pool.tensor_scalar(t, t, 1.0 / D, EPS, ALU.mult, ALU.add).then_inc(s_zvt, 1)
                pool.wait_ge(s_zvt, 6 * b + 5)
                pool.tensor_tensor(t, t, w["mhalf"][:, 0:NT], ALU.pow).then_inc(s_zvt, 1)
                pool.wait_ge(s_zvt, 6 * b + 6)
                pool.tensor_tensor(zs[:, 3, :], t, r, ALU.mult).then_inc(s_zrstd, 1)

            gather(0)
            attend_norm(0)
            def both(b):
                gather(b)
                expert_norm(b - 1)
                attend_norm(b)

            both(1)
            with pool.Fori(2, B, 1) as b:
                both(b)
            expert_norm(B - 1)

        @block.tensor
        def _(pe):
            def mm(out, lhsT, rhs, start=True, stop=True):
                return pe.matmul(out, lhsT, rhs, start=start, stop=stop)

            def embed(b):
                wait(pe, s_h1, NT * b)
                pe.wait_ge(s_xp, b + 1)
                for j in range(NT):
                    last = pe.transpose(bank(0, j * P, j * P + P, NF), xp[:, j, :, :].rearrange("p a b -> p (a b)"),
                                        w["ident"][:, :])
                last.then_inc(s_xpT, 1)
                wait(pe, s_Vs, NT * b)
                pe.wait_ge(s_xpTs, b + 1)
                for j in range(NT):
                    last = mm(bank(1, j * D, j * D + D), xpT[:, j * P:(j + 1) * P], w["coef"][:, :])
                last.then_inc(s_h0, 1)

            def project(b):
                pe.wait_ge(s_r, b + 1)
                for j in range(NT):
                    last = pe.transpose(bank(0, j * P, j * P + P), r2[:, j, :, :].rearrange("p a b -> p (a b)"),
                                        w["ident"][:, :])
                last.then_inc(s_rT, 1)
                pe.wait_ge(s_rTs, b + 1)
                for p in range(HP0):
                    if p == 1:
                        wait(pe, s_Oms, NT * b)
                    if p >= 2:
                        pe.wait_ge(s_As, HP0 * b + p - 1)
                    mm(bank(1 + p % 2, 0, S), w["qw0"][:, p * P:(p + 1) * P], rT[0:D, :]).then_inc(s_A, 1)

            def attend(b, j):
                t = slice(j * P, (j + 1) * P)
                if j == 0:
                    pe.wait_ge(s_As, HP0 * b + HP0)
                else:
                    pe.wait_ge(s_Vs, NT * b + j)
                    pe.wait_ge(s_Oms, NT * b + j)
                mm(bank(1, 0, H0 * D), rT[0:D, t], w["ew0"][0:D, :]).then_inc(s_V, 1)
                if j == 0:
                    wait(pe, s_Oms, NT * b)
                for h in range(H0):
                    c = slice((h % 2) * D, (h % 2) * D + D)
                    o = (2 + h % 2) * BANK + h // 2 * P
                    last = mm(psum[:, o:o + P], rT[c, t], AT[c, h // 2, t])
                last.then_inc(s_Om, 1)
                if j >= 1:
                    r = r2[:, j - 1, 0, :]
                    pe.wait_ge(s_h1, NT * b + j)
                    apart(pe, passed_pe)
                    mm(bank(0, 0, D, D), r, r).then_inc(s_G, 1)
                    pe.wait_ge(s_Gs, 3 * b + j)
                    apart(pe, passed_pe)
                    for half in range(2):
                        o = half * D
                        last = mm(psum[o:o + D, D:D + HP0 * D], Gs[:, :],
                                  w["ew0"][:, :].rearrange("p (c two d) -> p c two d", two=2, d=D)[:, :, half, :])
                    last.then_inc(s_GE, 1)
                pe.wait_ge(s_Vs, NT * b + j + 1)
                pe.wait_ge(s_Oms, NT * b + j + 1)
                if j >= 1:
                    pe.wait_ge(s_GEs, 3 * b + j)
                dst = bank(0, 5 * D, 6 * D)
                for h in range(H0):
                    last = mm(dst, Om[:, j % 2, (h % 2) * HP0 + h // 2, :], V0[:, j % 2, h * D:(h + 1) * D], h == 0,
                              j == 0 and h == H0 - 1)
                if j >= 1:
                    for p in range(HP0):
                        last = mm(dst, AT[:, p, t], GEs[:, p, :], False, p == HP0 - 1)
                last.then_inc(s_att, 1)

            def expert_input(b):
                pe.wait_ge(s_z, b + 1)
                wait(pe, s_acc0, b)
                apart(pe, passed_pe)
                for j in range(NT):
                    last = pe.transpose(bank(4, j * P, j * P + P, D), z[:, j, :], w["ident"][:, :])
                last.then_inc(s_zT, 1)

            def gate_logits(b):
                pe.wait_ge(s_xn, b + 1)
                for j in range(NT):
                    last = mm(bank(4, j * NE, j * NE + NE), xnT[:, j * P:(j + 1) * P], w["wr0"][:, :])
                last.then_inc(s_lg, 1)

            def gate_bias(b):
                pe.wait_ge(s_w, b + 1)
                pe.transpose(bank(4, P, 2 * P, NT * NE), wfull[:, :, :].rearrange("p a b -> p (a b)"),
                             w["ident"][:, :]).then_inc(s_wT, 1)
                pe.wait_ge(s_wTs, b + 1)
                for j in range(NT):
                    last = mm(bank(4, 2 * P + j * D, 2 * P + j * D + D), wT[:, :], w["b2p"][:, j, :])
                last.then_inc(s_b2, 1)

            def expert_hidden(b, e):
                wait(pe, s_g, NE * b + e - 1)
                mm(bank(5 + e % 2, 0, S), w["w1e"][:, e, :], xnT[:, :]).then_inc(s_hT, 1)

            def expert_out(b, e):
                pe.wait_ge(s_g, NE * b + e + 1)
                wait(pe, s_yt, NE * b + e)
                for j in range(NT):
                    last = mm(bank(7, j * D, j * D + D), g[:, e % 2, j * P:(j + 1) * P], w["w2e"][:, e, :])
                last.then_inc(s_y, 1)

            def experts(b, j):
                for e in (2 * j, 2 * j + 1):
                    expert_out(b, e)
                    if e + 2 < NE:
                        expert_hidden(b, e + 2)

            embed(0)
            project(0)
            for j in range(NT):
                attend(0, j)
            def both(b):
                expert_input(b - 1)
                embed(b)
                gate_logits(b - 1)
                project(b)
                expert_hidden(b - 1, 0)
                expert_hidden(b - 1, 1)
                gate_bias(b - 1)
                for j in range(NT):
                    attend(b, j)
                    experts(b - 1, j)

            both(1)
            with pe.Fori(2, B, 1) as b:
                both(b)
            expert_input(B - 1)
            gate_logits(B - 1)
            gate_bias(B - 1)
            expert_hidden(B - 1, 0)
            expert_hidden(B - 1, 1)
            for j in range(NT):
                experts(B - 1, j)

        @block.scalar
        def _(act):
            def embed(b):
                act.wait_ge(s_xpT, b + 1)
                act.copy(xpT[:, :], bank(0, 0, S, NF)).then_inc(s_xpTs, 1)

            def project(b):
                act.wait_ge(s_rT, b + 1)
                act.copy(rT[:, :], bank(0, 0, S)).then_inc(s_rTs, 1)
                for p in range(HP0):
                    act.wait_ge(s_A, HP0 * b + p + 1)
                    act.copy(AT[:, p, :], bank(1 + p % 2, 0, S)).then_inc(s_As, 1)

            def attend(b, j):
                act.wait_ge(s_V, NT * b + j + 1)
                if j >= 2:
                    act.wait_ge(s_att, NT * b + j - 1)
                act.copy(V0[:, j % 2, :], bank(1, 0, H0 * D)).then_inc(s_Vs, 1)
                if j >= 1:
                    act.wait_ge(s_GE, 3 * b + j)
                    act.wait_ge(s_att, NT * b + j)
                    act.copy(GEs[:, :, :].rearrange("p a b -> p (a b)"), bank(0, D, D + HP0 * D)).then_inc(s_GEs, 1)

            def expert_input(b):
                act.wait_ge(s_zT, b + 1)
                wait(act, s_hT, NE * b)
                act.activation(xnT[:, :], bank(4, 0, S, D), ACT.Identity, bias=w["bet"][:, 0:1],
                               scale=w["gam"][:, 0:1]).then_inc(s_xn, 1)

            def gate(b):
                act.wait_ge(s_gd, b + 1)
                act.activation(gd[:, 1, :], gd[:, 0, :], ACT.Tanh, scale=0.5).then_inc(s_th, 1)

            def gate_bias(b):
                act.wait_ge(s_wT, b + 1)
                act.copy(wT[:, :], bank(4, P, 2 * P, NT * NE)).then_inc(s_wTs, 1)

            def gelu(b, e):
                act.wait_ge(s_hT, NE * b + e + 1)
                wait(act, s_y, NE * b + e - 1)
                act.activation(g[:, e % 2, :], bank(5 + e % 2, 0, S), ACT.Gelu,
                               bias=w["b1e"][:, e:e + 1]).then_inc(s_g, 1)

            embed(0)
            project(0)
            for j in range(NT):
                attend(0, j)
            def both(b):
                expert_input(b - 1)
                embed(b)
                gate(b - 1)
                project(b)
                gate_bias(b - 1)
                gelu(b - 1, 0)
                gelu(b - 1, 1)
                for j in range(NT):
                    attend(b, j)
                    if j + 1 < NT:
                        gelu(b - 1, 2 * j + 2)
                        gelu(b - 1, 2 * j + 3)

            both(1)
            with act.Fori(2, B, 1) as b:
                both(b)
            expert_input(B - 1)
            gate(B - 1)
            gate_bias(B - 1)
            for e in range(NE):
                gelu(B - 1, e)

        @block.vector
        def _(dve):
            def powers(b):
                base = TK_STEPS * b
                xv = xp[:, :, :, :].rearrange("p a t d -> p (a t) d")
                dve.wait_ge(s_gath, 64 * b + 64)
                wait(dve, s_xpT, b)
                dve.scalar_tensor_tensor(tk[:, 0, :], gath[:, :], -1.0, gath[:, :], ALU.mult, ALU.max).then_inc(s_tk, 1)
                dve.wait_ge(s_tk, base + 1)
                dve.tensor_copy(tki[:, :], tk[:, 0, :]).then_inc(s_tk, 1)
                dve.wait_ge(s_tk, base + 2)
                dve.tensor_copy(tk[:, 1, :], tki[:, :]).then_inc(s_tk, 1)
                dve.wait_ge(s_tk, base + 3)
                dve.tensor_tensor(tk[:, 2, :], tk[:, 1, :], tk[:, 0, :], ALU.is_gt).then_inc(s_tk, 1)
                dve.wait_ge(s_tk, base + 4)
                dve.tensor_tensor(tk[:, 3, :], tk[:, 1, :], tk[:, 2, :], ALU.subtract).then_inc(s_tk, 1)
                dve.tensor_scalar(tk[:, 4, :], gath[:, :], 0.0, 2.0, ALU.is_ge, ALU.mult).then_inc(s_tk, 1)
                dve.wait_ge(s_tk, base + 6)
                dve.scalar_tensor_tensor(xv[:, :, 1], tk[:, 4, :], -1.0, tk[:, 3, :], ALU.add, ALU.mult).then_inc(s_tk, 1)
                dve.wait_ge(s_tk, base + 7)
                dve.tensor_tensor(xv[:, :, 2], xv[:, :, 1], xv[:, :, 1], ALU.mult).then_inc(s_tk, 1)
                dve.wait_ge(s_tk, base + 8)
                dve.tensor_tensor(xv[:, :, 3], xv[:, :, 1], xv[:, :, 2], ALU.mult).then_inc(s_tk, 1)
                dve.tensor_tensor(xv[:, :, 4], xv[:, :, 2], xv[:, :, 2], ALU.mult).then_inc(s_xp, 1)

            def attend_input(b):
                dve.wait_ge(s_h0, b + 1)
                dve.tensor_copy(flat(h0[:, :, :]), bank(1, 0, NT * D)).then_inc(s_h0s, 1)
                dve.wait_ge(s_h0s, b + 1)
                wait(dve, s_att, NT * b)
                layernorm_dve(dve, b, h0[:, :, :], lnc[:, :, :], lnq[:, :, :], lns, [r2[:, :, 0, :], r2[:, :, 1, :]],
                              s_ln, s_var, s_rstd, s_r)

            def attend(b, j):
                dve.wait_ge(s_Om, NT * b + j + 1)
                if j >= 2:
                    dve.wait_ge(s_att, NT * b + j - 1)
                dve.tensor_tensor(Om[:, j % 2, :, :], psum[:, 2 * BANK:4 * BANK].rearrange("p (h t) -> p h t", t=P),
                                  w["causal"][:, :].unsqueeze(1).broadcast_to([P, H0, P]), ALU.mult).then_inc(s_Oms, 1)
                if j >= 1:
                    dve.wait_ge(s_G, 3 * b + j)
                    if j == 1:
                        dve.tensor_copy(Gs[:, :], bank(0, 0, D, D)).then_inc(s_Gs, 1)
                    else:
                        dve.wait_ge(s_GE, 3 * b + j - 1)
                        dve.tensor_tensor(Gs[:, :], Gs[:, :], bank(0, 0, D, D), ALU.add).then_inc(s_Gs, 1)

            def residual(b, j):
                dve.wait_ge(s_att, NT * b + j + 1)
                dve.tensor_tensor(h1[:, j, :], h0[:, j, :], bank(0, 5 * D, 6 * D), ALU.add).then_inc(s_h1, 1)

            def expert_input(b):
                dve.wait_ge(s_h1, NT * b + NT)
                wait(dve, s_zT, b)
                layernorm_dve(dve, b, h1[:, :, :], zc[:, :, :], zq[:, :, :], zs, [z[:, :, :]],
                              s_zln, s_zvar, s_zrstd, s_z)

            def gate(b):
                base = GATE_STEPS * b
                dve.wait_ge(s_lg, b + 1)
                dve.tensor_tensor(lg[:, :, :], bank(4, 0, NT * NE).rearrange("p (a e) -> p a e", e=NE),
                                  w["br0"][:, :].unsqueeze(1).broadcast_to([P, NT, NE]), ALU.add).then_inc(s_gate, 1)
                dve.wait_ge(s_gate, base + 1)
                apart(dve, passed_dve)
                for j in range(NT):
                    dve.max(top[:, j, :], lg[:, j, :]).then_inc(s_gate, 1)
                for j in range(NT):
                    dve.wait_ge(s_gate, base + 2 + j)
                    apart(dve, passed_dve)
                    dve.max_index(topi[:, j, :], top[:, j, :], lg[:, j, :]).then_inc(s_gate, 1)
                dve.tensor_tensor(gd[:, 0, :], top[:, :, 0], top[:, :, 1], ALU.subtract).then_inc(s_gd, 1)
                dve.wait_ge(s_gate, base + 1 + 2 * NT)
                dve.tensor_copy(topf[:, :, :], topi[:, :, :]).then_inc(s_gate, 1)
                dve.wait_ge(s_gate, base + 2 + 2 * NT)
                for k in range(2):
                    dve.tensor_tensor(gw[:, k, :, :], w["iota8"][:, :].unsqueeze(1).broadcast_to([P, NT, NE]),
                                      each(topf[:, :, k], NE), ALU.is_equal)
                dve.wait_ge(s_th, b + 1)
                dve.tensor_scalar(gd[:, 2, :], gd[:, 1, :], 0.5, 0.5, ALU.mult, ALU.add)
                dve.tensor_scalar(gd[:, 3, :], gd[:, 1, :], -0.5, 0.5, ALU.mult, ALU.add).then_inc(s_gate, 1)
                dve.wait_ge(s_gate, base + 3 + 2 * NT)
                for k in range(2):
                    dve.tensor_tensor(gw[:, 2 + k, :, :], gw[:, k, :, :], each(gd[:, 2 + k, :], NE),
                                      ALU.mult).then_inc(s_gate, 1)
                dve.wait_ge(s_gate, base + 5 + 2 * NT)
                wait(dve, s_wT, b)
                dve.tensor_tensor(wfull[:, :, :], gw[:, 2, :, :], gw[:, 3, :, :], ALU.add).then_inc(s_w, 1)

            def start_sum(b):
                dve.wait_ge(s_b2, b + 1)
                dve.tensor_tensor(flat(acc[:, :, :]), flat(h1[:, :, :]), bank(4, 2 * P, 2 * P + NT * D),
                                  ALU.add).then_inc(s_acc0, 1)

            def add_expert(b, e):
                dve.wait_ge(s_y, NE * b + e + 1)
                dve.tensor_tensor(ytmp[:, e % 2, :, :], bank(7, 0, NT * D).rearrange("p (a d) -> p a d", d=D),
                                  each(wfull[:, :, e], D), ALU.mult).then_inc(s_yt, 1)
                dve.wait_ge(s_yt, NE * b + e + 1)
                if e == 0:
                    dve.wait_ge(s_acc0, b + 1)
                else:
                    dve.wait_ge(s_acc, NE * b + e)
                dst = acc[:, :, :] if e < NE - 1 else row(hid, b)
                dve.tensor_tensor(dst, acc[:, :, :], ytmp[:, e % 2, :, :], ALU.add).then_inc(s_acc, 1)

            dve.memset(xp[:, :, :, 0:1], 1.0)
            powers(0)
            attend_input(0)
            for j in range(NT):
                attend(0, j)
                residual(0, j)
            def both(b):
                expert_input(b - 1)
                powers(b)
                gate(b - 1)
                attend_input(b)
                start_sum(b - 1)
                for j in range(NT):
                    attend(b, j)
                    add_expert(b - 1, 2 * j)
                    residual(b, j)
                    add_expert(b - 1, 2 * j + 1)

            both(1)
            with dve.Fori(2, B, 1) as b:
                both(b)
            expert_input(B - 1)
            gate(B - 1)
            start_sum(B - 1)
            for e in range(NE):
                add_expert(B - 1, e)


def windowed_attention(nc, w, hid, psum):
    with ExitStack() as ctx:
        def sb(name, shape, dt=F32):
            return ctx.enter_context(nc.sbuf_tensor(name, shape, dt))

        def sem(name):
            return ctx.enter_context(nc.semaphore(name))

        NPROB = 4
        lnc = sb("lnc2", [P, NT, D])
        lnq = sb("lnq2", [P, NT, D])
        lns = sb("lns2", [P, 5, NT])
        x2 = sb("x2", [P, NT, D])
        xs = sb("xs", [P, NT, 2, D], F16)
        xsT = sb("xsT", [P, S], F16)
        sq = sb("sq", [P, QK, D])
        ss = sb("ss", [P, 3, QK])
        ra = sb("ra", [P, QK, D])
        rb = sb("rb", [P, QK, D])
        rc = sb("rc", [P, QK, D])
        qn = sb("qn", [P, QK, D])
        qs = sb("qs", [P, NQ + 2, 2, D], F16)
        qT = sb("qT", [P, 2, NQ * P], F16)
        kT = sb("kT", [P, 2, S], F16)
        vv = sb("vv", [P, NT, VC])
        mb = sb("mb", [P, 2, NQ], BF16)
        prob = sb("prob", [P, NPROB, 2, 2, P])
        rcp = sb("rcp", [P, 2, 2])
        o = sb("o", [P, 2, NQ, D])
        oT = sb("oT", [P, NP, P])

        s_ln = sem("s2_ln")
        s_var = sem("s2_var")
        s_vt = sem("s2_vt")
        s_rstd = sem("s2_rstd")
        s_x = sem("s2_x")
        s_xh = sem("s2_xh")
        s_xl = sem("s2_xl")
        s_xT = sem("s2_xT")
        s_xTs = sem("s2_xTs")
        s_qkv = sem("s2_qkv")
        s_sq = sem("s2_sq")
        s_ssum = sem("s2_ssum")
        s_sst = sem("s2_sst")
        s_rms = sem("s2_rms")
        s_rab = sem("s2_rab")
        s_rot = sem("s2_rot")
        s_qn = sem("s2_qn")
        s_qh = sem("s2_qh")
        s_qs = sem("s2_qs")
        s_qkT = sem("s2_qkT")
        s_qTs = sem("s2_qTs")
        s_S1 = sem("s2_S1")
        s_m = sem("s2_m")
        s_ST = sem("s2_ST")
        s_e = sem("s2_e")
        s_p = sem("s2_p")
        s_pv = sem("s2_pv")
        s_rcp = sem("s2_rcp")
        s_o = sem("s2_o")
        s_oT = sem("s2_oT")
        s_oTs = sem("s2_oTs")
        s_y = sem("s2_y")
        s_h = sem("s2_h")

        passed_pool, passed_pe = (sem(f"s2_passed_{e}") for e in ("pool", "pe"))

        proj = psum[:, 0:3 * BANK]
        qk_ps = proj[:, 0:QK * D].rearrange("p (h d) -> p h d", d=D)
        v_ps = proj[:, QK * D:(QK + 1) * D]
        qT_ps = psum[:, 0:2 * BANK].bitcast(F16)
        kT_ps = psum[:, 2 * BANK:2 * BANK + P].bitcast(F16)
        y_ps = proj[:, 1280:1280 + D]

        def blocks(j):
            return 2 if j > 0 else 1

        def after(b, j, n):
            if isinstance(b, int) and NT * b + j + n >= NT * B:
                return None
            return (b + (j + n) // NT, (j + n) % NT)

        def tiles(eng, step):
            for j in range(NT):
                step(0, j)
            with eng.Fori(1, B - 1, 1) as b:
                for j in range(NT):
                    step(b, j)
            for j in range(NT):
                step(B - 1, j)

        block = ctx.enter_context(nc.Block())

        @block.gpsimd
        def _(pool):
            def norm(b):
                rstd_pool(pool, b, lns[:, 3, :], lns[:, 2, :], lns[:, 4, :], w["mhalf"][:, 0:NT], D, EPS,
                          s_var, s_vt, s_rstd, passed_pool)

            def add_rotation(b, j):
                n = NT * b + j
                pool.wait_ge(s_rab, n + 1)
                wait(pool, s_qn, n)
                pool.tensor_tensor(rc[:, :, :], ra[:, :, :], rb[:, :, :], ALU.add).then_inc(s_rot, 1)

            def rms(b, j):
                rstd_pool(pool, NT * b + j, ss[:, 2, :], ss[:, 0, :], ss[:, 1, :], w["mhalf"][:, :], D, RMS_EPS,
                          s_ssum, s_sst, s_rms, passed_pool)

            def window(b, j, i):
                pool.wait_ge(s_e, NP * (NT * b + j) + i + 1)
                apart(pool, passed_pool)
                p = prob[:, i % NPROB, :, :, :]
                last = pool.affine_select(out=p[:, :, 0, :], in_=p[:, :, 0, :], compare_op=ALU.is_ge, fill=0.0, base=0,
                                          pattern=[[0, 2], [1, P]], channel_multiplier=-1)
                if blocks(j) == 2:
                    last = pool.affine_select(out=p[:, :, 1, :], in_=p[:, :, 1, :], compare_op=ALU.is_ge, fill=0.0,
                                              base=0, pattern=[[0, 2], [-1, P]], channel_multiplier=1)
                last.then_inc(s_p, 1)

            def step(b, j):
                nxt, ahead = after(b, j, 1), after(b, j, 2)
                for i in range(NP):
                    window(b, j, i)
                    if i == 0 and nxt is not None:
                        rms(*nxt)
                    if i == 6 and j == 1 and ahead is not None and after(b, j, 3) is not None:
                        norm(after(b, j, 3)[0])
                    if i == 7 and ahead is not None:
                        add_rotation(*ahead)

            norm(0)
            add_rotation(0, 0)
            rms(0, 0)
            add_rotation(0, 1)
            tiles(pool, step)

        @block.tensor
        def _(pe):
            def mm(out, lhsT, rhs, start=True, stop=True):
                return pe.matmul(out, lhsT, rhs, start=start, stop=stop, skip_group_check=True)

            def transpose_x(b):
                pe.wait_ge(s_xl, b + 1)
                wait(pe, s_qTs, NT * b)
                apart(pe, passed_pe)
                for j in range(NT):
                    last = pe.transpose(psum[:, j * P // 2:(j + 1) * P // 2].bitcast(F16),
                                        xs[:, j, :, :].rearrange("p a b -> p (a b)"), w["identh"][:, :])
                last.then_inc(s_xT, 1)

            def project(b, j):
                n = NT * b + j
                pe.wait_ge(s_xTs, b + 1)
                wait(pe, s_qTs, n)
                t = xsT[:, j * P:(j + 1) * P]
                for c in range(2):
                    mm(proj[:, c * BANK:(c + 1) * BANK], t, w["wqh"][:, c * BANK:(c + 1) * BANK], True, False)
                    mm(proj[:, c * BANK:(c + 1) * BANK], t, w["wql"][:, c * BANK:(c + 1) * BANK], False, True)
                mm(proj[:, 2 * BANK:2 * BANK + 2 * D], t, w["wkvh"][:, :], True, False)
                mm(proj[:, 2 * BANK:2 * BANK + 2 * D], t, w["wkvl"][:, :], False, True).then_inc(s_qkv, 1)

            def transpose_qk(b, j):
                n = NT * b + j
                pe.wait_ge(s_qs, n + 1)
                wait(pe, s_oTs, 2 * n - 2)
                wait(pe, s_h, n - 1)
                for h in range(NQ):
                    pe.transpose(qT_ps[:, h * P:(h + 1) * P], flat(qs[:, h, :, :]), w["identh"][:, :])
                for k in range(2):
                    last = pe.transpose(kT_ps[:, k * P:(k + 1) * P], flat(qs[:, NQ + k, :, :]), w["identh"][:, :])
                last.then_inc(s_qkT, 1)

            def scores(b, j, i):
                n = NP * (NT * b + j) + i
                if i == 0:
                    pe.wait_ge(s_qTs, NT * b + j + 1)
                wait(pe, s_m, n - 1)
                keys = P * blocks(j)
                dst = psum[:, (3 + i % 2) * BANK:(3 + i % 2) * BANK + 2 * keys].rearrange("p (h k) -> p h k", h=2)
                mm(dst, w["identb"][:, :],
                   w["wmask"][:, 2 * P - keys:2 * P].unsqueeze(1).broadcast_to([P, 2, keys]), True, False)
                for hh in range(2):
                    h = 2 * i + hh
                    last = mm(dst[:, hh, :], qT[:, j % 2, h * P:(h + 1) * P], kT[:, 0, (j + 1) * P - keys:(j + 1) * P],
                              False, True)
                last.then_inc(s_S1, 1)

            def shifted(b, j, i):
                n = NP * (NT * b + j) + i
                pe.wait_ge(s_m, n + 1)
                wait(pe, s_e, n - 1)
                for hh in range(2):
                    h = 2 * i + hh
                    lo = (5 + i % 2) * BANK + hh * 2 * P
                    nb = blocks(j)
                    mm(psum[:, lo:lo + nb * P].rearrange("p (k t) -> p k t", t=P),
                       mb[:, j % 2, h:h + 1].broadcast_to([P, P]),
                       w["nidentb"][:, :].unsqueeze(1).broadcast_to([P, nb, P]), True, False)
                    for k in range(nb):
                        dst = psum[:, lo + k * P:lo + (k + 1) * P]
                        for part in range(2):
                            last = mm(dst, kT[:, part, (j - k) * P:(j - k + 1) * P], qT[:, j % 2, h * P:(h + 1) * P],
                                      False, part == 1)
                last.then_inc(s_ST, 1)

            def weigh(b, j, i):
                n = NP * (NT * b + j) + i
                pe.wait_ge(s_p, n + 1)
                wait(pe, s_o, n)
                for hh in range(2):
                    lo = 7 * BANK + hh * VC
                    for k in range(blocks(j)):
                        last = mm(psum[:, lo:lo + VC], prob[:, i % NPROB, hh, k, :], vv[:, j - k, :], k == 0,
                                  k == blocks(j) - 1)
                last.then_inc(s_pv, 1)

            def transpose_out(b, j):
                n = NT * b + j
                pe.wait_ge(s_o, NP * (n + 1))
                wait(pe, s_rab, n + 3 if after(b, j, 2) is not None else 0)
                for c in range(2):
                    for i in range(NP // 2):
                        h = 2 * (c * NP // 2 + i)
                        last = pe.transpose(proj[:, c * BANK + i * P:c * BANK + (i + 1) * P],
                                            flat(o[:, j % 2, h:h + 2, :]), w["ident"][:, :])
                    last.then_inc(s_oT, 1)

            def output(b, j):
                n = NT * b + j
                for c in range(2):
                    pe.wait_ge(s_oTs, 2 * n + c + 1)
                    for i in range(c * NP // 2, (c + 1) * NP // 2):
                        last = mm(y_ps, oT[:, i, :], w["wo1"][:, i, :], i == 0, i == NP - 1)
                last.then_inc(s_y, 1)

            def step(b, j):
                first = isinstance(b, int) and b == 0 and j == 0
                nxt, ahead = after(b, j, 1), after(b, j, 2)
                prev = (b - 1, NT - 1) if j == 0 else (b, j - 1)
                for i in range(NP):
                    if i + 2 < NP:
                        scores(b, j, i + 2)
                    elif nxt is not None:
                        scores(*nxt, i + 2 - NP)
                    shifted(b, j, i)
                    if i >= 2:
                        weigh(b, j, i - 2)
                    elif not first:
                        weigh(*prev, i + NP - 2)
                    if i == 2 and not first:
                        transpose_out(*prev)
                    if i == 3 and not first:
                        output(*prev)
                    if i == 4 and nxt is not None:
                        transpose_qk(*nxt)
                    if i == 5 and ahead is not None:
                        if ahead[1] == 0:
                            transpose_x(ahead[0])
                        project(*ahead)

            transpose_x(0)
            project(0, 0)
            transpose_qk(0, 0)
            project(0, 1)
            scores(0, 0, 0)
            scores(0, 0, 1)
            tiles(pe, step)
            weigh(B - 1, NT - 1, NP - 2)
            weigh(B - 1, NT - 1, NP - 1)
            transpose_out(B - 1, NT - 1)
            output(B - 1, NT - 1)

        @block.scalar
        def _(act):
            def copy_xT(b):
                act.wait_ge(s_xT, b + 1)
                wait(act, s_qkv, NT * b)
                act.copy(xsT[:, :], psum[:, 0:S // 2].bitcast(F16)).then_inc(s_xTs, 1)

            def squares(b, j):
                n = NT * b + j
                act.wait_ge(s_qkv, n + 1)
                wait(act, s_ssum, n)
                wait(act, s_pv, NP * (n - 2))
                act.activation(sq[:, :, :], qk_ps, ACT.Square)
                act.copy(vv[:, j, 0:D], v_ps).then_inc(s_sq, 1)

            def copy_qk(b, j):
                n = NT * b + j
                act.wait_ge(s_qkT, n + 1)
                wait(act, s_ST, NP * (n - 1))
                act.copy(qT[:, j % 2, :], qT_ps)
                act.copy(kT[:, :, j * P:(j + 1) * P], kT_ps.rearrange("p (k t) -> p k t", t=P)).then_inc(s_qTs, 1)

            def exps(b, j, i):
                n = NP * (NT * b + j) + i
                act.wait_ge(s_ST, n + 1)
                wait(act, s_pv, n - NPROB + 1)
                src = psum[:, (5 + i % 2) * BANK:(6 + i % 2) * BANK].rearrange("p (h k t) -> p h k t", h=2, t=P)
                act.activation(prob[:, i % NPROB, :, 0:blocks(j), :], src[:, :, 0:blocks(j), :],
                               ACT.Exp).then_inc(s_e, 1)

            def copy_out(b, j):
                n = NT * b + j
                for c in range(2):
                    act.wait_ge(s_oT, 2 * n + c + 1)
                    if c == 0:
                        wait(act, s_y, n)
                    act.copy(flat(oT[:, c * NP // 2:(c + 1) * NP // 2, :]),
                             proj[:, c * BANK:(c + 1) * BANK]).then_inc(s_oTs, 1)

            def step(b, j):
                first = isinstance(b, int) and b == 0 and j == 0
                nxt, ahead = after(b, j, 1), after(b, j, 2)
                prev = (b - 1, NT - 1) if j == 0 else (b, j - 1)
                for i in range(NP):
                    exps(b, j, i)
                    if i == 2 and not first:
                        copy_out(*prev)
                    if i == 4 and nxt is not None:
                        copy_qk(*nxt)
                    if i == 5 and ahead is not None:
                        if ahead[1] == 0:
                            copy_xT(ahead[0])
                        squares(*ahead)

            copy_xT(0)
            squares(0, 0)
            copy_qk(0, 0)
            squares(0, 1)
            tiles(act, step)
            copy_out(B - 1, NT - 1)

        @block.vector
        def _(dve):
            def norm(b):
                wait(dve, s_xl, b)
                layernorm_dve(dve, b, row(hid, b), lnc[:, :, :], lnq[:, :, :], lns, [x2[:, :, :]],
                              s_ln, s_var, s_rstd, s_x)

            def split_x(b):
                dve.wait_ge(s_x, b + 1)
                wait(dve, s_xT, b)
                dve.tensor_copy(xs[:, :, 0, :], x2[:, :, :]).then_inc(s_xh, 1)
                dve.wait_ge(s_xh, b + 1)
                dve.tensor_tensor(xs[:, :, 1, :], x2[:, :, :], xs[:, :, 0, :], ALU.subtract).then_inc(s_xl, 1)

            def rotate_cos(b, j):
                n = NT * b + j
                dve.wait_ge(s_sq, n + 1)
                wait(dve, s_rot, n)
                dve.tensor_tensor(ra[:, :, :], qk_ps, w["cos_t"][:, j, :].unsqueeze(1).broadcast_to([P, QK, D]),
                                  ALU.mult)

            def rotate_sin(b, j):
                even = qk_ps[:, :, 0::2]
                odd = qk_ps[:, :, 1::2]
                dve.tensor_tensor(rb[:, :, 0::2], odd, w["nsin_t"][:, j, :].unsqueeze(1).broadcast_to([P, QK, D // 2]),
                                  ALU.mult)
                dve.tensor_tensor(rb[:, :, 1::2], even, w["sin_t"][:, j, :].unsqueeze(1).broadcast_to([P, QK, D // 2]),
                                  ALU.mult).then_inc(s_rab, 1)

            def sum_squares(b, j):
                n = NT * b + j
                dve.wait_ge(s_sq, n + 1)
                dve.tensor_reduce(ss[:, 0, :], sq[:, :, :], AX, ALU.add).then_inc(s_ssum, 1)

            def normalise(b, j):
                n = NT * b + j
                dve.wait_ge(s_rot, n + 1)
                dve.wait_ge(s_rms, n + 1)
                dve.tensor_tensor(qn[:, 0:NQ, :], rc[:, 0:NQ, :], each(ss[:, 2, 0:NQ], D), ALU.mult)
                dve.scalar_tensor_tensor(qn[:, NQ, :], rc[:, NQ, :], ss[:, 2, NQ:QK], w["kscale"][:, :],
                                         ALU.mult, ALU.mult).then_inc(s_qn, 1)

            def split_high(b, j):
                n = NT * b + j
                dve.wait_ge(s_qn, n + 1)
                wait(dve, s_qkT, n)
                dve.tensor_copy(qs[:, 0:NQ, 0, :], qn[:, 0:NQ, :])
                dve.tensor_copy(qs[:, NQ, :, :], qn[:, NQ:QK, :].broadcast_to([P, 2, D])).then_inc(s_qh, 1)

            def split_low(b, j):
                n = NT * b + j
                dve.wait_ge(s_qh, n + 1)
                dve.tensor_tensor(qs[:, 0:NQ, 1, :], qn[:, 0:NQ, :], qs[:, 0:NQ, 0, :], ALU.subtract)
                dve.tensor_tensor(qs[:, NQ + 1, :, :], qn[:, NQ:QK, :].broadcast_to([P, 2, D]), qs[:, NQ, :, :],
                                  ALU.subtract).then_inc(s_qs, 1)

            def maximum(b, j, i):
                n = NP * (NT * b + j) + i
                dve.wait_ge(s_S1, n + 1)
                if i == 0:
                    wait(dve, s_ST, n - NP)
                src = psum[:, (3 + i % 2) * BANK:(3 + i % 2) * BANK + 2 * P * blocks(j)]
                dve.tensor_reduce(mb[:, j % 2, 2 * i:2 * i + 2], src.rearrange("p (h k) -> p h k", h=2), AX,
                                  ALU.max).then_inc(s_m, 1)

            def divide(b, j, i):
                n = NP * (NT * b + j) + i
                dve.wait_ge(s_pv, n + 1)
                if i == 0:
                    wait(dve, s_oT, 2 * (NT * b + j) - 2)
                pv = psum[:, 7 * BANK:7 * BANK + 2 * VC].rearrange("p (h c) -> p h c", c=VC)
                dve.reciprocal(rcp[:, i % 2, :], pv[:, :, D]).then_inc(s_rcp, 1)
                dve.wait_ge(s_rcp, n + 1)
                dve.tensor_tensor(o[:, j % 2, 2 * i:2 * i + 2, :], pv[:, :, 0:D], each(rcp[:, i % 2, :], D),
                                  ALU.mult).then_inc(s_o, 1)

            def residual(b, j):
                dve.wait_ge(s_y, NT * b + j + 1)
                dst = row(hid, b)[:, j, :]
                dve.tensor_tensor(dst, dst, y_ps, ALU.add).then_inc(s_h, 1)

            def step(b, j):
                first = isinstance(b, int) and b == 0 and j == 0
                nxt, ahead = after(b, j, 1), after(b, j, 2)
                prev = (b - 1, NT - 1) if j == 0 else (b, j - 1)
                for i in range(NP):
                    if i + 2 < NP:
                        maximum(b, j, i + 2)
                    elif nxt is not None:
                        maximum(*nxt, i + 2 - NP)
                    if i >= 2:
                        divide(b, j, i - 2)
                    elif not first:
                        divide(*prev, i + NP - 2)
                    if i == 2 and nxt is not None:
                        normalise(*nxt)
                    if i == 3 and nxt is not None:
                        split_high(*nxt)
                        split_low(*nxt)
                    if i == 3 and not first:
                        residual(*prev)
                    if i == 5 and j == 1 and after(b, j, 3) is not None:
                        norm(after(b, j, 3)[0])
                        split_x(after(b, j, 3)[0])
                    if i == 6 and ahead is not None:
                        rotate_cos(*ahead)
                    if i == 7 and ahead is not None:
                        rotate_sin(*ahead)
                        sum_squares(*ahead)

            dve.memset(vv[:, :, D:VC], 1.0)
            norm(0)
            split_x(0)
            rotate_cos(0, 0)
            rotate_sin(0, 0)
            sum_squares(0, 0)
            normalise(0, 0)
            split_high(0, 0)
            split_low(0, 0)
            rotate_cos(0, 1)
            rotate_sin(0, 1)
            sum_squares(0, 1)
            maximum(0, 0, 0)
            maximum(0, 0, 1)
            tiles(dve, step)
            divide(B - 1, NT - 1, NP - 2)
            divide(B - 1, NT - 1, NP - 1)
            residual(B - 1, NT - 1)


def feed_forward(nc, w, hid, zw, wall, w_dram, psum):
    with ExitStack() as ctx:
        def sb(name, shape, dt=F32):
            return ctx.enter_context(nc.sbuf_tensor(name, shape, dt))

        def sem(name):
            return ctx.enter_context(nc.semaphore(name))

        def bank(n, lo, hi, parts=P):
            return psum[0:parts, n * BANK + lo:n * BANK + hi]

        lnc = sb("lnc3", [P, NT, D])
        lnq = sb("lnq3", [P, NT, D])
        lns = sb("lns3", [P, 5, NT])
        x3 = sb("x3", [P, NT, D])
        xT = sb("xT3", [D, S])
        gf = sb("gf", [P, FC, S])
        wcol = sb("wcol", [P, NT])
        yb = sb("yb", [P, NT, D])
        wrow = sb("wrow", [1, S])

        s_ln = sem("s3_ln")
        s_var = sem("s3_var")
        s_vt = sem("s3_vt")
        s_rstd = sem("s3_rstd")
        s_x = sem("s3_x")
        s_base = sem("s3_base")
        s_xT = sem("s3_xT")
        s_xTs = sem("s3_xTs")
        s_w = sem("s3_w")
        s_wrow = sem("s3_wrow")
        s_wall = sem("s3_wall")
        s_wback = sem("s3_wback")
        s_wcol = sem("s3_wcol")
        s_h = sem("s3_h")
        s_g = sem("s3_g")
        s_y = sem("s3_y")
        s_yb = sem("s3_yb")
        s_zw = sem("s3_zw")

        passed_pool, passed_pe, passed_dve = (sem(f"s3_passed_{e}") for e in ("pool", "pe", "dve"))

        block = ctx.enter_context(nc.Block())

        @block.sync
        def _(sp):
            def store(b):
                sp.wait_ge(s_wrow, b + 1)
                sp.dma_start(w_dram[bass.ds(b, 1), :], wrow[:, :]).then_inc(s_wall, 16)
            batches(sp, store)
            sp.wait_ge(s_wall, 16 * B)
            sp.dma_start(wall[:, :], w_dram[:, :]).then_inc(s_wback, 16)
            sp.wait_ge(s_wback, 16)

        @block.gpsimd
        def _(pool):
            batches(pool, lambda b: rstd_pool(pool, b, lns[:, 3, :], lns[:, 2, :], lns[:, 4, :],
                                              w["mhalf"][:, 0:NT], D, EPS, s_var, s_vt, s_rstd, passed_pool))

        @block.tensor
        def _(pe):
            def transpose_x(b):
                pe.wait_ge(s_x, b + 1)
                wait(pe, s_xTs, b)
                apart(pe, passed_pe)
                for j in range(NT):
                    last = pe.transpose(bank(0, j * P, j * P + P, D), x3[:, j, :], w["ident"][:, :])
                last.then_inc(s_xT, 1)

            def feed(b):
                pe.wait_ge(s_xTs, b + 1)
                wait(pe, s_wcol, b)
                wait(pe, s_wrow, b)
                for j in range(NT):
                    pe.matmul(bank(6, j, j + 1), xT[:, j * P:(j + 1) * P], w["wrf"][:, :], start=True, stop=True)
                pe.matmul(bank(7, 0, S, 1), w["wrf"][:, :], xT[:, :], start=True, stop=True).then_inc(s_w, 1)
                for c in range(FC):
                    wait(pe, s_g, FC * b)
                    pe.matmul(bank(1 + c, 0, S), w["w1f"][:, c * P:(c + 1) * P], xT[:, :], start=True,
                              stop=True).then_inc(s_h, 1)

            def out(b):
                pe.wait_ge(s_g, FC * b + FC)
                wait(pe, s_yb, b)
                for j in range(NT):
                    for c in range(FC):
                        last = pe.matmul(bank(5, j * D, j * D + D), gf[:, c, j * P:(j + 1) * P], w["w2f"][:, c, :],
                                         start=c == 0, stop=c == FC - 1)
                last.then_inc(s_y, 1)

            transpose_x(0)
            def both(b):
                feed(b - 1)
                transpose_x(b)
                out(b - 1)

            both(1)
            with pe.Fori(2, B, 1) as b:
                both(b)
            feed(B - 1)
            out(B - 1)

        @block.scalar
        def _(act):
            def copy_xT(b):
                act.wait_ge(s_xT, b + 1)
                wait(act, s_h, FC * b)
                act.copy(xT[:, :], bank(0, 0, S, D)).then_inc(s_xTs, 1)

            def feed(b):
                act.wait_ge(s_w, b + 1)
                wait(act, s_wall, 16 * b)
                act.activation(wrow[:, :], bank(7, 0, S, 1), ACT.Identity,
                               bias=w["brf"][0:1, 0:1]).then_inc(s_wrow, 1)
                for c in range(FC):
                    act.wait_ge(s_h, FC * b + c + 1)
                    wait(act, s_y, b)
                    act.activation(gf[:, c, :], bank(1 + c, 0, S), ACT.Gelu_apprx_tanh,
                                   bias=w["b1f"][:, c:c + 1]).then_inc(s_g, 1)

            copy_xT(0)
            def both(b):
                feed(b - 1)
                copy_xT(b)

            both(1)
            with act.Fori(2, B, 1) as b:
                both(b)
            feed(B - 1)

        @block.vector
        def _(dve):
            def norm(b):
                wait(dve, s_xT, b)
                layernorm_dve(dve, b, row(hid, b), lnc[:, :, :], lnq[:, :, :], lns, [x3[:, :, :]],
                              s_ln, s_var, s_rstd, s_x)
                dve.wait_ge(s_x, b + 1)
                dve.tensor_tensor(row(hid, b), row(hid, b), x3[:, :, :], ALU.add).then_inc(s_base, 1)

            def out(b):
                dve.wait_ge(s_w, b + 1)
                wait(dve, s_zw, b)
                dve.tensor_scalar(wcol[:, :], bank(6, 0, NT), w["brf"][:, 0:1], None, ALU.add).then_inc(s_wcol, 1)
                dve.wait_ge(s_y, b + 1)
                dve.tensor_tensor(yb[:, :, :], bank(5, 0, NT * D).rearrange("p (a d) -> p a d", d=D),
                                  w["b2f"][:, :].unsqueeze(1).broadcast_to([P, NT, D]), ALU.add).then_inc(s_yb, 1)
                dve.wait_ge(s_yb, b + 1)
                dve.tensor_tensor(row(zw, b), yb[:, :, :], each(wcol[:, :], D), ALU.mult).then_inc(s_zw, 1)

            norm(0)
            def both(b):
                norm(b)
                out(b - 1)

            both(1)
            with dve.Fori(2, B, 1) as b:
                both(b)
            out(B - 1)


def select_and_store(nc, w, hid, zw, wall, psum, out):
    OG = 4
    ROUNDS = (KEEP + 1) // 8
    with ExitStack() as ctx:
        def sb(name, shape, dt=F32):
            return ctx.enter_context(nc.sbuf_tensor(name, shape, dt))

        def sem(name):
            return ctx.enter_context(nc.semaphore(name))

        work = sb("work", [B, S])
        t8 = sb("t8", [B, 8])
        i8 = sb("i8", [B, 8], U32)
        i8f = sb("i8f", [B, 8])
        drop = sb("drop", [B, S])
        sel = sb("sel", [B, S])
        selT = sb("selT", [P, NT, B])
        add = sb("add", [P, 2, OG, NT, D])

        s_top = sem("s4_top")
        s_rep = sem("s4_rep")
        s_idx = sem("s4_idx")
        s_sel = sem("s4_sel")
        s_selT = sem("s4_selT")
        s_selTs = sem("s4_selTs")
        s_add = sem("s4_add")
        s_out = sem("s4_out")
        s_done = sem("s4_done")

        out_v = out.rearrange("b (j p) d -> p b j d", p=P)
        passed_pool, passed_pe, passed_dve = (sem(f"s4_passed_{e}") for e in ("pool", "pe", "dve"))

        block = ctx.enter_context(nc.Block())

        @block.vector
        def _(dve):
            dve.max(t8[:, :], wall[:, :]).then_inc(s_top, 1)
            dve.wait_ge(s_top, 1)
            dve.match_replace(work[:, :], t8[:, :], wall[:, :], TAKEN).then_inc(s_rep, 1)

            with dve.Fori(1, ROUNDS - 1, 1) as r:
                dve.wait_ge(s_rep, r)
                apart(dve, passed_dve)
                dve.max(t8[:, :], work[:, :]).then_inc(s_top, 1)
                dve.wait_ge(s_top, r + 1)
                apart(dve, passed_dve)
                dve.match_replace(work[:, :], t8[:, :], work[:, :], TAKEN).then_inc(s_rep, 1)
            dve.wait_ge(s_rep, ROUNDS - 1)
            dve.max(t8[:, :], work[:, :]).then_inc(s_top, 1)
            dve.wait_ge(s_top, ROUNDS)
            dve.max_index(i8[:, :], t8[:, :], work[:, :]).then_inc(s_idx, 1)
            dve.match_replace(work[:, :], t8[:, :], work[:, :], TAKEN).then_inc(s_rep, 1)
            dve.wait_ge(s_idx, 1)
            dve.tensor_copy(i8f[:, :], i8[:, :]).then_inc(s_idx, 1)
            dve.wait_ge(s_idx, 2)
            dve.tensor_scalar(drop[:, :], w["iota_row"][:, :], i8f[:, 7:8], None, ALU.is_equal).then_inc(s_idx, 1)
            dve.wait_ge(s_idx, 3)
            dve.wait_ge(s_rep, ROUNDS)
            dve.scalar_tensor_tensor(sel[:, :], work[:, :], TAKEN, drop[:, :], ALU.is_equal,
                                     ALU.subtract).then_inc(s_sel, 1)
            dve.wait_ge(s_selT, 1)
            dve.tensor_copy(selT[:, :, :].rearrange("p a b -> p (a b)"), psum[:, 0:NT * B]).then_inc(s_selTs, 1)
            dve.wait_ge(s_selTs, 1)
            for q in range(B // OG):
                rows = slice(q * OG, (q + 1) * OG)
                if q >= 2:
                    dve.wait_ge(s_out, q - 1)
                m = selT[:, :, rows].rearrange("p a b -> p b a").unsqueeze(3).broadcast_to([P, OG, NT, D])
                dve.tensor_tensor(add[:, q % 2, :, :, :], zw[:, rows, :, :], m, ALU.mult).then_inc(s_add, 1)
                dve.wait_ge(s_add, q + 1)
                dve.tensor_tensor(hid[:, rows, :, :], hid[:, rows, :, :], add[:, q % 2, :, :, :],
                                  ALU.add).then_inc(s_out, 1)

        @block.tensor
        def _(pe):
            pe.wait_ge(s_sel, 1)
            for j in range(NT):
                last = pe.transpose(psum[:, j * B:(j + 1) * B], sel[:, j * P:(j + 1) * P], w["ident"][0:B, 0:B])
            last.then_inc(s_selT, 1)

        @block.sync
        def _(sp):
            for q in range(B // OG):
                sp.wait_ge(s_out, q + 1)
                sp.dma_start(out_v[:, q * OG:(q + 1) * OG, :, :].rearrange("p b j d -> p (b j) d"),
                             hid[:, q * OG:(q + 1) * OG, :, :].rearrange("p b j d -> p (b j) d")).then_inc(s_done, 16)
            sp.wait_ge(s_done, 16 * (B // OG))


SHAPES = {
    "ident": (P, [P]), "causal": (P, [P]), "wmask_f": (P, [2 * P]), "cos_t": (P, [NT, D]), "sin_t": (P, [NT, D // 2]),
    "nsin_t": (P, [NT, D // 2]), "iota8": (P, [NE]), "iota_row": (B, [S]), "mhalf": (P, [QK]),
    "coef": (NF, [D]), "qw0": (D, [H0 * D]), "ew0": (D, [H0 * D]), "gam": (D, [1]), "bet": (D, [1]),
    "wr0": (D, [NE]), "br0": (P, [NE]), "w1e": (D, [NE, HID]), "b1e": (P, [NE]), "w2e": (P, [NE, D]),
    "b2p": (NT * NE, [NT, D]), "wq1": (P, [NQ * D]), "wkv": (P, [2 * D]), "wo1": (P, [NP, D]), "qnw": (P, [D]),
    "knw": (P, [D]), "wrf": (D, [1]), "brf": (P, [1]), "w1f": (D, [FF]), "b1f": (P, [FC]), "w2f": (P, [FC, D]),
    "b2f": (P, [D]),
}


def tower(nc, a, ids, turns, out):
    with ExitStack() as ctx:
        def sb(name, shape, dt=F32):
            return ctx.enter_context(nc.sbuf_tensor(name, shape, dt))

        def sem(name):
            return ctx.enter_context(nc.semaphore(name))

        w = {}
        for name, (parts, free) in SHAPES.items():
            w[name] = sb("c_" + name, [parts] + free)
        w["identb"] = sb("identb", [P, P], BF16)
        w["nidentb"] = sb("nidentb", [P, P], BF16)
        w["wmask"] = sb("wmask", [P, 2 * P], BF16)
        w["identh"] = sb("identh", [P, P], F16)
        w["kscale"] = sb("kscale", [P, D])
        for name, cols in (("wq", NQ * D), ("wkv", 2 * D)):
            w[name + "h"] = sb(name + "h", [P, cols], F16)
            w[name + "l"] = sb(name + "l", [P, cols], F16)
        hid = sb("hid", [P, B, NT, D])
        zw = sb("zw", [P, B, NT, D])
        wall = sb("wall", [B, S])
        w_dram = nc.dram_tensor("router_weights", (B, S), F32).ap()
        psum = ctx.enter_context(nc.psum_tensor("psum", [P, 8 * BANK], F32))

        s_load = sem("s_load")
        s_high = sem("s_high")
        with nc.Block() as block:
            @block.sync
            def _(sp):
                for name in SHAPES:
                    parts, free = SHAPES[name]
                    dst = w[name]
                    dst = dst[:, :] if len(free) == 1 else dst[:, :, :]
                    sp.dma_start(dst, a[name]).then_inc(s_load, 16)

            @block.vector
            def _(dve):
                dve.wait_ge(s_load, 16 * len(SHAPES))
                dve.tensor_copy(w["identb"][:, :], w["ident"][:, :])
                dve.tensor_scalar(w["nidentb"][:, :], w["ident"][:, :], -1.0, None, ALU.mult)
                dve.tensor_copy(w["wmask"][:, :], w["wmask_f"][:, :])
                dve.tensor_copy(w["identh"][:, :], w["ident"][:, :])
                dve.scalar_tensor_tensor(w["kscale"][:, :], w["qnw"][:, :], float(D) ** -0.5, w["knw"][:, :],
                                         ALU.mult, ALU.mult)
                dve.tensor_copy(w["wqh"][:, :], w["wq1"][:, :])
                dve.tensor_copy(w["wkvh"][:, :], w["wkv"][:, :]).then_inc(s_high, 1)
                dve.wait_ge(s_high, 1)
                dve.tensor_tensor(w["wql"][:, :], w["wq1"][:, :], w["wqh"][:, :], ALU.subtract)
                dve.tensor_tensor(w["wkvl"][:, :], w["wkv"][:, :], w["wkvh"][:, :], ALU.subtract)

        embed_attend_experts(nc, w, ids, turns, hid, psum)
        windowed_attention(nc, w, hid, psum)
        feed_forward(nc, w, hid, zw, wall, w_dram, psum)
        select_and_store(nc, w, hid, zw, wall, psum, out)


def layouts(x):
    f = {k: np.asarray(v) for k, v in x.items()}
    t = np.arange(S, dtype=np.float32)[:, None]
    freq = np.float32(10000.0) ** (-2.0 * np.arange(D // 2, dtype=np.float32) / D)
    theta = (t * freq[None, :].astype(np.float32)).astype(np.float32)
    cos = np.cos(theta).astype(np.float32).reshape(NT, P, D // 2).transpose(1, 0, 2)
    sin = np.sin(theta).astype(np.float32).reshape(NT, P, D // 2).transpose(1, 0, 2)
    q, k = np.arange(P)[:, None], np.arange(2 * P)[None, :] - P
    b2p = np.zeros((NT, NE, NT, D), np.float32)
    for j in range(NT):
        b2p[j, :, j, :] = f["L0_ffn_b2"]
    arrays = {
        "ident": np.eye(P, dtype=np.float32),
        "causal": np.triu(np.ones((P, P), np.float32)),
        "wmask_f": np.where((k <= q) & (q - k <= P), 0.0, NEG).astype(np.float32),
        "cos_t": np.repeat(cos, 2, axis=2), "sin_t": sin, "nsin_t": -sin,
        "iota8": np.tile(np.arange(NE, dtype=np.float32), (P, 1)),
        "iota_row": np.tile(np.arange(S, dtype=np.float32), (B, 1)),
        "mhalf": np.full((P, QK), -0.5, np.float32),
        "coef": f["L0_tok_poly_coeffs"].reshape(NF, D),
        "qw0": f["L0_attn_Q"].transpose(1, 0, 2).reshape(D, H0 * D),
        "ew0": f["L0_attn_E"].transpose(2, 0, 1).reshape(D, H0 * D),
        "gam": f["L0_ffn_gamma"].reshape(D, 1), "bet": f["L0_ffn_beta"].reshape(D, 1),
        "wr0": f["L0_ffn_Wr"], "br0": np.tile(f["L0_ffn_br"], (P, 1)),
        "w1e": f["L0_ffn_W1"].transpose(1, 0, 2), "b1e": f["L0_ffn_b1"].T,
        "w2e": f["L0_ffn_W2"].transpose(1, 0, 2), "b2p": b2p.reshape(NT * NE, NT, D),
        "wq1": np.tile(f["L1_attn_wq"].T, (2, 1)), "wkv": np.tile(f["L1_attn_wkv"].T, (2, 1)),
        "wo1": f["L1_attn_wo"].T.reshape(NP, P, D).transpose(1, 0, 2),
        "qnw": np.tile(f["L1_attn_q_norm_w"], (P, 1)), "knw": np.tile(f["L1_attn_k_norm_w"], (P, 1)),
        "wrf": f["L1_ffn_wr"], "brf": np.tile(f["L1_ffn_br"], (P, 1)),
        "w1f": f["L1_ffn_w1"], "b1f": f["L1_ffn_b1"].reshape(FC, P).T,
        "w2f": f["L1_ffn_w2"].reshape(FC, P, D).transpose(1, 0, 2), "b2f": np.tile(f["L1_ffn_b2"], (P, 1)),
    }
    arrays = {k: np.ascontiguousarray(v) for k, v in arrays.items()}
    ids = np.ascontiguousarray(f["x"].reshape(B * NT, P).T)
    return arrays, ids, np.ascontiguousarray(f["L0_tok_turns"])


def kernel(**inputs):
    import concourse.bacc as bacc
    from concourse.bass_utils import run_bass_kernel_spmd

    arrays, ids, turns = layouts(inputs)
    nc = bacc.Bacc("TRN2", target_bir_lowering=False, num_devices=1)
    feeds, a = {}, {}
    for name, v in arrays.items():
        feeds["in_" + name] = v
        a[name] = nc.dram_tensor("in_" + name, v.shape, F32, kind="ExternalInput").ap()
    feeds["in_ids"], feeds["in_turns"] = ids, turns
    ids_d = nc.dram_tensor("in_ids", ids.shape, mybir.dt.from_np(ids.dtype), kind="ExternalInput").ap()
    turns_d = nc.dram_tensor("in_turns", turns.shape, F32, kind="ExternalInput").ap()
    out = nc.dram_tensor("out", (B, S, D), F32, kind="ExternalOutput").ap()
    tower(nc, a, ids_d, turns_d, out)
    r = run_bass_kernel_spmd(nc, [feeds], core_ids=[0])
    return r.results[0]["out"]
```

```python
from contextlib import ExitStack

import numpy as np

import concourse.bass as bass
from concourse import mybir

F32 = mybir.dt.float32
BF16 = mybir.dt.bfloat16
F16 = mybir.dt.float16
I32 = mybir.dt.int32
U32 = mybir.dt.uint32
ALU = mybir.AluOpType
ACT = mybir.ActivationFunctionType
AX = mybir.AxisListType.X

P = 128
B, S, D = 32, 512, 64
NT = S // P
TURNS, DEG = 4, 5
NF = TURNS * DEG
H0 = 8
HP0 = H0 // 2
NE, HID = 8, 128
NQ = 16
NP = NQ // 2
FF = 256
FC = FF // P
KEEP = 255
EPS = 1e-5
RMS_EPS = 1.1920929e-07
NEG = -1e30
TAKEN = -3.0e38
QK = NQ + 1
VC = D + 1
BANK = 512


def wait(eng, sem, value):
    if isinstance(value, int) and value <= 0:
        return
    eng.wait_ge(sem, value)


def apart(eng, passed):
    eng.sem_inc(passed, 1)


def each(ap, n):
    return ap.unsqueeze(2).broadcast_to([ap.shape[0], ap.shape[1], n])


def flat(ap):
    return ap.rearrange("p a b -> p (a b)")


def row(hid, b):
    return hid[:, bass.ds(b, 1), :, :].rearrange("p o a b -> p (o a) b")


LN_STEPS = 4
SCALE0 = 64.0


def layernorm_sums(eng, b, src, cent, sq, st, step, var_ready):
    base = LN_STEPS * b
    eng.tensor_reduce(st[:, 0, :], src, AX, ALU.add).then_inc(step, 1)
    eng.wait_ge(step, base + 1)
    eng.tensor_scalar(st[:, 1, :], st[:, 0, :], 1.0 / D, None, ALU.mult).then_inc(step, 1)
    eng.wait_ge(step, base + 2)
    eng.tensor_tensor(cent, src, each(st[:, 1, :], D), ALU.subtract).then_inc(step, 1)
    eng.wait_ge(step, base + 3)
    eng.tensor_tensor(sq, cent, cent, ALU.mult).then_inc(step, 1)
    eng.wait_ge(step, base + 4)
    eng.tensor_reduce(st[:, 2, :], sq, AX, ALU.add).then_inc(var_ready, 1)


def rstd_pool(eng, n, out, ssum, tmp, mhalf, width, eps, sum_ready, tmp_ready, ready, passed):
    eng.wait_ge(sum_ready, n + 1)
    apart(eng, passed)
    eng.tensor_scalar(tmp, ssum, 1.0 / width, eps, ALU.mult, ALU.add).then_inc(tmp_ready, 1)
    eng.wait_ge(tmp_ready, n + 1)
    eng.tensor_tensor(out, tmp, mhalf, ALU.pow).then_inc(ready, 1)


def batches(eng, body, first=0, last=B):
    body(first)
    with eng.Fori(first + 1, last, 1) as b:
        body(b)


def embed_attend_experts(nc, w, ids, turns, hid, psum):
    with ExitStack() as ctx:
        def sb(name, shape, dt=F32):
            return ctx.enter_context(nc.sbuf_tensor(name, shape, dt))

        def sem(name):
            return ctx.enter_context(nc.semaphore(name))

        def bank(n, lo, hi, parts=P):
            return psum[0:parts, n * BANK + lo:n * BANK + hi]

        VA = 0
        SCORES = 2
        KV = 4
        Y = 6
        MISC = 7
        B2 = 2 * P

        def hidden_bank(e):
            return (5, 1)[e % 2]

        NYT = 4
        idx = sb("idx", [P, NT], I32)
        gath = sb("gath", [P, NT * TURNS])
        tk = sb("tk", [P, 5, NT * TURNS])
        tki = sb("tki", [P, NT * TURNS], I32)
        xp = sb("xp", [P, NT, TURNS, DEG])
        xpT = sb("xpT", [NF, S])
        lnc = sb("lnc", [P, NT, D])
        lnq = sb("lnq", [P, NT, D])
        lns = sb("lns", [P, 5, NT])
        r2 = sb("r2", [P, NT, 2, D])
        rs = sb("rs", [P, NT, 2, D], F16)
        rT = sb("rT", [P, S])
        rsT = sb("rsT", [P, S], F16)
        AT = sb("AT", [P, HP0, S])
        V0 = sb("V0", [P, 2, H0 * D])
        Om = sb("Om", [P, 2, H0, P])
        KVs = sb("KVs", [P, 2, HP0 * D])
        zc = sb("zc", [P, NT, D])
        zq = sb("zq", [P, NT, D])
        zs = sb("zs", [P, 6, NT])
        z = sb("z", [P, NT, D])
        zp = sb("zp", [P, NT, 2, D], F16)
        zT = sb("zT", [P, S], F16)
        lg = sb("lg", [P, NT, NE])
        top = sb("top", [P, NT, 8])
        topi = sb("topi", [P, NT, 8], U32)
        topf = sb("topf", [P, NT, 8])
        gd = sb("gd", [P, 4, NT])
        gw = sb("gw", [P, 4, NT, NE])
        wfull = sb("wfull", [P, NT, NE])
        wT = sb("wT", [NT * NE, P])
        g = sb("g", [P, 2, S])
        ytmp = sb("ytmp", [P, NYT, NT, D])

        s_ids = sem("s_ids")
        s_gath = sem("s_gath")
        s_tk = sem("s_tk")
        s_xp = sem("s_xp")
        s_xpT = sem("s_xpT")
        s_xpTs = sem("s_xpTs")
        s_h0 = sem("s_h0")
        s_h0s = sem("s_h0s")
        s_ln = sem("s_ln")
        s_var = sem("s_var")
        s_vt = sem("s_vt")
        s_rstd = sem("s_rstd")
        s_r = sem("s_r")
        s_rs = sem("s_rs")
        s_rT = sem("s_rT")
        s_rTs = sem("s_rTs")
        s_rsT = sem("s_rsT")
        s_rsTs = sem("s_rsTs")
        s_A = sem("s_A")
        s_As = sem("s_As")
        s_V = sem("s_V")
        s_Vs = sem("s_Vs")
        s_Om = sem("s_Om")
        s_Oms = sem("s_Oms")
        s_KV = sem("s_KV")
        s_KVs = sem("s_KVs")
        s_att = sem("s_att")
        s_h1 = sem("s_h1")
        s_zln = sem("s_zln")
        s_zvar = sem("s_zvar")
        s_zvt = sem("s_zvt")
        s_zrstd = sem("s_zrstd")
        s_z = sem("s_z")
        s_zp = sem("s_zp")
        s_zT = sem("s_zT")
        s_zTs = sem("s_zTs")
        s_lg = sem("s_lg")
        s_lgs = sem("s_lgs")
        s_gate = sem("s_gate")
        s_gd = sem("s_gd")
        s_th = sem("s_th")
        s_w = sem("s_w")
        s_wT = sem("s_wT")
        s_wTs = sem("s_wTs")
        s_b2 = sem("s_b2")
        s_b2s = sem("s_b2s")
        s_hT = sem("s_hT")
        s_g = sem("s_g")
        s_y = sem("s_y")
        s_yt = sem("s_yt")
        s_add = sem("s_add")

        GATE_STEPS = 4 + 2 * NT
        TK_STEPS = 9

        passed_pool, passed_pe, passed_dve = (sem(f"s1_passed_{e}") for e in ("pool", "pe", "dve"))

        def upto(n, each_batch=1):
            return min(n, B * each_batch) if isinstance(n, int) else n

        def steps(eng, start, step):
            start()
            step(0, True, True, False, False)
            step(1, True, True, True, False)
            step(2, True, True, True, True)
            with eng.Fori(3, B - 2, 1) as b:
                step(b, True, True, True, True)
            step(B - 2, True, True, True, True)
            step(B - 1, False, True, True, True)
            step(B, False, False, True, True)
            step(B + 1, False, False, False, True)

        block = ctx.enter_context(nc.Block())

        @block.sync
        def _(sp):
            def load(b):
                wait(sp, s_gath, 64 * b)
                sp.dma_start(idx[:, :], ids[:, bass.ds(b * NT, NT)]).then_inc(s_ids, 16)
            batches(sp, load)

        @block.gpsimd
        def _(pool):
            def gather(b):
                pool.wait_ge(s_ids, 16 * b + 16)
                wait(pool, s_xp, b)
                apart(pool, passed_pool)
                for j in range(NT):
                    pool.indirect_dma_start(gath[:, j * TURNS:(j + 1) * TURNS], None, turns,
                                            bass.IndirectOffsetOnAxis(ap=idx[:, j:j + 1], axis=0)
                                            ).then_inc(s_gath, 16)

            def attend_norm(b):
                rstd_pool(pool, b, lns[:, 3, :], lns[:, 2, :], lns[:, 4, :], w["mhalf"][:, 0:NT], D, EPS,
                          s_var, s_vt, s_rstd, passed_pool)

            def expert_norm(b):
                pool.wait_ge(s_zvar, b + 1)
                apart(pool, passed_pool)
                v, t, r = zs[:, 2, :], zs[:, 4, :], zs[:, 5, :]
                pool.tensor_scalar(t, v, 1.0 / D, EPS, ALU.mult, ALU.add).then_inc(s_zvt, 1)
                pool.wait_ge(s_zvt, 6 * b + 1)
                pool.tensor_tensor(r, t, w["mhalf"][:, 0:NT], ALU.pow).then_inc(s_zvt, 1)
                pool.wait_ge(s_zvt, 6 * b + 2)
                pool.tensor_tensor(t, r, r, ALU.mult).then_inc(s_zvt, 1)
                pool.wait_ge(s_zvt, 6 * b + 3)
                pool.tensor_tensor(t, t, v, ALU.mult).then_inc(s_zvt, 1)
                pool.wait_ge(s_zvt, 6 * b + 4)
                apart(pool, passed_pool)
                pool.tensor_scalar(t, t, 1.0 / D, EPS, ALU.mult, ALU.add).then_inc(s_zvt, 1)
                pool.wait_ge(s_zvt, 6 * b + 5)
                pool.tensor_tensor(t, t, w["mhalf"][:, 0:NT], ALU.pow).then_inc(s_zvt, 1)
                pool.wait_ge(s_zvt, 6 * b + 6)
                pool.tensor_tensor(zs[:, 3, :], t, r, ALU.mult).then_inc(s_zrstd, 1)

            def add_expert(b, e):
                pool.wait_ge(s_yt, NE * b + e + 1)
                if e == 0:
                    pool.wait_ge(s_b2s, b + 1)
                else:
                    pool.wait_ge(s_add, NE * b + e)
                apart(pool, passed_pool)
                pool.tensor_tensor(row(hid, b), row(hid, b), ytmp[:, e % NYT, :, :], ALU.add).then_inc(s_add, 1)

            def start():
                gather(0)
                attend_norm(0)
                gather(1)

            def step(b, nxt, own, before, experts):
                if before:
                    expert_norm(b - 1)
                for j in range(NT):
                    if experts:
                        add_expert(b - 2, 2 * j)
                    if j == 0 and nxt and not (isinstance(b, int) and b + 2 >= B):
                        gather(b + 2)
                    if experts:
                        add_expert(b - 2, 2 * j + 1)
                    if j == 1 and nxt:
                        attend_norm(b + 1)

            steps(pool, start, step)

        @block.tensor
        def _(pe):
            def mm(out, lhsT, rhs, start=True, stop=True):
                return pe.matmul(out, lhsT, rhs, start=start, stop=stop, skip_group_check=True)

            def transpose_powers(b):
                pe.wait_ge(s_xp, b + 1)
                wait(pe, s_b2s, b - 2)
                for j in range(NT):
                    last = pe.transpose(bank(MISC, j * P, j * P + P, NF), flat(xp[:, j, :, :]), w["ident"][:, :])
                last.then_inc(s_xpT, 1)

            def embed(b):
                pe.wait_ge(s_xpTs, b + 1)
                for j in range(NT):
                    last = mm(bank(MISC, j * D, j * D + D), xpT[:, j * P:(j + 1) * P], w["coef"][:, :])
                last.then_inc(s_h0, 1)

            def transpose_r(b):
                pe.wait_ge(s_r, b + 1)
                wait(pe, s_lgs, b - 1)
                for j in range(NT):
                    last = pe.transpose(bank(MISC, j * P, j * P + P), flat(r2[:, j, :, :]), w["ident"][:, :])
                last.then_inc(s_rT, 1)

            def transpose_rs(b):
                pe.wait_ge(s_rs, b + 1)
                wait(pe, s_h1, NT * b)
                for j in range(NT):
                    last = pe.transpose(bank(VA, j * D, j * D + D).bitcast(F16), flat(rs[:, j, :, :]),
                                        w["identh"][:, :])
                last.then_inc(s_rsT, 1)

            def project(b, p):
                if p == 0:
                    pe.wait_ge(s_rsTs, b + 1)
                elif p == 1:
                    pe.wait_ge(s_rTs, b + 1)
                else:
                    pe.wait_ge(s_As, HP0 * b + p - 1)
                dst = bank(VA if p % 2 == 0 else MISC, 0, S)
                mm(dst, w["qwh"][:, p * P:(p + 1) * P], rsT[:, :], True, False)
                mm(dst, w["qwl"][:, p * P:(p + 1) * P], rsT[:, :], False, True).then_inc(s_A, 1)

            def values(b, j):
                if j == 0:
                    pe.wait_ge(s_As, HP0 * b + HP0 - 1)
                else:
                    pe.wait_ge(s_h1, NT * b + j)
                t = slice(j * P, (j + 1) * P)
                mm(bank(VA, 0, H0 * D), rsT[:, t], w["ewh"][:, :], True, False)
                mm(bank(VA, 0, H0 * D), rsT[:, t], w["ewl"][:, :], False, True).then_inc(s_V, 1)

            def scores(b, j):
                t = slice(j * P, (j + 1) * P)
                if j == 0:
                    pe.wait_ge(s_As, HP0 * b + HP0)
                wait(pe, s_Oms, NT * b + j)
                for h in range(H0):
                    c = slice((h % 2) * D, (h % 2) * D + D)
                    o = (SCORES + h % 2) * BANK + h // 2 * P
                    last = mm(psum[:, o:o + P], rT[c, t], AT[c, h // 2, t])
                last.then_inc(s_Om, 1)

            def add_kv(b, j):
                pe.wait_ge(s_Vs, NT * b + j + 1)
                wait(pe, s_KVs, 3 * b + j)
                apart(pe, passed_pe)
                v = V0[:, j % 2, :].rearrange("p (c two d) -> p c two d", two=2, d=D)
                for half in range(2):
                    last = mm(psum[half * D:half * D + D, KV * BANK:KV * BANK + HP0 * D], r2[:, j, 0, :],
                              v[:, :, half, :], j == 0, j == NT - 2)
                last.then_inc(s_KV, 1)

            def attend(b, j):
                pe.wait_ge(s_Oms, NT * b + j + 1)
                pe.wait_ge(s_Vs, NT * b + j + 1)
                if j >= 1:
                    pe.wait_ge(s_KVs, 3 * b + j)
                t = slice(j * P, (j + 1) * P)
                dst = bank(VA, 0, D)
                for h in range(H0):
                    last = mm(dst, Om[:, j % 2, (h % 2) * HP0 + h // 2, :], V0[:, j % 2, h * D:(h + 1) * D], h == 0,
                              j == 0 and h == H0 - 1)
                if j >= 1:
                    for p in range(HP0):
                        last = mm(dst, AT[:, p, t], KVs[:, (j - 1) % 2, p * D:(p + 1) * D], False, p == HP0 - 1)
                last.then_inc(s_att, 1)

            def transpose_z(b):
                pe.wait_ge(s_zp, b + 1)
                pe.wait_ge(s_h0s, upto(b + 3))
                for j in range(NT):
                    last = pe.transpose(bank(MISC, j * D, j * D + D).bitcast(F16), flat(zp[:, j, :, :]),
                                        w["identh"][:, :])
                last.then_inc(s_zT, 1)

            def gate_logits(b):
                pe.wait_ge(s_zTs, b + 1)
                for j in range(NT):
                    dst = bank(MISC, j * NE, j * NE + NE)
                    mm(dst, zT[:, j * P:(j + 1) * P], w["wrh"][:, :], True, False)
                    last = mm(dst, zT[:, j * P:(j + 1) * P], w["wrl"][:, :], False, True)
                last.then_inc(s_lg, 1)

            def transpose_gates(b):
                pe.wait_ge(s_w, b + 1)
                wait(pe, s_As, upto(HP0 * (b + 3), HP0))
                pe.transpose(bank(MISC, 0, P, NT * NE), flat(wfull[:, :, :]), w["ident"][:, :]).then_inc(s_wT, 1)

            def gated_biases(b):
                pe.wait_ge(s_wTs, b + 1)
                for j in range(NT):
                    last = mm(bank(MISC, B2 + j * D, B2 + j * D + D), wT[:, :], w["b2p"][:, j, :])
                last.then_inc(s_b2, 1)

            def expert_hidden(b, e):
                if e == 0:
                    pe.wait_ge(s_zTs, b + 1)
                wait(pe, s_g, NE * b + e - 1)
                dst = bank(hidden_bank(e), 0, S)
                mm(dst, w["w1h"][:, e * HID:(e + 1) * HID], zT[:, :], True, False)
                mm(dst, w["w1l"][:, e * HID:(e + 1) * HID], zT[:, :], False, True).then_inc(s_hT, 1)

            def expert_out(b, e):
                pe.wait_ge(s_g, NE * b + e + 1)
                wait(pe, s_yt, NE * b + e)
                for j in range(NT):
                    last = mm(bank(Y, j * D, j * D + D), g[:, e % 2, j * P:(j + 1) * P], w["w2e"][:, e, :])
                last.then_inc(s_y, 1)
                if e + 2 < NE:
                    expert_hidden(b, e + 2)

            def start():
                transpose_powers(0)
                embed(0)
                transpose_r(0)
                transpose_rs(0)
                for p in range(HP0):
                    project(0, p)

            def step(b, nxt, own, before, experts):
                for j in range(NT):
                    if own:
                        values(b, j)
                        scores(b, j)
                    if j == 0 and experts:
                        transpose_gates(b - 2)
                    if j == 1 and nxt:
                        transpose_powers(b + 1)
                    if own and j < NT - 1:
                        add_kv(b, j)
                    if j == 0 and experts:
                        gated_biases(b - 2)
                    if j == 3 and before:
                        gate_logits(b - 1)
                    if experts:
                        expert_out(b - 2, 2 * j)
                    if j == 2 and before:
                        transpose_z(b - 1)
                    if own:
                        attend(b, j)
                    if j == 1 and nxt:
                        embed(b + 1)
                    if experts:
                        expert_out(b - 2, 2 * j + 1)
                    if j == 3 and nxt:
                        transpose_r(b + 1)
                        transpose_rs(b + 1)
                for e in range(2):
                    if before:
                        expert_hidden(b - 1, e)
                    if nxt:
                        project(b + 1, 2 * e)
                        project(b + 1, 2 * e + 1)

            steps(pe, start, step)

        @block.scalar
        def _(act):
            def copy_powers(b):
                act.wait_ge(s_xpT, b + 1)
                act.copy(xpT[:, :], bank(MISC, 0, S, NF)).then_inc(s_xpTs, 1)

            def copy_r(b):
                act.wait_ge(s_rT, b + 1)
                act.copy(rT[:, :], bank(MISC, 0, S)).then_inc(s_rTs, 1)

            def copy_rs(b):
                act.wait_ge(s_rsT, b + 1)
                act.copy(rsT[:, :], bank(VA, 0, S // 2).bitcast(F16)).then_inc(s_rsTs, 1)

            def copy_project(b, p):
                act.wait_ge(s_A, HP0 * b + p + 1)
                act.mul(AT[:, p, :], bank(VA if p % 2 == 0 else MISC, 0, S), 1.0 / SCALE0).then_inc(s_As, 1)

            def copy_values(b, j):
                act.wait_ge(s_V, NT * b + j + 1)
                act.mul(V0[:, j % 2, :], bank(VA, 0, H0 * D), 1.0 / SCALE0).then_inc(s_Vs, 1)

            def copy_kv(b, j):
                act.wait_ge(s_KV, 3 * b + j + 1)
                act.copy(KVs[:, j % 2, :], bank(KV, 0, HP0 * D)).then_inc(s_KVs, 1)

            def copy_z(b):
                act.wait_ge(s_zT, b + 1)
                wait(act, s_hT, NE * b)
                act.copy(zT[:, :], bank(MISC, 0, S // 2).bitcast(F16)).then_inc(s_zTs, 1)

            def gate(b):
                act.wait_ge(s_gd, b + 1)
                act.activation(gd[:, 1, :], gd[:, 0, :], ACT.Tanh, scale=0.5).then_inc(s_th, 1)

            def copy_gates(b):
                act.wait_ge(s_wT, b + 1)
                act.copy(wT[:, :], bank(MISC, 0, P, NT * NE)).then_inc(s_wTs, 1)

            def gelu(b, e):
                act.wait_ge(s_hT, NE * b + e + 1)
                wait(act, s_y, NE * b + e - 1)
                act.activation(g[:, e % 2, :], bank(hidden_bank(e), 0, S), ACT.Gelu,
                               bias=w["b1e"][:, e:e + 1]).then_inc(s_g, 1)

            def start():
                copy_powers(0)
                copy_r(0)
                copy_rs(0)
                for p in range(HP0):
                    copy_project(0, p)

            def step(b, nxt, own, before, experts):
                for j in range(NT):
                    if own:
                        copy_values(b, j)
                    if j == 0 and experts:
                        copy_gates(b - 2)
                    if j == 1 and nxt:
                        copy_powers(b + 1)
                    if own and j < NT - 1:
                        copy_kv(b, j)
                    if j == 3 and before:
                        gate(b - 1)
                    if j == 3 and nxt:
                        copy_r(b + 1)
                        copy_rs(b + 1)
                    if experts and j < NT - 1:
                        gelu(b - 2, 2 * j + 2)
                        gelu(b - 2, 2 * j + 3)
                    if j == 2 and before:
                        copy_z(b - 1)
                for e in range(2):
                    if before:
                        gelu(b - 1, e)
                    if nxt:
                        copy_project(b + 1, 2 * e)
                        copy_project(b + 1, 2 * e + 1)

            steps(act, start, step)

        @block.vector
        def _(dve):
            def powers(b):
                base = TK_STEPS * b
                xv = xp[:, :, :, :].rearrange("p a t d -> p (a t) d")
                dve.wait_ge(s_gath, 64 * b + 64)
                wait(dve, s_xpT, b)
                dve.scalar_tensor_tensor(tk[:, 0, :], gath[:, :], -1.0, gath[:, :], ALU.mult, ALU.max).then_inc(s_tk, 1)
                dve.wait_ge(s_tk, base + 1)
                dve.tensor_copy(tki[:, :], tk[:, 0, :]).then_inc(s_tk, 1)
                dve.wait_ge(s_tk, base + 2)
                dve.tensor_copy(tk[:, 1, :], tki[:, :]).then_inc(s_tk, 1)
                dve.wait_ge(s_tk, base + 3)
                dve.tensor_tensor(tk[:, 2, :], tk[:, 1, :], tk[:, 0, :], ALU.is_gt).then_inc(s_tk, 1)
                dve.wait_ge(s_tk, base + 4)
                dve.tensor_tensor(tk[:, 3, :], tk[:, 1, :], tk[:, 2, :], ALU.subtract).then_inc(s_tk, 1)
                dve.tensor_scalar(tk[:, 4, :], gath[:, :], 0.0, 2.0, ALU.is_ge, ALU.mult).then_inc(s_tk, 1)
                dve.wait_ge(s_tk, base + 6)
                dve.scalar_tensor_tensor(xv[:, :, 1], tk[:, 4, :], -1.0, tk[:, 3, :], ALU.add, ALU.mult).then_inc(s_tk, 1)
                dve.wait_ge(s_tk, base + 7)
                dve.tensor_tensor(xv[:, :, 2], xv[:, :, 1], xv[:, :, 1], ALU.mult).then_inc(s_tk, 1)
                dve.wait_ge(s_tk, base + 8)
                dve.tensor_tensor(xv[:, :, 3], xv[:, :, 1], xv[:, :, 2], ALU.mult).then_inc(s_tk, 1)
                dve.tensor_tensor(xv[:, :, 4], xv[:, :, 2], xv[:, :, 2], ALU.mult).then_inc(s_xp, 1)

            def store_embedding(b):
                dve.wait_ge(s_h0, b + 1)
                dve.tensor_copy(row(hid, b), bank(MISC, 0, NT * D).rearrange("p (a d) -> p a d", d=D)
                                ).then_inc(s_h0s, 1)

            def attend_norm(b):
                dve.wait_ge(s_h0s, b + 1)
                apart(dve, passed_dve)
                layernorm_sums(dve, b, row(hid, b), lnc[:, :, :], lnq[:, :, :], lns, s_ln, s_var)

            def attend_split(b):
                dve.wait_ge(s_rstd, b + 1)
                wait(dve, s_KV, 3 * b)
                rstd = each(lns[:, 3, :], D)
                dve.tensor_tensor(r2[:, :, 0, :], lnc[:, :, :], rstd, ALU.mult)
                dve.tensor_tensor(rs[:, :, 0, :], lnc[:, :, :], rstd, ALU.mult)
                dve.tensor_tensor(r2[:, :, 1, :], lnc[:, :, :], rstd, ALU.mult).then_inc(s_r, 1)
                dve.wait_ge(s_r, b + 1)
                dve.tensor_tensor(rs[:, :, 1, :], r2[:, :, 0, :], rs[:, :, 0, :], ALU.subtract).then_inc(s_rs, 1)

            def mask(b, j):
                dve.wait_ge(s_Om, NT * b + j + 1)
                dve.tensor_tensor(Om[:, j % 2, :, :],
                                  psum[:, SCORES * BANK:(SCORES + 2) * BANK].rearrange("p (h t) -> p h t", t=P),
                                  w["causal"][:, :].unsqueeze(1).broadcast_to([P, H0, P]), ALU.mult).then_inc(s_Oms, 1)

            def residual(b, j):
                dve.wait_ge(s_att, NT * b + j + 1)
                dst = row(hid, b)[:, j, :]
                dve.tensor_tensor(dst, dst, bank(VA, 0, D), ALU.add).then_inc(s_h1, 1)

            def expert_input(b):
                dve.wait_ge(s_h1, NT * b + NT)
                apart(dve, passed_dve)
                layernorm_sums(dve, b, row(hid, b), zc[:, :, :], zq[:, :, :], zs, s_zln, s_zvar)

            def expert_split(b):
                dve.wait_ge(s_zrstd, b + 1)
                wait(dve, s_zT, b)
                rstd = each(zs[:, 3, :], D)
                dve.tensor_tensor(z[:, :, :], zc[:, :, :], rstd, ALU.mult)
                dve.tensor_tensor(zp[:, :, 0, :], zc[:, :, :], rstd, ALU.mult).then_inc(s_z, 1)
                dve.wait_ge(s_z, b + 1)
                dve.tensor_tensor(zp[:, :, 1, :], z[:, :, :], zp[:, :, 0, :], ALU.subtract).then_inc(s_zp, 1)

            def best_two(b):
                base = GATE_STEPS * b
                dve.wait_ge(s_lg, b + 1)
                dve.tensor_tensor(lg[:, :, :], bank(MISC, 0, NT * NE).rearrange("p (a e) -> p a e", e=NE),
                                  w["br0"][:, :].unsqueeze(1).broadcast_to([P, NT, NE]), ALU.add).then_inc(s_lgs, 1)
                dve.wait_ge(s_lgs, b + 1)
                apart(dve, passed_dve)
                for j in range(NT):
                    dve.max(top[:, j, :], lg[:, j, :]).then_inc(s_gate, 1)
                for j in range(NT):
                    dve.wait_ge(s_gate, base + 1 + j)
                    apart(dve, passed_dve)
                    dve.max_index(topi[:, j, :], top[:, j, :], lg[:, j, :]).then_inc(s_gate, 1)
                dve.tensor_tensor(gd[:, 0, :], top[:, :, 0], top[:, :, 1], ALU.subtract).then_inc(s_gd, 1)

            def gates(b):
                base = GATE_STEPS * b
                dve.wait_ge(s_gate, base + 2 * NT)
                dve.tensor_copy(topf[:, :, :], topi[:, :, :]).then_inc(s_gate, 1)
                dve.wait_ge(s_gate, base + 1 + 2 * NT)
                for k in range(2):
                    dve.tensor_tensor(gw[:, k, :, :], w["iota8"][:, :].unsqueeze(1).broadcast_to([P, NT, NE]),
                                      each(topf[:, :, k], NE), ALU.is_equal)
                dve.wait_ge(s_th, b + 1)
                dve.tensor_scalar(gd[:, 2, :], gd[:, 1, :], 0.5, 0.5, ALU.mult, ALU.add)
                dve.tensor_scalar(gd[:, 3, :], gd[:, 1, :], -0.5, 0.5, ALU.mult, ALU.add).then_inc(s_gate, 1)
                dve.wait_ge(s_gate, base + 2 + 2 * NT)
                for k in range(2):
                    dve.tensor_tensor(gw[:, 2 + k, :, :], gw[:, k, :, :], each(gd[:, 2 + k, :], NE),
                                      ALU.mult).then_inc(s_gate, 1)
                dve.wait_ge(s_gate, base + 4 + 2 * NT)
                dve.tensor_tensor(wfull[:, :, :], gw[:, 2, :, :], gw[:, 3, :, :], ALU.add).then_inc(s_w, 1)

            def add_biases(b):
                dve.wait_ge(s_b2, b + 1)
                dve.tensor_tensor(row(hid, b), row(hid, b),
                                  bank(MISC, B2, B2 + NT * D).rearrange("p (a d) -> p a d", d=D),
                                  ALU.add).then_inc(s_b2s, 1)

            def weigh_expert(b, e):
                dve.wait_ge(s_y, NE * b + e + 1)
                wait(dve, s_add, NE * b + e + 1 - NYT)
                dve.tensor_tensor(ytmp[:, e % NYT, :, :], bank(Y, 0, NT * D).rearrange("p (a d) -> p a d", d=D),
                                  each(wfull[:, :, e], D), ALU.mult).then_inc(s_yt, 1)

            def start():
                dve.memset(xp[:, :, :, 0:1], 1.0)
                powers(0)
                store_embedding(0)
                attend_norm(0)
                attend_split(0)

            def step(b, nxt, own, before, experts):
                for j in range(NT):
                    if j == 0 and before:
                        expert_input(b - 1)
                    if j == 2 and nxt:
                        store_embedding(b + 1)
                    if own:
                        mask(b, j)
                    if j == 0 and experts:
                        add_biases(b - 2)
                    if j == 2 and nxt:
                        attend_norm(b + 1)
                    if j == 3 and before:
                        best_two(b - 1)
                    if j == 3 and nxt:
                        attend_split(b + 1)
                    if experts:
                        weigh_expert(b - 2, 2 * j)
                    if j == 0 and nxt:
                        powers(b + 1)
                    if j == 1 and before:
                        expert_split(b - 1)
                    if own:
                        residual(b, j)
                    if experts:
                        weigh_expert(b - 2, 2 * j + 1)
                if before:
                    gates(b - 1)

            steps(dve, start, step)


def windowed_attention(nc, w, hid, psum):
    with ExitStack() as ctx:
        def sb(name, shape, dt=F32):
            return ctx.enter_context(nc.sbuf_tensor(name, shape, dt))

        def sem(name):
            return ctx.enter_context(nc.semaphore(name))

        HALVES = (slice(0, NP), slice(NP, QK))
        THIRDS = (slice(0, 6), slice(6, 12), slice(12, QK))
        QHALVES = (slice(0, NP), slice(NP, NQ))
        NDIV = NP // 2
        NPROB = 8
        lnc = sb("lnc2", [P, NT, D])
        lnq = sb("lnq2", [P, NT, D])
        lns = sb("lns2", [P, 5, NT])
        x2 = sb("x2", [P, NT, D])
        xs = sb("xs", [P, NT, 2, D], F16)
        xsT = sb("xsT", [P, S], F16)
        sq = sb("sq", [P, QK, D])
        ss = sb("ss", [P, 3, QK])
        ra = sb("ra", [P, QK, D])
        rb = sb("rb", [P, QK, D])
        rc = sb("rc", [P, QK, D])
        qn = sb("qn", [P, QK, D])
        qs = sb("qs", [P, 2, NQ + 2, 2, D], F16)
        qT = sb("qT", [P, 2, NQ * P], F16)
        kT = sb("kT", [P, 2, S], F16)
        vt = sb("vt", [P, D])
        vv = sb("vv", [P, NT, VC])
        masked = sb("masked", [P, 4, 2, 2 * P], BF16)
        mb = sb("mb", [P, 2, NQ], BF16)
        prob = sb("prob", [P, NPROB, 2, 2, P])
        rcp = sb("rcp", [P, 2, 4])
        o = sb("o", [P, 2, NQ, D])
        oT = sb("oT", [P, NP, P])

        s_ln = sem("s2_ln")
        s_var = sem("s2_var")
        s_vt = sem("s2_vt")
        s_rstd = sem("s2_rstd")
        s_x = sem("s2_x")
        s_xl = sem("s2_xl")
        s_xT = sem("s2_xT")
        s_xTs = sem("s2_xTs")
        s_qkv = sem("s2_qkv")
        s_sq = sem("s2_sq")
        s_v = sem("s2_v")
        s_ssum = sem("s2_ssum")
        s_sst = sem("s2_sst")
        s_rms = sem("s2_rms")
        s_rab = sem("s2_rab")
        s_rot = sem("s2_rot")
        s_qn = sem("s2_qn")
        s_qh = sem("s2_qh")
        s_qs = sem("s2_qs")
        s_qkT = sem("s2_qkT")
        s_qTs = sem("s2_qTs")
        s_qTs2 = sem("s2_qTs2")
        s_S1 = sem("s2_S1")
        s_m = sem("s2_m")
        s_ST = sem("s2_ST")
        s_e = sem("s2_e")
        s_p = sem("s2_p")
        s_pv = sem("s2_pv")
        s_rcp = sem("s2_rcp")
        s_o = sem("s2_o")
        s_oT = sem("s2_oT")
        s_oTs = sem("s2_oTs")
        s_y = sem("s2_y")
        s_h = sem("s2_h")

        passed_pool, passed_pe, passed_dve = (sem(f"s2_passed_{e}") for e in ("pool", "pe", "dve"))

        proj = psum[:, 0:3 * BANK]
        qk_ps = proj[:, 0:QK * D].rearrange("p (h d) -> p h d", d=D)
        v_ps = proj[:, QK * D:(QK + 1) * D]
        qT_ps = psum[:, 0:2 * BANK].bitcast(F16)
        kT_ps = psum[:, 2 * BANK:2 * BANK + P].bitcast(F16)
        y_ps = proj[:, 1280:1280 + D]

        def blocks(j):
            return 2 if j > 0 else 1

        def after(b, j, n):
            if isinstance(b, int) and NT * b + j + n >= NT * B:
                return None
            return (b + (j + n) // NT, (j + n) % NT)

        def tiles(eng, step):
            for j in range(NT):
                step(0, j)
            with eng.Fori(1, B - 1, 1) as b:
                for j in range(NT):
                    step(b, j)
            for j in range(NT):
                step(B - 1, j)

        block = ctx.enter_context(nc.Block())

        @block.gpsimd
        def _(pool):
            def norm(b):
                rstd_pool(pool, b, lns[:, 3, :], lns[:, 2, :], lns[:, 4, :], w["mhalf"][:, 0:NT], D, EPS,
                          s_var, s_vt, s_rstd, passed_pool)

            def rms(b, j, part):
                n = NT * b + j
                if part == 0:
                    pool.wait_ge(s_ssum, n + 1)
                    wait(pool, s_qn, 2 * n)
                    apart(pool, passed_pool)
                    pool.tensor_scalar(ss[:, 1, :], ss[:, 0, :], 1.0 / D, RMS_EPS, ALU.mult, ALU.add).then_inc(s_sst, 1)
                    pool.wait_ge(s_sst, n + 1)
                hs = THIRDS[part]
                pool.tensor_tensor(ss[:, 2, hs], ss[:, 1, hs], w["mhalf"][:, hs], ALU.pow).then_inc(s_rms, 1)

            def window(b, j, i):
                pool.wait_ge(s_e, NP * (NT * b + j) + i + 1)
                apart(pool, passed_pool)
                p = prob[:, i % NPROB, :, :, :]
                last = pool.affine_select(out=p[:, :, 0, :], in_=p[:, :, 0, :], compare_op=ALU.is_ge, fill=0.0, base=0,
                                          pattern=[[0, 2], [1, P]], channel_multiplier=-1)
                if blocks(j) == 2:
                    last = pool.affine_select(out=p[:, :, 1, :], in_=p[:, :, 1, :], compare_op=ALU.is_ge, fill=0.0,
                                              base=0, pattern=[[0, 2], [-1, P]], channel_multiplier=1)
                last.then_inc(s_p, 1)

            def step(b, j):
                for i in range(NP):
                    window(b, j, i)
                    if i <= 2 and after(b, j, 2) is not None:
                        rms(*after(b, j, 2), i)
                    if i == 4 and j == 0 and after(b, j, NT) is not None:
                        norm(after(b, j, NT)[0])

            norm(0)
            for j in range(2):
                for part in range(3):
                    rms(0, j, part)
            tiles(pool, step)

        @block.tensor
        def _(pe):
            def mm(out, lhsT, rhs, start=True, stop=True):
                return pe.matmul(out, lhsT, rhs, start=start, stop=stop, skip_group_check=True)

            def transpose_x(b):
                pe.wait_ge(s_xl, b + 1)
                wait(pe, s_qTs, NT * b - 1)
                wait(pe, s_qTs2, NT * b - 1)
                apart(pe, passed_pe)
                for j in range(NT):
                    last = pe.transpose(psum[:, j * P // 2:(j + 1) * P // 2].bitcast(F16),
                                        xs[:, j, :, :].rearrange("p a b -> p (a b)"), w["identh"][:, :])
                last.then_inc(s_xT, 1)

            def project(b, j, copied):
                pe.wait_ge(s_xTs, b + 1)
                wait(pe, s_qTs, copied)
                wait(pe, s_qTs2, copied)
                t = xsT[:, j * P:(j + 1) * P]
                for c in range(2):
                    mm(proj[:, c * BANK:(c + 1) * BANK], t, w["wqh"][:, c * BANK:(c + 1) * BANK], True, False)
                    mm(proj[:, c * BANK:(c + 1) * BANK], t, w["wql"][:, c * BANK:(c + 1) * BANK], False, True)
                mm(proj[:, 2 * BANK:2 * BANK + 2 * D], t, w["wkvh"][:, :], True, False)
                mm(proj[:, 2 * BANK:2 * BANK + 2 * D], t, w["wkvl"][:, :], False, True).then_inc(s_qkv, 1)

            def transpose_qk(b, j, rotated):
                n = NT * b + j
                pe.wait_ge(s_qs, n + 1)
                wait(pe, s_rab, rotated)
                wait(pe, s_oTs, 2 * n - 2)
                wait(pe, s_h, n - 1)
                for h in range(NQ):
                    pe.transpose(qT_ps[:, h * P:(h + 1) * P], flat(qs[:, j % 2, h, :, :]), w["identh"][:, :])
                for k in range(2):
                    last = pe.transpose(kT_ps[:, k * P:(k + 1) * P], flat(qs[:, j % 2, NQ + k, :, :]), w["identh"][:, :])
                last.then_inc(s_qkT, 1)

            def scores(b, j, i):
                n = NP * (NT * b + j) + i
                if i == 0:
                    pe.wait_ge(s_qTs, NT * b + j + 1)
                if i == NP // 2:
                    pe.wait_ge(s_qTs2, NT * b + j + 1)
                wait(pe, s_m, n - 1)
                keys = P * blocks(j)
                dst = psum[:, (3 + i % 2) * BANK:(3 + i % 2) * BANK + 2 * keys].rearrange("p (h k) -> p h k", h=2)
                for hh in range(2):
                    h = 2 * i + hh
                    last = mm(dst[:, hh, :], qT[:, j % 2, h * P:(h + 1) * P], kT[:, 0, (j + 1) * P - keys:(j + 1) * P])
                last.then_inc(s_S1, 1)

            def shifted(b, j, i):
                n = NP * (NT * b + j) + i
                pe.wait_ge(s_m, n + 1)
                wait(pe, s_e, n - 1)
                for hh in range(2):
                    h = 2 * i + hh
                    lo = (5 + i % 2) * BANK + hh * 2 * P
                    nb = blocks(j)
                    mm(psum[:, lo:lo + nb * P].rearrange("p (k t) -> p k t", t=P),
                       mb[:, j % 2, h:h + 1].broadcast_to([P, P]),
                       w["nidentb"][:, :].unsqueeze(1).broadcast_to([P, nb, P]), True, False)
                    for k in range(nb):
                        dst = psum[:, lo + k * P:lo + (k + 1) * P]
                        for part in range(2):
                            last = mm(dst, kT[:, part, (j - k) * P:(j - k + 1) * P], qT[:, j % 2, h * P:(h + 1) * P],
                                      False, part == 1)
                last.then_inc(s_ST, 1)

            def weigh(b, j, i):
                n = NP * (NT * b + j) + i
                pe.wait_ge(s_p, n + 1)
                if i % 2 == 0:
                    wait(pe, s_o, NDIV * (NT * b + j) + i // 2)
                for hh in range(2):
                    lo = 7 * BANK + (2 * (i % 2) + hh) * VC
                    for k in range(blocks(j)):
                        last = mm(psum[:, lo:lo + VC], prob[:, i % NPROB, hh, k, :], vv[:, j - k, :], k == 0,
                                  k == blocks(j) - 1)
                last.then_inc(s_pv, 1)

            def transpose_out(b, j):
                n = NT * b + j
                pe.wait_ge(s_o, NDIV * (n + 1))
                if after(b, j, 3) is not None:
                    wait(pe, s_rab, n + 4)
                for c in range(2):
                    for i in range(NP // 2):
                        h = 2 * (c * NP // 2 + i)
                        last = pe.transpose(proj[:, c * BANK + i * P:c * BANK + (i + 1) * P],
                                            flat(o[:, j % 2, h:h + 2, :]), w["ident"][:, :])
                    last.then_inc(s_oT, 1)

            def output(b, j):
                n = NT * b + j
                for c in range(2):
                    pe.wait_ge(s_oTs, 2 * n + c + 1)
                    for i in range(c * NP // 2, (c + 1) * NP // 2):
                        last = mm(y_ps, oT[:, i, :], w["wo1"][:, i, :], i == 0, i == NP - 1)
                last.then_inc(s_y, 1)

            def step(b, j):
                first = isinstance(b, int) and b == 0 and j == 0
                nxt, ahead, far = (after(b, j, n) for n in (1, 2, 3))
                prev = (b - 1, NT - 1) if j == 0 else (b, j - 1)
                for i in range(NP):
                    if i + 2 < NP:
                        scores(b, j, i + 2)
                    elif nxt is not None:
                        scores(*nxt, i + 2 - NP)
                    shifted(b, j, i)
                    if i >= 2:
                        weigh(b, j, i - 2)
                    elif not first:
                        weigh(*prev, i + NP - 2)
                    if i == 2 and not first:
                        transpose_out(*prev)
                    if i == 3 and not first:
                        output(*prev)
                    if i == 4 and nxt is not None:
                        transpose_qk(*nxt, NT * b + j + (3 if ahead is not None else 2))
                    if i == 5 and far is not None:
                        if far[1] == 0:
                            transpose_x(far[0])
                        project(*far, NT * b + j + 2)

            transpose_x(0)
            project(0, 0, 0)
            transpose_qk(0, 0, 1)
            project(0, 1, 1)
            pe.wait_ge(s_rab, 2)
            project(0, 2, 1)
            scores(0, 0, 0)
            scores(0, 0, 1)
            tiles(pe, step)
            weigh(B - 1, NT - 1, NP - 2)
            weigh(B - 1, NT - 1, NP - 1)
            transpose_out(B - 1, NT - 1)
            output(B - 1, NT - 1)

        @block.scalar
        def _(act):
            def copy_xT(b):
                act.wait_ge(s_xT, b + 1)
                wait(act, s_qkv, NT * b)
                act.copy(xsT[:, :], psum[:, 0:S // 2].bitcast(F16)).then_inc(s_xTs, 1)

            def squares(b, j):
                n = NT * b + j
                act.wait_ge(s_qkv, n + 1)
                wait(act, s_ssum, n)
                wait(act, s_v, n)
                act.activation(sq[:, :, :], qk_ps, ACT.Square)
                act.copy(vt[:, :], v_ps).then_inc(s_sq, 1)

            def store_values(b, j):
                n = NT * b + j
                act.wait_ge(s_sq, n + 1)
                wait(act, s_pv, NP * (n - 2))
                act.copy(vv[:, j, 0:D], vt[:, :]).then_inc(s_v, 1)

            def split_high(b, j, part):
                n = NT * b + j
                act.wait_ge(s_qn, 2 * n + part + 1)
                if part == 0:
                    wait(act, s_qkT, n - 1)
                hs = QHALVES[part]
                last = act.copy(qs[:, j % 2, hs, 0, :], qn[:, hs, :])
                if part == 1:
                    last = act.copy(qs[:, j % 2, NQ, :, :], qn[:, NQ:QK, :].broadcast_to([P, 2, D]))
                last.then_inc(s_qh, 1)

            def copy_qk(b, j):
                n = NT * b + j
                act.wait_ge(s_qkT, n + 1)
                wait(act, s_ST, NP * (n - 1))
                act.copy(qT[:, j % 2, 0:NP * P], qT_ps[:, 0:NP * P])
                act.copy(kT[:, :, j * P:(j + 1) * P], kT_ps.rearrange("p (k t) -> p k t", t=P)).then_inc(s_qTs, 1)

            def exps(b, j, i):
                n = NP * (NT * b + j) + i
                act.wait_ge(s_ST, n + 1)
                wait(act, s_pv, n - NPROB + 1)
                src = psum[:, (5 + i % 2) * BANK:(6 + i % 2) * BANK].rearrange("p (h k t) -> p h k t", h=2, t=P)
                act.activation(prob[:, i % NPROB, :, 0:blocks(j), :], src[:, :, 0:blocks(j), :],
                               ACT.Exp).then_inc(s_e, 1)

            def copy_out(b, j):
                n = NT * b + j
                for c in range(2):
                    act.wait_ge(s_oT, 2 * n + c + 1)
                    if c == 0:
                        wait(act, s_y, n)
                    act.copy(flat(oT[:, c * NP // 2:(c + 1) * NP // 2, :]),
                             proj[:, c * BANK:(c + 1) * BANK]).then_inc(s_oTs, 1)

            def step(b, j):
                first = isinstance(b, int) and b == 0 and j == 0
                nxt, ahead, far = (after(b, j, n) for n in (1, 2, 3))
                prev = (b - 1, NT - 1) if j == 0 else (b, j - 1)
                for i in range(NP):
                    exps(b, j, i)
                    if i == 2 and not first:
                        copy_out(*prev)
                    if i in (4, 5) and ahead is not None:
                        split_high(*ahead, i - 4)
                    if i == 4 and nxt is not None:
                        copy_qk(*nxt)
                    if i == 5 and ahead is not None:
                        store_values(*ahead)
                    if i == 5 and far is not None:
                        if far[1] == 0:
                            copy_xT(far[0])
                        squares(*far)

            copy_xT(0)
            squares(0, 0)
            store_values(0, 0)
            split_high(0, 0, 0)
            split_high(0, 0, 1)
            copy_qk(0, 0)
            squares(0, 1)
            store_values(0, 1)
            split_high(0, 1, 0)
            split_high(0, 1, 1)
            squares(0, 2)
            tiles(act, step)
            copy_out(B - 1, NT - 1)

        @block.vector
        def _(dve):
            def norm_sums(b):
                layernorm_sums(dve, b, row(hid, b), lnc[:, :, :], lnq[:, :, :], lns, s_ln, s_var)

            def norm(b):
                dve.wait_ge(s_rstd, b + 1)
                wait(dve, s_xT, b)
                dve.tensor_tensor(x2[:, :, :], lnc[:, :, :], each(lns[:, 3, :], D), ALU.mult)
                dve.tensor_tensor(xs[:, :, 0, :], lnc[:, :, :], each(lns[:, 3, :], D), ALU.mult).then_inc(s_x, 1)
                dve.wait_ge(s_x, b + 1)
                dve.tensor_tensor(xs[:, :, 1, :], x2[:, :, :], xs[:, :, 0, :], ALU.subtract).then_inc(s_xl, 1)

            def rotate_cos(b, j, part):
                n = NT * b + j
                if part == 0:
                    dve.wait_ge(s_sq, n + 1)
                hs = HALVES[part]
                dve.tensor_tensor(ra[:, hs, :], qk_ps[:, hs, :],
                                  w["cos_t"][:, j, :].unsqueeze(1).broadcast_to([P, hs.stop - hs.start, D]), ALU.mult)

            def rotate_sin(b, j, part):
                other = qk_ps[:, :, 1 - part::2]
                sin = w["nsin_t" if part == 0 else "sin_t"][:, j, :].unsqueeze(1).broadcast_to([P, QK, D // 2])
                last = dve.tensor_tensor(rb[:, :, part::2], other, sin, ALU.mult)
                if part == 1:
                    last.then_inc(s_rab, 1)

            def rotate(b, j, part):
                n = NT * b + j
                if part == 0:
                    dve.wait_ge(s_rab, n + 1)
                hs = HALVES[part]
                last = dve.tensor_tensor(rc[:, hs, :], ra[:, hs, :], rb[:, hs, :], ALU.add)
                if part == 1:
                    last.then_inc(s_rot, 1)

            def sum_squares(b, j, part):
                n = NT * b + j
                if part == 0:
                    dve.wait_ge(s_sq, n + 1)
                hs = HALVES[part]
                last = dve.tensor_reduce(ss[:, 0, hs], sq[:, hs, :], AX, ALU.add)
                if part == 1:
                    last.then_inc(s_ssum, 1)

            def normalise(b, j, part):
                n = NT * b + j
                if part == 0:
                    dve.wait_ge(s_rot, n + 1)
                    dve.wait_ge(s_rms, 3 * n + 3)
                hs = QHALVES[part]
                last = dve.tensor_tensor(qn[:, hs, :], rc[:, hs, :], each(ss[:, 2, hs], D), ALU.mult)
                if part == 1:
                    last = dve.scalar_tensor_tensor(qn[:, NQ, :], rc[:, NQ, :], ss[:, 2, NQ:QK], w["kscale"][:, :],
                                                    ALU.mult, ALU.mult)
                last.then_inc(s_qn, 1)

            def split_low(b, j, part):
                n = NT * b + j
                dve.wait_ge(s_qh, 2 * n + part + 1)
                hs = QHALVES[part]
                dve.tensor_tensor(qs[:, j % 2, hs, 1, :], qn[:, hs, :], qs[:, j % 2, hs, 0, :], ALU.subtract)
                if part == 1:
                    dve.tensor_tensor(qs[:, j % 2, NQ + 1, :, :], qn[:, NQ:QK, :].broadcast_to([P, 2, D]), qs[:, j % 2, NQ, :, :],
                                      ALU.subtract).then_inc(s_qs, 1)

            def maximum(b, j, i):
                n = NP * (NT * b + j) + i
                dve.wait_ge(s_S1, n + 1)
                if i == 0:
                    wait(dve, s_ST, n - NP)
                apart(dve, passed_dve)
                keys = P * blocks(j)
                for hh in range(2):
                    lo = (3 + i % 2) * BANK + hh * keys
                    last = dve.tensor_tensor_reduce(masked[:, i % 4, hh, 0:keys], psum[:, lo:lo + keys],
                                                    w["wmask"][:, 2 * P - keys:2 * P], 1.0, TAKEN, ALU.add, ALU.max,
                                                    mb[:, j % 2, 2 * i + hh:2 * i + hh + 1])
                last.then_inc(s_m, 1)

            def divide(b, j, k):
                t = NT * b + j
                dve.wait_ge(s_pv, NP * t + 2 * k + 2)
                if k == 0:
                    wait(dve, s_oT, 2 * t - 2)
                pv = psum[:, 7 * BANK:7 * BANK + 4 * VC].rearrange("p (h c) -> p h c", c=VC)
                dve.reciprocal(rcp[:, k % 2, :], pv[:, :, D]).then_inc(s_rcp, 1)
                dve.wait_ge(s_rcp, NDIV * t + k + 1)
                dve.tensor_tensor(o[:, j % 2, 4 * k:4 * k + 4, :], pv[:, :, 0:D], each(rcp[:, k % 2, :], D),
                                  ALU.mult).then_inc(s_o, 1)

            def copy_q(b, j):
                n = NT * b + j
                dve.wait_ge(s_qkT, n + 1)
                wait(dve, s_ST, NP * (n - 1))
                dve.tensor_copy(qT[:, j % 2, NP * P:], qT_ps[:, NP * P:]).then_inc(s_qTs2, 1)

            def residual(b, j):
                dve.wait_ge(s_y, NT * b + j + 1)
                dst = row(hid, b)[:, j, :]
                dve.tensor_tensor(dst, dst, y_ps, ALU.add).then_inc(s_h, 1)

            def between(b, j, i, part):
                ahead, far = after(b, j, 2), after(b, j, 3)
                if ahead is not None:
                    if i == 0:
                        rotate_cos(*ahead, part)
                    if i == 1:
                        rotate_sin(*ahead, part)
                    if i == 2:
                        rotate(*ahead, part)
                    if (i, part) == (3, 1):
                        normalise(*ahead, 0)
                    if (i, part) == (4, 0):
                        normalise(*ahead, 1)
                    if (i, part) == (5, 1):
                        split_low(*ahead, 0)
                    if (i, part) == (6, 0):
                        split_low(*ahead, 1)
                if far is not None:
                    if (i, part) == (6, 1):
                        sum_squares(*far, 0)
                    if (i, part) == (7, 0):
                        sum_squares(*far, 1)

            def step(b, j):
                first = isinstance(b, int) and b == 0 and j == 0
                nxt = after(b, j, 1)
                prev = (b - 1, NT - 1) if j == 0 else (b, j - 1)
                for i in range(NP):
                    if i + 2 < NP:
                        maximum(b, j, i + 2)
                    elif nxt is not None:
                        maximum(*nxt, i + 2 - NP)
                    between(b, j, i, 0)
                    if i in (3, 5, 7):
                        divide(b, j, (i - 3) // 2)
                    if i == 1 and not first:
                        divide(*prev, NDIV - 1)
                    between(b, j, i, 1)
                    if i == 3 and not first:
                        residual(*prev)
                    if i == 4 and nxt is not None:
                        copy_q(*nxt)
                    if i == 4 and j == 0 and after(b, j, NT) is not None:
                        norm_sums(after(b, j, NT)[0])
                    if i == 4 and j == 1 and after(b, j, 3) is not None:
                        norm(after(b, j, 3)[0])

            dve.memset(vv[:, :, D:VC], 1.0)
            norm_sums(0)
            norm(0)
            for j in range(2):
                for first_step in (sum_squares, rotate_cos, rotate_sin, rotate, normalise, split_low):
                    for part in range(2):
                        first_step(0, j, part)
                if j == 0:
                    copy_q(0, 0)
            for part in range(2):
                sum_squares(0, 2, part)
            maximum(0, 0, 0)
            maximum(0, 0, 1)
            tiles(dve, step)
            divide(B - 1, NT - 1, NDIV - 1)
            residual(B - 1, NT - 1)


def feed_forward(nc, w, hid, zw, wall, w_dram, psum):
    with ExitStack() as ctx:
        def sb(name, shape, dt=F32):
            return ctx.enter_context(nc.sbuf_tensor(name, shape, dt))

        def sem(name):
            return ctx.enter_context(nc.semaphore(name))

        def bank(n, lo, hi, parts=P):
            return psum[0:parts, n * BANK + lo:n * BANK + hi]

        lnc = sb("lnc3", [P, NT, D])
        lnq = sb("lnq3", [P, NT, D])
        lns = sb("lns3", [P, 5, NT])
        x3 = sb("x3", [P, NT, D])
        xp3 = sb("xp3", [P, NT, 2, D], F16)
        xT = sb("xT3", [P, S], F16)
        gf = sb("gf", [P, FC, S])
        wcol = sb("wcol", [P, NT])
        yb = sb("yb", [P, NT, D])
        wrow = sb("wrow", [1, S])

        s_ln = sem("s3_ln")
        s_var = sem("s3_var")
        s_vt = sem("s3_vt")
        s_rstd = sem("s3_rstd")
        s_x = sem("s3_x")
        s_xl = sem("s3_xl")
        s_base = sem("s3_base")
        s_xT = sem("s3_xT")
        s_xTs = sem("s3_xTs")
        s_w = sem("s3_w")
        s_wrow = sem("s3_wrow")
        s_wall = sem("s3_wall")
        s_wback = sem("s3_wback")
        s_wcol = sem("s3_wcol")
        s_h = sem("s3_h")
        s_g = sem("s3_g")
        s_y = sem("s3_y")
        s_yb = sem("s3_yb")
        s_zw = sem("s3_zw")

        passed_pool, passed_pe, passed_dve = (sem(f"s3_passed_{e}") for e in ("pool", "pe", "dve"))

        def steps(eng, step):
            step(-2, True, False, False, False)
            step(-1, True, True, False, False)
            step(0, True, True, True, False)
            with eng.Fori(1, B - 2, 1) as b:
                step(b, True, True, True, True)
            step(B - 2, False, True, True, True)
            step(B - 1, False, False, True, True)
            step(B, False, False, False, True)

        block = ctx.enter_context(nc.Block())

        @block.sync
        def _(sp):
            def store(b):
                sp.wait_ge(s_wrow, b + 1)
                sp.dma_start(w_dram[bass.ds(b, 1), :], wrow[:, :]).then_inc(s_wall, 16)
            batches(sp, store)
            sp.wait_ge(s_wall, 16 * B)
            sp.dma_start(wall[:, :], w_dram[:, :]).then_inc(s_wback, 16)
            sp.wait_ge(s_wback, 16)

        @block.gpsimd
        def _(pool):
            def step(b, two, one, own, before):
                if one:
                    pool.wait_ge(s_x, b + 2)
                    apart(pool, passed_pool)
                    pool.tensor_tensor(row(hid, b + 1), row(hid, b + 1), x3[:, :, :], ALU.add).then_inc(s_base, 1)
                if two:
                    rstd_pool(pool, b + 2, lns[:, 3, :], lns[:, 2, :], lns[:, 4, :], w["mhalf"][:, 0:NT], D, EPS,
                              s_var, s_vt, s_rstd, passed_pool)

            steps(pool, step)

        @block.tensor
        def _(pe):
            def transpose_x(b):
                pe.wait_ge(s_xl, b + 1)
                wait(pe, s_xTs, b)
                for j in range(NT):
                    last = pe.transpose(bank(0, j * D, j * D + D).bitcast(F16), flat(xp3[:, j, :, :]),
                                        w["identh"][:, :])
                last.then_inc(s_xT, 1)

            def feed(b):
                pe.wait_ge(s_xTs, b + 1)
                wait(pe, s_wcol, b)
                for j in range(NT):
                    for part in range(2):
                        pe.matmul(bank(6, j, j + 1), xT[:, j * P:(j + 1) * P], w[("wrfh", "wrfl")[part]][:, :],
                                  start=part == 0, stop=part == 1)
                wait(pe, s_wrow, b)
                for part in range(2):
                    last = pe.matmul(bank(7, 0, S, 1), w[("wrfh", "wrfl")[part]][:, :], xT[:, :], start=part == 0,
                                     stop=part == 1)
                last.then_inc(s_w, 1)
                wait(pe, s_g, FC * b)
                for c in range(FC):
                    for part in range(2):
                        last = pe.matmul(bank(1 + c, 0, S), w[("w1fh", "w1fl")[part]][:, c * P:(c + 1) * P], xT[:, :],
                                         start=part == 0, stop=part == 1)
                    last.then_inc(s_h, 1)

            def out(b):
                pe.wait_ge(s_g, FC * b + FC)
                wait(pe, s_yb, b)
                for j in range(NT):
                    for c in range(FC):
                        last = pe.matmul(bank(5, j * D, j * D + D), gf[:, c, j * P:(j + 1) * P], w["w2f"][:, c, :],
                                         start=c == 0, stop=c == FC - 1)
                last.then_inc(s_y, 1)

            def step(b, two, one, own, before):
                if own:
                    feed(b)
                if one:
                    transpose_x(b + 1)
                if before:
                    out(b - 1)

            steps(pe, step)

        @block.scalar
        def _(act):
            def copy_xT(b):
                act.wait_ge(s_xT, b + 1)
                wait(act, s_h, FC * b)
                act.copy(xT[:, :], bank(0, 0, S // 2).bitcast(F16)).then_inc(s_xTs, 1)

            def store_router(b):
                act.wait_ge(s_w, b + 1)
                wait(act, s_wall, 16 * b)
                act.activation(wrow[:, :], bank(7, 0, S, 1), ACT.Identity,
                               bias=w["brf"][0:1, 0:1]).then_inc(s_wrow, 1)

            def gelu(b):
                for c in range(FC):
                    act.wait_ge(s_h, FC * b + c + 1)
                    wait(act, s_y, b)
                    act.activation(gf[:, c, :], bank(1 + c, 0, S), ACT.Gelu_apprx_tanh,
                                   bias=w["b1f"][:, c:c + 1]).then_inc(s_g, 1)

            def step(b, two, one, own, before):
                if own:
                    store_router(b)
                if one:
                    copy_xT(b + 1)
                if own:
                    gelu(b)

            steps(act, step)

        @block.vector
        def _(dve):
            def scale(b):
                dve.wait_ge(s_rstd, b + 1)
                wait(dve, s_xT, b)
                wait(dve, s_base, b)
                rstd = each(lns[:, 3, :], D)
                dve.tensor_tensor(x3[:, :, :], lnc[:, :, :], rstd, ALU.mult)
                dve.tensor_tensor(xp3[:, :, 0, :], lnc[:, :, :], rstd, ALU.mult).then_inc(s_x, 1)
                dve.wait_ge(s_x, b + 1)
                dve.tensor_tensor(xp3[:, :, 1, :], x3[:, :, :], xp3[:, :, 0, :], ALU.subtract).then_inc(s_xl, 1)

            def router(b):
                dve.wait_ge(s_w, b + 1)
                wait(dve, s_zw, b)
                dve.tensor_scalar(wcol[:, :], bank(6, 0, NT), w["brf"][:, 0:1], None, ALU.add).then_inc(s_wcol, 1)

            def out(b):
                dve.wait_ge(s_y, b + 1)
                dve.tensor_tensor(yb[:, :, :], bank(5, 0, NT * D).rearrange("p (a d) -> p a d", d=D),
                                  w["b2f"][:, :].unsqueeze(1).broadcast_to([P, NT, D]), ALU.add).then_inc(s_yb, 1)
                dve.wait_ge(s_yb, b + 1)
                dve.tensor_tensor(row(zw, b), yb[:, :, :], each(wcol[:, :], D), ALU.mult).then_inc(s_zw, 1)

            def step(b, two, one, own, before):
                if one:
                    scale(b + 1)
                if two:
                    layernorm_sums(dve, b + 2, row(hid, b + 2), lnc[:, :, :], lnq[:, :, :], lns, s_ln, s_var)
                if before:
                    out(b - 1)
                if own:
                    router(b)

            steps(dve, step)


def select_and_store(nc, w, hid, zw, wall, psum, out):
    OG = 4
    ROUNDS = (KEEP + 1) // 8
    with ExitStack() as ctx:
        def sb(name, shape, dt=F32):
            return ctx.enter_context(nc.sbuf_tensor(name, shape, dt))

        def sem(name):
            return ctx.enter_context(nc.semaphore(name))

        work = sb("work", [B, S])
        t8 = sb("t8", [B, 8])
        i8 = sb("i8", [B, 8], U32)
        i8f = sb("i8f", [B, 8])
        drop = sb("drop", [B, S])
        sel = sb("sel", [B, S])
        selT = sb("selT", [P, NT, B])
        add = sb("add", [P, 2, OG, NT, D])

        s_top = sem("s4_top")
        s_rep = sem("s4_rep")
        s_idx = sem("s4_idx")
        s_sel = sem("s4_sel")
        s_selT = sem("s4_selT")
        s_selTs = sem("s4_selTs")
        s_add = sem("s4_add")
        s_out = sem("s4_out")
        s_done = sem("s4_done")

        out_v = out.rearrange("b (j p) d -> p b j d", p=P)
        passed_pool, passed_pe, passed_dve = (sem(f"s4_passed_{e}") for e in ("pool", "pe", "dve"))

        block = ctx.enter_context(nc.Block())

        @block.vector
        def _(dve):
            dve.max(t8[:, :], wall[:, :]).then_inc(s_top, 1)
            dve.wait_ge(s_top, 1)
            dve.match_replace(work[:, :], t8[:, :], wall[:, :], TAKEN).then_inc(s_rep, 1)

            with dve.Fori(1, ROUNDS - 1, 1) as r:
                dve.wait_ge(s_rep, r)
                apart(dve, passed_dve)
                dve.max(t8[:, :], work[:, :]).then_inc(s_top, 1)
                dve.wait_ge(s_top, r + 1)
                apart(dve, passed_dve)
                dve.match_replace(work[:, :], t8[:, :], work[:, :], TAKEN).then_inc(s_rep, 1)
            dve.wait_ge(s_rep, ROUNDS - 1)
            dve.max(t8[:, :], work[:, :]).then_inc(s_top, 1)
            dve.wait_ge(s_top, ROUNDS)
            dve.max_index(i8[:, :], t8[:, :], work[:, :]).then_inc(s_idx, 1)
            dve.match_replace(work[:, :], t8[:, :], work[:, :], TAKEN).then_inc(s_rep, 1)
            dve.wait_ge(s_idx, 1)
            dve.tensor_copy(i8f[:, :], i8[:, :]).then_inc(s_idx, 1)
            dve.wait_ge(s_idx, 2)
            dve.tensor_scalar(drop[:, :], w["iota_row"][:, :], i8f[:, 7:8], None, ALU.is_equal).then_inc(s_idx, 1)
            dve.wait_ge(s_idx, 3)
            dve.wait_ge(s_rep, ROUNDS)
            dve.scalar_tensor_tensor(sel[:, :], work[:, :], TAKEN, drop[:, :], ALU.is_equal,
                                     ALU.subtract).then_inc(s_sel, 1)
            dve.wait_ge(s_selT, 1)
            dve.tensor_copy(selT[:, :, :].rearrange("p a b -> p (a b)"), psum[:, 0:NT * B]).then_inc(s_selTs, 1)
            dve.wait_ge(s_selTs, 1)
            for q in range(B // OG):
                rows = slice(q * OG, (q + 1) * OG)
                if q >= 2:
                    dve.wait_ge(s_out, q - 1)
                m = selT[:, :, rows].rearrange("p a b -> p b a").unsqueeze(3).broadcast_to([P, OG, NT, D])
                dve.tensor_tensor(add[:, q % 2, :, :, :], zw[:, rows, :, :], m, ALU.mult).then_inc(s_add, 1)
                dve.wait_ge(s_add, q + 1)
                dve.tensor_tensor(hid[:, rows, :, :], hid[:, rows, :, :], add[:, q % 2, :, :, :],
                                  ALU.add).then_inc(s_out, 1)

        @block.tensor
        def _(pe):
            pe.wait_ge(s_sel, 1)
            for j in range(NT):
                last = pe.transpose(psum[:, j * B:(j + 1) * B], sel[:, j * P:(j + 1) * P], w["ident"][0:B, 0:B])
            last.then_inc(s_selT, 1)

        @block.sync
        def _(sp):
            for q in range(B // OG):
                sp.wait_ge(s_out, q + 1)
                sp.dma_start(out_v[:, q * OG:(q + 1) * OG, :, :].rearrange("p b j d -> p (b j) d"),
                             hid[:, q * OG:(q + 1) * OG, :, :].rearrange("p b j d -> p (b j) d")).then_inc(s_done, 16)
            sp.wait_ge(s_done, 16 * (B // OG))


SHAPES = {
    "ident": (P, [P]), "causal": (P, [P]), "wmask": (P, [2 * P]), "cos_t": (P, [NT, D]), "sin_t": (P, [NT, D // 2]),
    "nsin_t": (P, [NT, D // 2]), "iota8": (P, [NE]), "iota_row": (B, [S]), "mhalf": (P, [QK]),
    "coef": (NF, [D]), "qw0": (P, [H0 * D]), "ew0": (P, [H0 * D]), "gam": (P, [1]), "bet": (P, [1]),
    "wr0": (P, [NE]), "br0": (P, [NE]), "w1e": (P, [NE * HID]), "b1e": (P, [NE]), "w2e": (P, [NE, D]),
    "b2p": (NT * NE, [NT, D]), "wq1": (P, [NQ * D]), "wkv": (P, [2 * D]), "wo1": (P, [NP, D]), "qnw": (P, [D]),
    "knw": (P, [D]), "wrf": (P, [1]), "brf": (P, [1]), "w1f": (P, [FF]), "b1f": (P, [FC]), "w2f": (P, [FC, D]),
    "b2f": (P, [D]),
}


SPLIT = (("wq1", "wq"), ("wkv", "wkv"), ("qw0", "qw"), ("ew0", "ew"), ("w1e", "w1"), ("wr0", "wr"),
         ("w1f", "w1f"), ("wrf", "wrf"))


def tower(nc, a, ids, turns, out):
    with ExitStack() as ctx:
        def sb(name, shape, dt=F32):
            return ctx.enter_context(nc.sbuf_tensor(name, shape, dt))

        def sem(name):
            return ctx.enter_context(nc.semaphore(name))

        w = {}
        for name, (parts, free) in SHAPES.items():
            w[name] = sb("c_" + name, [parts] + free)
        w["nidentb"] = sb("nidentb", [P, P], BF16)
        w["identh"] = sb("identh", [P, P], F16)
        w["kscale"] = sb("kscale", [P, D])
        for whole, name in SPLIT:
            cols = SHAPES[whole][1][0]
            w[name + "h"] = sb(name + "h", [P, cols], F16)
            w[name + "l"] = sb(name + "l", [P, cols], F16)
        hid = sb("hid", [P, B, NT, D])
        zw = sb("zw", [P, B, NT, D])
        wall = sb("wall", [B, S])
        w_dram = nc.dram_tensor("router_weights", (B, S), F32).ap()
        psum = ctx.enter_context(nc.psum_tensor("psum", [P, 8 * BANK], F32))

        s_load = sem("s_load")
        s_beta = sem("s_beta")
        s_scaled = sem("s_scaled")
        s_high = sem("s_high")
        with nc.Block() as block:
            @block.sync
            def _(sp):
                for name in SHAPES:
                    parts, free = SHAPES[name]
                    dst = w[name]
                    dst = dst[:, :] if len(free) == 1 else dst[:, :, :]
                    sp.dma_start(dst, a[name]).then_inc(s_load, 16)

            @block.tensor
            def _(pe):
                pe.wait_ge(s_load, 16 * len(SHAPES))
                for e in range(NE):
                    pe.matmul(psum[:, e:e + 1], w["w1e"][0:D, e * HID:(e + 1) * HID], w["bet"][0:D, :], start=True,
                              stop=True)
                pe.matmul(psum[:, NE:2 * NE], w["bet"][0:D, :].broadcast_to([D, P]), w["wr0"][0:D, :], start=True,
                          stop=True).then_inc(s_beta, 1)

            @block.vector
            def _(dve):
                dve.wait_ge(s_load, 16 * len(SHAPES))
                dve.tensor_scalar(w["nidentb"][:, :], w["ident"][:, :], -1.0, None, ALU.mult)
                dve.tensor_copy(w["identh"][:, :], w["ident"][:, :])
                dve.scalar_tensor_tensor(w["kscale"][:, :], w["qnw"][:, :], float(D) ** -0.5, w["knw"][:, :],
                                         ALU.mult, ALU.mult)
                dve.wait_ge(s_beta, 1)
                dve.tensor_tensor(w["b1e"][:, :], w["b1e"][:, :], psum[:, 0:NE], ALU.add)
                dve.tensor_tensor(w["br0"][:, :], w["br0"][:, :], psum[:, NE:2 * NE], ALU.add)
                for name in ("w1e", "wr0"):
                    dve.tensor_scalar(w[name][:, :], w[name][:, :], w["gam"][:, 0:1], None, ALU.mult)
                for name in ("qw0", "ew0"):
                    last = dve.tensor_scalar(w[name][:, :], w[name][:, :], SCALE0, None, ALU.mult)
                last.then_inc(s_scaled, 1)
                dve.wait_ge(s_scaled, 1)
                for whole, name in SPLIT:
                    last = dve.tensor_copy(w[name + "h"][:, :], w[whole][:, :])
                last.then_inc(s_high, 1)
                dve.wait_ge(s_high, 1)
                for whole, name in SPLIT:
                    dve.tensor_tensor(w[name + "l"][:, :], w[whole][:, :], w[name + "h"][:, :], ALU.subtract)

        embed_attend_experts(nc, w, ids, turns, hid, psum)
        windowed_attention(nc, w, hid, psum)
        feed_forward(nc, w, hid, zw, wall, w_dram, psum)
        select_and_store(nc, w, hid, zw, wall, psum, out)


def layouts(x):
    f = {k: np.asarray(v) for k, v in x.items()}
    t = np.arange(S, dtype=np.float32)[:, None]
    freq = np.float32(10000.0) ** (-2.0 * np.arange(D // 2, dtype=np.float32) / D)
    theta = (t * freq[None, :].astype(np.float32)).astype(np.float32)
    cos = np.cos(theta).astype(np.float32).reshape(NT, P, D // 2).transpose(1, 0, 2)
    sin = np.sin(theta).astype(np.float32).reshape(NT, P, D // 2).transpose(1, 0, 2)
    q, k = np.arange(P)[:, None], np.arange(2 * P)[None, :] - P
    b2p = np.zeros((NT, NE, NT, D), np.float32)
    for j in range(NT):
        b2p[j, :, j, :] = f["L0_ffn_b2"]
    arrays = {
        "ident": np.eye(P, dtype=np.float32),
        "causal": np.triu(np.ones((P, P), np.float32)),
        "wmask": np.where((k <= q) & (q - k <= P), 0.0, NEG).astype(np.float32),
        "cos_t": np.repeat(cos, 2, axis=2), "sin_t": sin, "nsin_t": -sin,
        "iota8": np.tile(np.arange(NE, dtype=np.float32), (P, 1)),
        "iota_row": np.tile(np.arange(S, dtype=np.float32), (B, 1)),
        "mhalf": np.full((P, QK), -0.5, np.float32),
        "coef": f["L0_tok_poly_coeffs"].reshape(NF, D),
        "qw0": np.tile(f["L0_attn_Q"].transpose(1, 0, 2).reshape(D, H0 * D), (2, 1)),
        "ew0": np.tile(f["L0_attn_E"].transpose(2, 0, 1).reshape(D, H0 * D), (2, 1)),
        "gam": np.tile(f["L0_ffn_gamma"].reshape(D, 1), (2, 1)), "bet": np.tile(f["L0_ffn_beta"].reshape(D, 1), (2, 1)),
        "wr0": np.tile(f["L0_ffn_Wr"], (2, 1)), "br0": np.tile(f["L0_ffn_br"], (P, 1)),
        "w1e": np.tile(f["L0_ffn_W1"].transpose(1, 0, 2).reshape(D, NE * HID), (2, 1)), "b1e": f["L0_ffn_b1"].T,
        "w2e": f["L0_ffn_W2"].transpose(1, 0, 2), "b2p": b2p.reshape(NT * NE, NT, D),
        "wq1": np.tile(f["L1_attn_wq"].T, (2, 1)), "wkv": np.tile(f["L1_attn_wkv"].T, (2, 1)),
        "wo1": f["L1_attn_wo"].T.reshape(NP, P, D).transpose(1, 0, 2),
        "qnw": np.tile(f["L1_attn_q_norm_w"], (P, 1)), "knw": np.tile(f["L1_attn_k_norm_w"], (P, 1)),
        "wrf": np.tile(f["L1_ffn_wr"], (2, 1)), "brf": np.tile(f["L1_ffn_br"], (P, 1)),
        "w1f": np.tile(f["L1_ffn_w1"], (2, 1)), "b1f": f["L1_ffn_b1"].reshape(FC, P).T,
        "w2f": f["L1_ffn_w2"].reshape(FC, P, D).transpose(1, 0, 2), "b2f": np.tile(f["L1_ffn_b2"], (P, 1)),
    }
    arrays = {k: np.ascontiguousarray(v) for k, v in arrays.items()}
    ids = np.ascontiguousarray(f["x"].reshape(B * NT, P).T)
    return arrays, ids, np.ascontiguousarray(f["L0_tok_turns"])


def kernel(**inputs):
    import concourse.bacc as bacc
    from concourse.bass_utils import run_bass_kernel_spmd

    arrays, ids, turns = layouts(inputs)
    nc = bacc.Bacc("TRN2", target_bir_lowering=False, num_devices=1)
    feeds, a = {}, {}
    for name, v in arrays.items():
        feeds["in_" + name] = v
        a[name] = nc.dram_tensor("in_" + name, v.shape, F32, kind="ExternalInput").ap()
    feeds["in_ids"], feeds["in_turns"] = ids, turns
    ids_d = nc.dram_tensor("in_ids", ids.shape, mybir.dt.from_np(ids.dtype), kind="ExternalInput").ap()
    turns_d = nc.dram_tensor("in_turns", turns.shape, F32, kind="ExternalInput").ap()
    out = nc.dram_tensor("out", (B, S, D), F32, kind="ExternalOutput").ap()
    tower(nc, a, ids_d, turns_d, out)
    r = run_bass_kernel_spmd(nc, [feeds], core_ids=[0])
    return r.results[0]["out"]
```
